# Optimizing a Trainium2 kernel written in Bass

```python
import numpy as np
import jax
import jax.numpy as jnp

def _softmax(x, axis=-1):
    return jax.nn.softmax(x, axis=axis)

def _gelu(x):
    return jax.nn.gelu(x, approximate=True)

def _silu(x):
    return jax.nn.silu(x)

def _sigmoid(x):
    return jax.nn.sigmoid(x)

def _layernorm(x, axis=-1, eps=1e-05):
    m = jnp.mean(x, axis=axis, keepdims=True)
    v = jnp.var(x, axis=axis, keepdims=True)
    return (x - m) / jnp.sqrt(v + eps)

def _scatter_add(tgt, idx, src, axis=0):
    return tgt.at[idx].add(src)

def _segment_sum(src, seg, n):
    return jax.ops.segment_sum(src, seg, n)
kernel_name = 'mk_adaln_d1_jaxref_r4_6d898b'

def setup_inputs(seed: int=0):
    np.random.seed(seed)
    _w = jnp.asarray

    def _L0_attn_setup():
        import jax, jax.numpy as jnp
        import numpy as np
        DIM = 256
        NUM_HEADS = 16
        HD = DIM // NUM_HEADS
        ROPE_DIM = 64
        ROPE_BASE = 10000.0

        def _apply_rope(t):
            D = t.shape[-1]
            N = t.shape[2]
            pos = jnp.arange(N, dtype=t.dtype)
            inv = 1.0 / ROPE_BASE ** (jnp.arange(0, D, 2, dtype=t.dtype) / D)
            freqs = pos[:, None] * inv[None, :]
            cos = jnp.cos(freqs)[None, None]
            sin = jnp.sin(freqs)[None, None]
            e = t[..., 0::2]
            o = t[..., 1::2]
            eo = e * cos - o * sin
            oo = e * sin + o * cos
            return jnp.stack([eo, oo], axis=-1).reshape(t.shape)
        key = jax.random.key(seed)
        ks = jax.random.split(key, 5)
        B, N = (2, 512)
        s = 0.02
        return {'x': jax.random.normal(ks[0], (B, N, DIM), dtype=jnp.float32), 'qkv_w': jax.random.normal(ks[1], (3 * DIM, DIM), dtype=jnp.float32) * s, 'qkv_b': jax.random.normal(ks[2], (3 * DIM,), dtype=jnp.float32) * s, 'proj_w': jax.random.normal(ks[3], (DIM, DIM), dtype=jnp.float32) * s, 'proj_b': jax.random.normal(ks[4], (DIM,), dtype=jnp.float32) * s}
    _L0_attn_in = _L0_attn_setup()

    def _L0_ffn_setup():
        import jax, jax.numpy as jnp
        import numpy as np
        D_MODEL = 256
        D_FF = 1024
        NUM_EXPERTS = 8
        key = jax.random.key(seed)
        ks = jax.random.split(key, 8)
        scale_in = 1.0 / np.sqrt(D_MODEL)
        scale_ff = 1.0 / np.sqrt(D_FF)
        x = jax.random.normal(ks[0], (4, 512, D_MODEL), dtype=jnp.float32)
        gate_w = jax.random.uniform(ks[1], (NUM_EXPERTS, D_MODEL), jnp.float32, -scale_in, scale_in)
        gate_b = jax.random.uniform(ks[2], (NUM_EXPERTS,), jnp.float32, -scale_in, scale_in)
        expert_bias = jnp.zeros((NUM_EXPERTS,), dtype=jnp.float32)
        w1 = jax.random.uniform(ks[3], (NUM_EXPERTS, D_MODEL, D_FF), jnp.float32, -scale_in, scale_in)
        b1 = jax.random.uniform(ks[4], (NUM_EXPERTS, D_FF), jnp.float32, -scale_in, scale_in)
        w2 = jax.random.uniform(ks[5], (NUM_EXPERTS, D_FF, D_MODEL), jnp.float32, -scale_ff, scale_ff)
        b2 = jax.random.uniform(ks[6], (NUM_EXPERTS, D_MODEL), jnp.float32, -scale_ff, scale_ff)
        return {'x': x, 'gate_w': gate_w, 'gate_b': gate_b, 'expert_bias': expert_bias, 'w1': w1, 'b1': b1, 'w2': w2, 'b2': b2}
    _L0_ffn_in = _L0_ffn_setup()
    _L0_c = _w((lambda *s: np.random.randn(*s).astype(np.float32) * 0.05)(2, 256))
    _L0_wmod = _w((lambda *s: np.random.randn(*s).astype(np.float32) * 0.05)(256, 6 * 256) * 256 ** (-0.5))
    _d = {'L0_attn_x': _L0_attn_in['x'], 'L0_attn_qkv_w': _L0_attn_in['qkv_w'], 'L0_attn_qkv_b': _L0_attn_in['qkv_b'], 'L0_attn_proj_w': _L0_attn_in['proj_w'], 'L0_attn_proj_b': _L0_attn_in['proj_b'], 'L0_ffn_gate_w': _L0_ffn_in['gate_w'], 'L0_ffn_gate_b': _L0_ffn_in['gate_b'], 'L0_ffn_expert_bias': _L0_ffn_in['expert_bias'], 'L0_ffn_w1': _L0_ffn_in['w1'], 'L0_ffn_b1': _L0_ffn_in['b1'], 'L0_ffn_w2': _L0_ffn_in['w2'], 'L0_ffn_b2': _L0_ffn_in['b2'], 'L0_c': _L0_c, 'L0_wmod': _L0_wmod}
    _x0 = _d['L0_attn_x']
    _d['L0_attn_x'] = jax.random.normal(jax.random.fold_in(jax.random.key(seed), 1), (2, 2048, 256), dtype=_x0.dtype)
    del _x0
    return _d

def reference(L0_attn_x, L0_attn_qkv_w, L0_attn_qkv_b, L0_attn_proj_w, L0_attn_proj_b, L0_ffn_gate_w, L0_ffn_gate_b, L0_ffn_expert_bias, L0_ffn_w1, L0_ffn_b1, L0_ffn_w2, L0_ffn_b2, L0_c, L0_wmod):

    def _L0_attn_ref(x, qkv_w, qkv_b, proj_w, proj_b):
        import jax, jax.numpy as jnp
        import numpy as np
        DIM = 256
        NUM_HEADS = 16
        HD = DIM // NUM_HEADS
        ROPE_DIM = 64
        ROPE_BASE = 10000.0

        def _apply_rope(t):
            D = t.shape[-1]
            N = t.shape[2]
            pos = jnp.arange(N, dtype=t.dtype)
            inv = 1.0 / ROPE_BASE ** (jnp.arange(0, D, 2, dtype=t.dtype) / D)
            freqs = pos[:, None] * inv[None, :]
            cos = jnp.cos(freqs)[None, None]
            sin = jnp.sin(freqs)[None, None]
            e = t[..., 0::2]
            o = t[..., 1::2]
            eo = e * cos - o * sin
            oo = e * sin + o * cos
            return jnp.stack([eo, oo], axis=-1).reshape(t.shape)
        B, N, C = x.shape
        H, D = (NUM_HEADS, HD)
        scale = D ** (-0.5)
        qkv = x @ qkv_w.T + qkv_b
        qkv = qkv.reshape(B, N, 3, H, D).transpose(2, 0, 3, 1, 4)
        q, k, v = (qkv[0], qkv[1], qkv[2])
        q = jnp.concatenate([_apply_rope(q[..., :ROPE_DIM]), q[..., ROPE_DIM:]], axis=-1)
        k = jnp.concatenate([_apply_rope(k[..., :ROPE_DIM]), k[..., ROPE_DIM:]], axis=-1)
        attn = jnp.einsum('bhnd,bhmd->bhnm', q, k) * scale
        attn = jax.nn.softmax(attn, axis=-1)
        out = jnp.einsum('bhnm,bhmd->bhnd', attn, v)
        out = out.transpose(0, 2, 1, 3).reshape(B, N, C)
        return out @ proj_w.T + proj_b

    def _L0_ffn_ref(x, gate_w, gate_b, expert_bias, w1, b1, w2, b2):
        import jax, jax.numpy as jnp
        import numpy as np
        D_MODEL = 256
        D_FF = 1024
        NUM_EXPERTS = 8
        gate_logits = jnp.einsum('bsd,ed->bse', x, gate_w) + gate_b + expert_bias
        top_idx = jnp.argmax(gate_logits, axis=-1)
        out = jnp.zeros_like(x)
        for e in range(NUM_EXPERTS):
            mask = (top_idx == e)[..., None].astype(x.dtype)
            h = jax.nn.relu(jnp.einsum('bsd,df->bsf', x, w1[e]) + b1[e])
            y = jnp.einsum('bsf,fd->bsd', h, w2[e]) + b2[e]
            out = out + mask * y
        return out
    x = L0_attn_x
    mod = (_silu(L0_c) @ L0_wmod).reshape(L0_c.shape[0], 6, 1, -1)
    sa, ca, ga, sb, cb, gb = (mod[:, 0], mod[:, 1], mod[:, 2], mod[:, 3], mod[:, 4], mod[:, 5])
    ga = (2 * (ga >= 0) - 1) * jnp.maximum(jnp.abs(ga), 0.25)
    gb = (2 * (gb >= 0) - 1) * jnp.maximum(jnp.abs(gb), 0.25)
    h = _layernorm(x, axis=-1) * (1 + ca) + sa
    x = x + ga * _L0_attn_ref(h, L0_attn_qkv_w, L0_attn_qkv_b, L0_attn_proj_w, L0_attn_proj_b)
    h = _layernorm(x, axis=-1) * (1 + cb) + sb
    x = x + gb * _L0_ffn_ref(h, L0_ffn_gate_w, L0_ffn_gate_b, L0_ffn_expert_bias, L0_ffn_w1, L0_ffn_b1, L0_ffn_w2, L0_ffn_b2)
    return x

_drawn_inputs = setup_inputs


def setup_inputs(seed=0):
    import zlib

    import numpy as np

    out = dict(_drawn_inputs(seed))
    spreads = {'L0_ffn_expert_bias': (0.0, 0.33)}
    factors = {'L0_attn_qkv_w': 8.0,
     'L0_attn_qkv_b': 8.0,
     'L0_attn_proj_w': 8.0,
     'L0_attn_proj_b': 8.0,
     'L0_ffn_gate_b': 3.741,
     'L0_ffn_b1': 28.057,
     'L0_ffn_b2': 8.0}
    for name, (base, spread) in spreads.items():
        noise = np.random.default_rng([zlib.crc32(name.encode()), seed]).standard_normal(out[name].shape)
        drawn = base * np.exp(spread * noise) if base else spread * noise
        out[name] = jnp.asarray(drawn.astype(out[name].dtype))
    for name, factor in factors.items():
        out[name] = (out[name] * factor).astype(out[name].dtype)
    return out
```

```python
from contextlib import ExitStack

import numpy as np
import concourse.bass as bass
from concourse import mybir

ALU = mybir.AluOpType
ACT = mybir.ActivationFunctionType
AX = mybir.AxisListType.X
F32 = mybir.dt.float32
F32R = mybir.dt.float32r
I32 = mybir.dt.int32
U32 = mybir.dt.uint32

P = 128
B, N, D = 2, 2048, 256
H, HD = 16, 16
F, E = 1024, 8
T = B * N // P
TB = N // P
KD = D // P
KF = F // P
QKV = 3 * D
EPS = 1e-5
SCALE = HD ** -0.5
PAIRS = H // 2
UNITS = B * PAIRS
CH = 512
CHUNKS = N // CH
STEPS = UNITS * CHUNKS
ROWS = 50
GROUP = 8
FT = 256
NT = (B * N) // FT + E - 1
AHEAD = 2


class Ctx:
    pass


def open_sem(ctx, nc, stage):
    return lambda name: ctx.enter_context(nc.semaphore(f"{stage}_{name}"))


def open_mem(ctx, nc, stage):
    sb = lambda name, shape, dt=F32: ctx.enter_context(nc.sbuf_tensor(f"{stage}_{name}", shape, dt))
    ps = lambda name, shape, dt=F32: ctx.enter_context(nc.psum_tensor(f"{stage}_{name}", shape, dt))
    return sb, ps


def setup(nc, g):
    with ExitStack() as ctx:
        sem = open_sem(ctx, nc, "set")
        sb, ps = open_mem(ctx, nc, "set")
        cT = sb("cT", [P, KD, B])
        cs = sb("cs", [P, 3, KD * B])
        cb = sb("cb", [P, KD, B, P])
        wmod = sb("wmod", [P, KD, 6 * D])
        st = sb("st", [P, T, 6])
        mag = sb("mag", [P, B, D])
        psm = [ps(f"psm{b}", [P, 6 * D]) for b in range(B)]
        s_x, s_c, s_w, s_id = sem("s_x"), sem("s_c"), sem("s_w"), sem("s_id")
        s_exp, s_v, s_cb, s_mod, s_ev = sem("s_exp"), sem("s_v"), sem("s_cb"), sem("s_mod"), sem("s_ev")
        s_mv, s_sd = sem("s_mv"), sem("s_sd")
        block = ctx.enter_context(nc.Block())

        @block.sync
        def _(sp):
            sp.dma_start(cT[:], g.cT.rearrange("(k p) b -> p k b", p=P)).then_inc(s_c, 16)
            sp.dma_start(wmod[:], g.wmod.rearrange("(k p) n -> p k n", p=P)).then_inc(s_w, 16)
            xd = g.x.rearrange("b (t p) d -> p (b t) d", p=P)
            for i in range(4):
                sp.dma_start(g.X[:, i * 8:(i + 1) * 8, :], xd[:, i * 8:(i + 1) * 8, :]).then_inc(s_x, 16)
            sp.wait_ge(s_c, 16)
            sp.wait_ge(s_w, 16)
            sp.wait_ge(s_x, 64)

        @block.gpsimd
        def _(pool):
            nc.gpsimd.memset(g.ident[:], 0.0).then_inc(s_id, 1)
            pool.wait_ge(s_id, 1)
            nc.gpsimd.affine_select(out=g.ident[:], in_=g.ident[:], compare_op=ALU.not_equal, fill=1.0, base=0,
                                    pattern=[[-1, P]], channel_multiplier=1).then_inc(s_id, 1)
            pool.wait_ge(s_id, 2)

        @block.scalar
        def _(act):
            act.wait_ge(s_c, 16)
            nc.scalar.activation(cs[:, 0, :], cT[:].rearrange("p k b -> p (k b)"), ACT.Exp, scale=-1.0).then_inc(s_exp, 1)
            act.wait_ge(s_mv, 2)
            nc.scalar.activation(g.sd[:, 0, :], g.sd[:, 1, :], ACT.Sqrt).then_inc(s_sd, 1)

        @block.vector
        def _(dve):
            dve.wait_ge(s_exp, 1)
            nc.vector.tensor_scalar_add(cs[:, 1, :], cs[:, 0, :], 1.0).then_inc(s_v, 1)
            dve.wait_ge(s_v, 1)
            nc.vector.reciprocal(cs[:, 2, :], cs[:, 1, :]).then_inc(s_v, 1)
            dve.wait_ge(s_v, 2)
            nc.vector.tensor_mul(cs[:, 0, :], cs[:, 2, :], cT[:].rearrange("p k b -> p (k b)")).then_inc(s_v, 1)
            dve.wait_ge(s_v, 3)
            for k in range(KD):
                for b in range(B):
                    last = nc.vector.tensor_copy(cb[:, k, b, :], cs[:, 0, k * B + b:k * B + b + 1].to_broadcast([P, P]))
            last.then_inc(s_cb, 1)
            dve.wait_ge(s_x, 64)
            for t in range(T):
                last = nc.vector.bn_stats(st[:, t, :], g.X[:, t, :])
            last.then_inc(s_mv, 1)
            dve.wait_ge(s_mv, 1)
            for t in range(T):
                last = nc.vector.bn_aggr(g.mv[:, t, :], st[:, t, :])
            last.then_inc(s_v, 1)
            dve.wait_ge(s_v, 4)
            nc.vector.tensor_scalar_add(g.sd[:, 1, :], g.mv[:, :, 1], EPS).then_inc(s_mv, 1)
            dve.wait_ge(s_mod, 1)
            for b in range(B):
                for j, part in enumerate(("shift", "scale", "gate") * 2):
                    src, dst = psm[b][:, j * D:(j + 1) * D], g.mod[:, b, j, :]
                    if part == "scale":
                        nc.vector.tensor_scalar_add(dst, src, 1.0).then_inc(s_ev, 1)
                    else:
                        nc.vector.tensor_copy(dst, src).then_inc(s_ev, 1)
            dve.wait_ge(s_ev, 6 * B)
            n = 4
            for j in (2, 5):
                gate = g.mod[:, :, j, :]
                nc.vector.scalar_tensor_tensor(mag[:], gate, -1.0, gate, ALU.mult, ALU.max).then_inc(s_v, 1)
                dve.wait_ge(s_v, n + 1)
                nc.vector.tensor_scalar_max(mag[:], mag[:], 0.25).then_inc(s_v, 1)
                nc.vector.tensor_scalar(gate, gate, 0.0, 2.0, ALU.is_ge, ALU.mult).then_inc(s_v, 1)
                dve.wait_ge(s_v, n + 3)
                nc.vector.scalar_tensor_tensor(gate, gate, -1.0, mag[:], ALU.add, ALU.mult).then_inc(s_v, 1)
                dve.wait_ge(s_v, n + 4)
                n += 4
            inverse_deviation(nc, dve, g, s_sd, s_v, n)

        @block.tensor
        def _(pe):
            pe.wait_ge(s_cb, 1)
            pe.wait_ge(s_w, 16)
            for b in range(B):
                for j in range(3):
                    for k in range(KD):
                        last = nc.tensor.matmul(psm[b][:, j * 512:(j + 1) * 512], cb[:, k, b, :],
                                                wmod[:, k, j * 512:(j + 1) * 512], start=k == 0, stop=k == KD - 1)
            last.then_inc(s_mod, 1)


def inverse_deviation(nc, dve, g, s_sd, s_v, n):
    dve.wait_ge(s_sd, 1)
    nc.vector.reciprocal(g.sd[:, 2, :], g.sd[:, 0, :]).then_inc(s_v, 1)
    dve.wait_ge(s_v, n + 1)
    nc.vector.tensor_mul(g.sd[:, 2, :], g.sd[:, 2, :], g.sd[:, 1, :]).then_inc(s_v, 1)
    dve.wait_ge(s_v, n + 2)
    nc.vector.tensor_add(g.sd[:, 2, :], g.sd[:, 2, :], g.sd[:, 0, :]).then_inc(s_v, 1)
    dve.wait_ge(s_v, n + 3)
    nc.vector.tensor_scalar_mul(g.sd[:, 2, :], g.sd[:, 2, :], 0.5).then_inc(s_v, 1)
    dve.wait_ge(s_v, n + 4)
    nc.vector.reciprocal(g.rs[:], g.sd[:, 2, :]).then_inc(s_v, 1)
    dve.wait_ge(s_v, n + 5)


def qkv_stage(nc, g):
    with ExitStack() as ctx:
        sem = open_sem(ctx, nc, "qkv")
        sb, ps = open_mem(ctx, nc, "qkv")
        wq = sb("wq", [P, KD, QKV])
        qb = sb("qb", [P, QKV])
        tab = sb("tab", [P, 2, TB, HD])
        hn = sb("hn", [P, 2, D])
        hm = sb("hm", [P, 2, D])
        hT = sb("hT", [P, 2, KD, P])
        qk = sb("qk", [P, 2, 2 * D])
        rc = sb("rc", [P, 2, 2 * D])
        rw = sb("rw", [P, 2, 2 * D])
        rq = sb("rq", [P, 2, 2 * D])
        zero = sb("zero", [P, 2048])
        hi = [sb(f"hi{i}", [P, 4, CH], F32R) for i in range(2)]
        lo = [sb(f"lo{i}", [P, 4, CH], F32R) for i in range(2)]
        pst = [ps(f"pst{i}", [P, KD, P]) for i in range(2)]
        psq = [ps(f"psq{i}", [P, 1024]) for i in range(2)]
        psr = [ps(f"psr{i}", [P, 4, P]) for i in range(2)]
        names = "s_par s_zero s_fill s_hn s_hm s_tr s_hT s_q s_qb s_vb s_rc s_rw s_rq s_rt s_hi s_lo s_put0 s_put1 s_tick s_tick_sp"
        (s_par, s_zero, s_fill, s_hn, s_hm, s_tr, s_hT, s_q, s_qb, s_vb, s_rc, s_rw, s_rq, s_rt, s_hi, s_lo,
         s_put0, s_put1, s_tick, s_tick_sp) = [sem(n) for n in names.split()]
        s_put = [s_put0, s_put1]
        block = ctx.enter_context(nc.Block())


        @block.sync
        def _(sp):
            sp.dma_start(wq[:], g.wqkvT.rearrange("(k p) n -> p k n", p=P)).then_inc(s_par, 16)
            sp.dma_start(qb[:], g.qkv_b.partition_broadcast(P)).then_inc(s_par, 16)
            sp.dma_start(tab[:], g.rope.rearrange("a (t p) d -> p a t d", p=P)).then_inc(s_par, 16)
            sp.wait_ge(s_zero, 1)
            rows = 2048 // D
            left = g.hs.shape[0] // P - (g.hs.shape[0] // P // rows) * rows
            full = g.hs.shape[0] // P // rows
            hs = g.hs[0:full * rows * P, :].rearrange("(n p r) d -> n p (r d)", r=rows, p=P) if full else None
            for n in range(full):
                sp.dma_start(hs[n], zero[:]).then_inc(s_fill, 16)
            if left:
                sp.dma_start(g.hs[full * rows * P:, :].rearrange("(p r) d -> p (r d)", r=left, p=P),
                             zero[:, 0:left * D]).then_inc(s_fill, 16)
            for c in range(2):
                sp.sem_inc(s_put[c], 16)
            with sp.Fori(0, B) as b:
                with sp.Fori(0, 2) as half:
                    m = 2 * b + half
                    for c in range(2):
                        sp.wait_ge(s_lo, GROUP * m + 4 * c + 4 + AHEAD)
                        sp.sem_inc(s_tick_sp)
                        cols = bass.ds(half * 2 * CH + c * CH, CH)
                        for part, buf in enumerate((hi, lo)):
                            dst = g.qkT[part].rearrange("q (b f p) n -> q b f p n", b=B, p=P)
                            for q in range(2):
                                sp.dma_start(
                                    dst[q, bass.ds(b, 1), :, :, cols].rearrange("o f p n -> p (o f) n"),
                                    buf[c][:, 2 * q:2 * q + 2, :].bitcast(F32)).then_inc(s_put[c], 16)
            for c in range(2):
                sp.wait_ge(s_put[c], 64 * T // GROUP + 16)
            sp.wait_ge(s_fill, 16 * (full + (1 if left else 0)))

        @block.gpsimd
        def _(pool):
            nc.gpsimd.memset(zero[:], 0.0).then_inc(s_zero, 1)
            pool.wait_ge(s_par, 48)
            with pool.Fori(0, B) as b:
                with pool.Fori(0, 2) as half:
                    m = 2 * b + half

                    def modulate(r):
                        t = GROUP * m + r
                        pool.wait_ge(s_hn, t + 1)
                        if r >= 2:
                            pool.wait_ge(s_tr, t - 1)
                        pool.sem_inc(s_tick)
                        nc.gpsimd.tensor_mul(hm[:, r % 2, :], hn[:, r % 2, :], g.mod[:, bass.ds(b, 1), 1, :].rearrange("p o d -> p (o d)")).then_inc(s_hm, 1)
                        pool.wait_ge(s_hm, 2 * t + 1)
                        pool.sem_inc(s_tick)
                        nc.gpsimd.tensor_add(hm[:, r % 2, :], hm[:, r % 2, :], g.mod[:, bass.ds(b, 1), 0, :].rearrange("p o d -> p (o d)")).then_inc(s_hm, 1)

                    def swapped(r):
                        t = GROUP * m + r
                        pool.wait_ge(s_qb, t + 1)
                        if r >= 2:
                            pool.wait_ge(s_rq, t - 1)
                        src = qk[:, r % 2, :].rearrange("p (h i e) -> p h i e", h=2 * H, e=2)
                        dst = rw[:, r % 2, :].rearrange("p (h i e) -> p h i e", h=2 * H, e=2)
                        sn = tab[:, 1, bass.ds(8 * half + r, 1), :].rearrange("p o (i e) -> p o i e", e=2)
                        pool.sem_inc(s_tick)
                        for e in range(2):
                            last = nc.gpsimd.tensor_mul(dst[:, :, :, e], src[:, :, :, 1 - e],
                                                        sn[:, :, :, e].to_broadcast([P, 2 * H, HD // 2]))
                        last.then_inc(s_rw, 1)

                    for k in range(GROUP + 1):
                        if k < GROUP:
                            modulate(k)
                        if k:
                            swapped(k - 1)

        @block.scalar
        def _(act):
            with act.Fori(0, T // GROUP) as m:
                for k in range(GROUP + 1):
                    if k < GROUP:
                        t = GROUP * m + k
                        act.wait_ge(s_tr, t + 1)
                        if k >= 2:
                            act.wait_ge(s_q, t - 1)
                        nc.scalar.copy(hT[:, k % 2, :, :], pst[k % 2][:]).then_inc(s_hT, 1)
                    if k:
                        r = k - 1
                        c, o = r // 4, (r % 4) * P
                        act.wait_ge(s_rt, GROUP * m + r + 1)
                        if r % 4 == 0:
                            act.wait_ge(s_put[c], 64 * m + 16)
                        nc.scalar.mul(hi[c][:, 0:2, o:o + P], psr[r % 2][:, 0:2, :], SCALE)
                        nc.scalar.copy(hi[c][:, 2:4, o:o + P], psr[r % 2][:, 2:4, :]).then_inc(s_hi, 1)

        @block.vector
        def _(dve):
            dve.wait_ge(s_par, 48)
            dve.sem_inc(s_lo, AHEAD)
            with dve.Fori(0, B) as b:
                with dve.Fori(0, 2) as half:
                    m = 2 * b + half

                    def normalise(r):
                        t = GROUP * m + r
                        if r >= 2:
                            dve.wait_ge(s_hm, 2 * t - 2)
                        nc.vector.tensor_scalar(hn[:, r % 2, :], g.X[:, bass.ds(t, 1), :].rearrange("p o d -> p (o d)"),
                                                g.mv[:, bass.ds(t, 1), 0], g.rs[:, bass.ds(t, 1)],
                                                ALU.subtract, ALU.mult).then_inc(s_hn, 1)

                    def add_bias(r):
                        t = GROUP * m + r
                        dve.wait_ge(s_q, t + 1)
                        if r >= 2:
                            dve.wait_ge(s_rw, t - 1)
                        nc.vector.tensor_add(qk[:, r % 2, :], psq[r % 2][:, 0:2 * D], qb[:, 0:2 * D]).then_inc(s_qb, 1)
                        v = g.V[:].rearrange("p (b h) t e -> p b h t e", b=B)
                        nc.vector.tensor_add(
                            v[:, bass.ds(b, 1), :, bass.ds(8 * half + r, 1), :].rearrange("p o h u e -> p (o h u) e"),
                            psq[r % 2][:, 2 * D:3 * D].rearrange("p (h e) -> p h e", h=PAIRS),
                            qb[:, 2 * D:3 * D].rearrange("p (h e) -> p h e", h=PAIRS)).then_inc(s_vb, 1)

                    def rotate(r):
                        t = GROUP * m + r
                        src = qk[:, r % 2, :].rearrange("p (h e) -> p h e", h=2 * H)
                        dve.wait_ge(s_qb, t + 1)
                        nc.vector.tensor_mul(rc[:, r % 2, :].rearrange("p (h e) -> p h e", h=2 * H), src,
                                             tab[:, 0, bass.ds(8 * half + r, 1), :].to_broadcast([P, 2 * H, HD])).then_inc(s_rc, 1)
                        dve.wait_ge(s_rc, t + 1)
                        dve.wait_ge(s_rw, t + 1)
                        if r >= 2:
                            dve.wait_ge(s_rt, t - 1)
                        nc.vector.tensor_add(rq[:, r % 2, :], rc[:, r % 2, :], rw[:, r % 2, :]).then_inc(s_rq, 1)

                    def low_part(r):
                        t = GROUP * m + r
                        c, o = r // 4, (r % 4) * P
                        dve.wait_ge(s_hi, t + 1)
                        if r % 4 == 0:
                            dve.wait_ge(s_put[c], 64 * m + 16)
                        for q, scale in ((0, SCALE), (1, 1.0)):
                            last = nc.vector.scalar_tensor_tensor(
                                lo[c][:, 2 * q:2 * q + 2, o:o + P], psr[r % 2][:, 2 * q:2 * q + 2, :], scale,
                                hi[c][:, 2 * q:2 * q + 2, o:o + P].bitcast(F32), ALU.mult, ALU.subtract)
                        last.then_inc(s_lo, 1)

                    for k in range(GROUP + 2):
                        if k < GROUP:
                            normalise(k)
                        if 1 <= k <= GROUP:
                            add_bias(k - 1)
                            rotate(k - 1)
                        if k >= 2:
                            low_part(k - 2)

        @block.tensor
        def _(pe):
            pe.wait_ge(s_par, 48)
            with pe.Fori(0, T // GROUP) as m:
                def tiles_in(r):
                    t = GROUP * m + r
                    pe.wait_ge(s_hm, 2 * t + 2)
                    if r >= 2:
                        pe.wait_ge(s_hT, t - 1)
                    for k in range(KD):
                        last = nc.tensor.transpose(pst[r % 2][:, k, :], hm[:, r % 2, k * P:(k + 1) * P], g.ident[:])
                    last.then_inc(s_tr, 1)

                def project(r):
                    t = GROUP * m + r
                    pe.wait_ge(s_hT, t + 1)
                    if r >= 2:
                        pe.wait_ge(s_vb, t - 1)
                    for n0, n1 in ((0, 512), (512, QKV)):
                        for k in range(KD):
                            last = nc.tensor.matmul(psq[r % 2][:, n0:n1], hT[:, r % 2, k, :], wq[:, k, n0:n1],
                                                    start=k == 0, stop=k == KD - 1)
                    last.then_inc(s_q, 1)

                def tiles_out(r):
                    t = GROUP * m + r
                    pe.wait_ge(s_rq, t + 1)
                    pe.wait_ge(s_lo, t - 1 + AHEAD if r >= 2 else t - r + AHEAD)
                    for k in range(4):
                        last = nc.tensor.transpose(psr[r % 2][:, k, :], rq[:, r % 2, k * P:(k + 1) * P], g.ident[:])
                    last.then_inc(s_rt, 1)

                for k in range(GROUP + 2):
                    if k < GROUP:
                        tiles_in(k)
                    if 1 <= k <= GROUP:
                        project(k - 1)
                    if k >= 2:
                        tiles_out(k - 2)


def attention(nc, g):
    KT = N // P
    GROUPS = KT // 2
    EARLY = 2
    SLOTS = 8
    BODY = GROUP
    ITERS = STEPS // BODY
    VW = 32
    WIDTH = HD + 1
    USED = 64 + ROWS
    with ExitStack() as ctx:
        sem = open_sem(ctx, nc, "att")
        sb, ps = open_mem(ctx, nc, "att")
        K = [sb(f"K{i}", [P, N], F32R) for i in range(2)]
        QM = [sb(f"QM{i}", [P, 2, CH], F32R) for i in range(2)]
        QE = [sb(f"QE{i}", [P, 2, CH], F32R) for i in range(2)]
        VU = [sb(f"VU{i}", [P, KT, 2, VW]) for i in range(2)]
        probs = sb("probs", [P, SLOTS, 2 * CH])
        mx = sb("mx", [P, 8, 4])
        m8 = sb("m8", [P, 8])
        mh = sb("mh", [P, 8], F32R)
        mt = sb("mt", [P, 4, P])
        sums = sb("sums", [P, CH])
        sel = sb("sel", [P, 2, WIDTH])
        rden = sb("rden", [P, 4, 2])
        PS = [ps(f"PS{i}", [P, 2 * CH]) for i in range(2)]
        PM = [ps(f"PM{i}", [P, CH]) for i in range(2)]
        PV = ps("PV", [P, CH])
        MISC = ps("MISC", [P, CH])

        keys_in = [sem(f"keys_in{i}") for i in range(2)]
        queries_in = [sem(f"queries_in{i}") for i in range(2)]
        queries_moved = sem("queries_moved")
        buffers_set = sem("buffers_set")
        sel_set = sem("sel_set")
        values_in = sem("values_in")
        max_products = sem("max_products")
        maxima = sem("maxima")
        chain = sem("chain")
        shifts_ready = sem("shifts_ready")
        shifts_turned = sem("shifts_turned")
        shifts_placed = sem("shifts_placed")
        scores = sem("scores")
        exps = sem("exps")
        pv_groups = sem("pv_groups")
        sums_out = sem("sums_out")
        gathered = sem("gathered")
        recips = sem("recips")
        outputs = sem("outputs")
        tick, tick_sp = sem("tick"), sem("tick_sp")
        block = ctx.enter_context(nc.Block())

        def steps_done(n):
            return GROUPS * n + SLOTS // 2

        def over_iterations(eng, body):
            with eng.Fori(0, ITERS - 1) as it:
                body(it, False)
            body(ITERS - 1, True)

        @block.sync
        def _(sp):
            def hold(semaphore, value):
                sp.wait_ge(semaphore, value)
                sp.sem_inc(tick_sp)

            def rows(part, which, first, cols):
                return g.qkT[part][which, bass.ds(first, HD), cols]

            def load_keys(i, unit):
                for hh in range(2):
                    for at, part in ((0, 0), (16, 1), (34, 0)):
                        sp.dma_start(K[i][64 * hh + at:64 * hh + at + HD, :].bitcast(F32),
                                     rows(part, 1, unit * 2 * HD + HD * hh, slice(0, N))).then_inc(keys_in[i], 16)

            def load_queries(i, unit, c):
                for hh in range(2):
                    for at, part in ((0, 0), (16, 0), (34, 1)):
                        sp.dma_start(QM[i][64 * hh + at:64 * hh + at + HD, hh, :].bitcast(F32),
                                     rows(part, 0, unit * 2 * HD + HD * hh, slice(c * CH, (c + 1) * CH))
                                     ).then_inc(queries_in[i], 16)

            def move_queries(i):
                sp.dma_start(QE[i][:].bitcast(F32), QM[i][:].bitcast(F32)).then_inc(queries_moved, 16)

            hold(buffers_set, 8)
            load_keys(0, 0)
            load_queries(0, 0, 0)
            load_queries(1, 0, 1)
            load_keys(1, 1)
            hold(queries_in[0], 96)
            move_queries(0)
            hold(queries_moved, 16)
            hold(max_products, 32)
            load_queries(0, 0, 2)

            def body(it, last):
                for r in range(BODY):
                    s = BODY * it + r
                    if r % CHUNKS == 1 and not (last or r < CHUNKS):
                        hold(pv_groups, steps_done(s - 1))
                        load_keys(0, 2 * it + 2)
                    if not (last and r == BODY - 1):
                        n = (r + 1) // 2
                        hold(queries_in[(r + 1) % 2], 96 * (4 * it + n + 1))
                        hold(pv_groups, steps_done(s))
                        move_queries((r + 1) % 2)
                    if not (last and r >= BODY - 3):
                        hold(max_products, 32 * (s + 2))
                        hold(queries_moved, 16 * (s + 2))
                        n = r + 3
                        load_queries((r + 1) % 2, 2 * it + n // CHUNKS, n % CHUNKS)
                if not last:
                    hold(pv_groups, steps_done(BODY * it + BODY))
                    load_keys(1, 2 * it + 3)

            over_iterations(sp, body)

        @block.gpsimd
        def _(pool):
            for i in range(2):
                nc.gpsimd.memset(K[i][:].bitcast(F32), 1.0).then_inc(buffers_set, 1)
                nc.gpsimd.memset(QM[i][:].bitcast(F32), 0.0).then_inc(buffers_set, 1)
                nc.gpsimd.memset(VU[i][:], 0.0).then_inc(buffers_set, 1)
            nc.gpsimd.memset(mt[:], 0.0).then_inc(buffers_set, 1)
            nc.gpsimd.memset(sel[:], 0.0).then_inc(buffers_set, 1)
            pool.wait_ge(buffers_set, 8)
            for i in range(2):
                nc.gpsimd.memset(VU[i][:, :, :, HD:WIDTH], 1.0).then_inc(sel_set, 1)
            for hh in range(2):
                for par in range(2):
                    nc.gpsimd.affine_select(out=sel[:, hh, :], in_=sel[:, hh, :], compare_op=ALU.not_equal, fill=1.0,
                                            base=-32 * (2 * hh + par), pattern=[[-1, WIDTH]],
                                            channel_multiplier=1).then_inc(sel_set, 1)
                    pool.wait_ge(sel_set, 3 + 2 * hh + par)

            def load_values(i, unit):
                nc.gpsimd.tensor_copy(VU[i][:, :, :, 0:HD],
                                      g.V[:, bass.ds(unit, 1), :, :].rearrange("p o t (h e) -> p (o t) h e", h=2)
                                      ).then_inc(values_in, 1)

            load_values(0, 0)
            load_values(1, 1)

            def body(it, last):
                if last:
                    return
                for i in range(2):
                    pool.wait_ge(pv_groups, steps_done(BODY * it + CHUNKS * (i + 1)))
                    pool.sem_inc(tick)
                    load_values(i, 2 * it + 2 + i)

            over_iterations(pool, body)

        @block.tensor
        def _(pe):
            def score_products(s, r, kt):
                pe.wait_ge(exps, KT * s + kt + 1)
                for hh in range(2):
                    last = nc.tensor.matmul(PS[kt % 2][:, hh * CH:(hh + 1) * CH],
                                            K[r % BODY // CHUNKS][0:USED, kt * P:(kt + 1) * P], QE[r % 2][0:USED, hh, :],
                                            start=True, stop=True)
                last.then_inc(scores, 1)

            def max_group(s, r, it, grp, h):
                qt, i = grp // 2, (r % BODY) // CHUNKS
                if grp == 0 and h == 0:
                    pe.wait_ge(queries_in[r % 2], 96 * (4 * it + r // 2 + 1))
                    if r % CHUNKS == 0:
                        pe.wait_ge(keys_in[i], 96 * (it + r // BODY + 1))
                kc = 2 * (grp % 2) + h
                for hh in range(2):
                    n = 32 * s + 8 * qt + 2 * kc + hh
                    pe.wait_ge(maxima, n + 1)
                    nc.tensor.matmul(PM[hh][:], QM[r % 2][0:USED, hh, qt * P:(qt + 1) * P],
                                     K[i][0:USED, kc * CH:(kc + 1) * CH], start=True, stop=True
                                     ).then_inc(max_products, 1)

            def turn_shifts(s):
                pe.wait_ge(shifts_ready, s + 1)
                pe.wait_ge(outputs, s if not isinstance(s, int) else max(s, 1))
                for qt in range(4):
                    last = nc.tensor.transpose(MISC[:, qt * P:(qt + 1) * P], mt[:, qt, :], g.ident[:])
                last.then_inc(shifts_turned, 1)

            def value_products(s, r, it, j):
                pe.wait_ge(exps, KT * s + 2 * j + 2 + AHEAD)
                if j == 0:
                    pe.wait_ge(sums_out, s + 1)
                    pe.wait_ge(values_in, 2 * it + r // CHUNKS + 1)
                for hh in range(2):
                    for par in range(2):
                        kt, quad = 2 * j + par, 2 * hh + par
                        last = nc.tensor.matmul(PV[32 * quad:32 * quad + VW, :], VU[r // CHUNKS][:, kt, hh, :],
                                                probs[:, kt % SLOTS, hh * CH:(hh + 1) * CH],
                                                start=j == 0, stop=j == GROUPS - 1, tile_position=(0, 32 * quad))
                last.then_inc(pv_groups, 1)

            def gather(s):
                pe.wait_ge(outputs, s + 1)
                pe.wait_ge(sums_out, s + 2)
                for qt in range(4):
                    last = nc.tensor.matmul(MISC[:, qt * 2 * WIDTH:(qt + 1) * 2 * WIDTH], sums[:, qt * P:(qt + 1) * P],
                                            sel[:].rearrange("p h e -> p (h e)"), start=True, stop=True)
                last.then_inc(gathered, 1)

            pe.sem_inc(pv_groups, SLOTS // 2)
            pe.sem_inc(gathered, 1)
            pe.wait_ge(sel_set, 6)
            for grp in range(2 * GROUPS):
                max_group(0, 0, 0, grp // 2, grp % 2)
            turn_shifts(0)
            for grp in range(2 * EARLY):
                max_group(1, 1, 0, grp // 2, grp % 2)
            pe.wait_ge(shifts_placed, 2)
            for kt in range(2):
                score_products(0, 0, kt)

            def body(it, last):
                for r in range(BODY):
                    s = BODY * it + r
                    final = last and r == BODY - 1
                    for j in range(GROUPS):
                        def maxima_half(h):
                            if j < GROUPS - EARLY:
                                if not final:
                                    max_group(s + 1, r + 1, it, j + EARLY, h)
                            elif not (last and r >= BODY - 2):
                                max_group(s + 2, r + 2, it, j - GROUPS + EARLY, h)

                        maxima_half(0)
                        if j == GROUPS - 1 and not final:
                            pe.wait_ge(shifts_placed, 2 * s + 4)
                        for h in range(2):
                            if j < GROUPS - 1:
                                score_products(s, r, 2 * j + 2 + h)
                            elif not final:
                                score_products(s + 1, r + 1, h)
                        maxima_half(1)
                        if j == 2 and r > 0:
                            pe.wait_ge(shifts_placed, 2 * s + 2)
                            gather(s - 1)
                        if j == GROUPS - 2 and not final:
                            turn_shifts(s + 1)
                        value_products(s, r, it, j)
                if not final:
                    pe.wait_ge(shifts_placed, 2 * s + 4)
                gather(s)

            over_iterations(pe, body)

        @block.scalar
        def _(act):
            def place_shifts(s, r):
                act.wait_ge(queries_moved, 16 * (s + 1))
                act.wait_ge(shifts_turned, s + 1)
                for hh in range(2):
                    at = slice(64 * hh + 32, 64 * hh + 34)
                    nc.scalar.copy(QE[r % 2][at, hh, :], MISC[at, :]).then_inc(shifts_placed, 1)

            act.sem_inc(exps, AHEAD)
            act.sem_inc(sums_out, 1)
            place_shifts(0, 0)

            def body(it, last):
                for r in range(BODY):
                    s = BODY * it + r
                    for kt in range(KT):
                        n = KT * s + kt
                        if kt == KT - 2 and not (last and r == BODY - 1):
                            place_shifts(s + 1, r + 1)
                        if kt % 2 == 0:
                            act.wait_ge(pv_groups, (KT // 2) * s + kt // 2 + 1)
                        act.wait_ge(scores, n + 1)
                        nc.scalar.activation(probs[:, kt % SLOTS, :], PS[kt % 2][:], ACT.Exp).then_inc(exps, 1)
                    act.wait_ge(pv_groups, steps_done(s + 1))
                    act.wait_ge(gathered, s + 1)
                    nc.scalar.copy(sums[:], PV[:]).then_inc(sums_out, 1)

            over_iterations(act, body)

        @block.vector
        def _(dve):
            def max_group(s, grp):
                qt = grp // 2
                for kc in range(2 * (grp % 2), 2 * (grp % 2) + 2):
                    for hh in range(2):
                        n = 32 * s + 8 * qt + 2 * kc + hh
                        dve.wait_ge(max_products, n + 1)
                        nc.vector.reduce_max(mx[:, 2 * qt + hh, kc:kc + 1], PM[hh][:], AX).then_inc(maxima, 1)

            def shifts(s):
                dve.wait_ge(maxima, 32 * s + 32 + AHEAD)
                nc.vector.reduce_max(m8[:], mx[:], AX).then_inc(chain, 1)
                dve.wait_ge(chain, 3 * s + 1)
                nc.vector.tensor_scalar_mul(mh[:], m8[:], -1.0).then_inc(chain, 1)
                if not (isinstance(s, int) and s == 0):
                    dve.wait_ge(shifts_turned, s)
                dve.wait_ge(chain, 3 * s + 2)
                cols = mt[:].rearrange("p q (h c) -> p q h c", h=2)
                m = m8[:].rearrange("p (q h) -> p q h", h=2)
                top = mh[:].bitcast(F32).rearrange("p (q h) -> p q h", h=2)
                nc.vector.tensor_copy(cols[:, :, :, 32], top).then_inc(chain, 1)
                nc.vector.scalar_tensor_tensor(cols[:, :, :, 33], m, -1.0, top, ALU.mult, ALU.subtract
                                               ).then_inc(shifts_ready, 1)

            def normalise(s, it, r):
                dve.wait_ge(gathered, s + 2)
                src = MISC[:, 0:8 * WIDTH].rearrange("p (q h e) -> p q h e", q=4, h=2)
                nc.vector.reciprocal(rden[:], src[:, :, :, HD]).then_inc(recips, 1)
                dve.wait_ge(recips, s + 1)
                u = 2 * it + r // CHUNKS
                t0 = 4 * (r % CHUNKS)
                for hh in range(2):
                    last = nc.vector.tensor_mul(
                        g.O[:, bass.ds(u, 1), t0:t0 + 4, hh * HD:(hh + 1) * HD].rearrange("p o t e -> p (o t) e"),
                        src[:, :, hh, 0:HD], rden[:, :, hh:hh + 1].to_broadcast([P, 4, HD]))
                last.then_inc(outputs, 1)

            dve.sem_inc(maxima, AHEAD)
            dve.sem_inc(outputs, 1)
            dve.wait_ge(buffers_set, 8)
            for grp in range(GROUPS):
                max_group(0, grp)
            shifts(0)
            for grp in range(EARLY):
                max_group(1, grp)

            def body(it, last):
                for r in range(BODY):
                    s = BODY * it + r
                    final = last and r == BODY - 1
                    for j in range(GROUPS):
                        if j < GROUPS - EARLY:
                            if not final:
                                max_group(s + 1, j + EARLY)
                                if j == GROUPS - EARLY - 1:
                                    shifts(s + 1)
                        elif not (last and r >= BODY - 2):
                            max_group(s + 2, j - GROUPS + EARLY)
                        if j == 3 and r > 0:
                            normalise(s - 1, it, r - 1)
                normalise(s, it, r)

            over_iterations(dve, body)



def projection(nc, g):
    with ExitStack() as ctx:
        sem = open_sem(ctx, nc, "proj")
        sb, ps = open_mem(ctx, nc, "proj")
        wp = sb("wp", [P, KD, D])
        pb = sb("pb", [P, D])
        oc = sb("oc", [P, 2, D])
        oT = sb("oT", [P, 2, KD, P])
        y = sb("y", [P, 2, D])
        yg = sb("yg", [P, 2, D])
        st = sb("st2", [P, T, 6])
        pst = [ps(f"pst{i}", [P, KD, P]) for i in range(2)]
        psy = [ps(f"psy{i}", [P, CH]) for i in range(2)]
        (s_par, s_oc, s_tr, s_oT, s_prod, s_y, s_yg, s_x, s_st, s_tick) = [
            sem(n) for n in "s_par s_oc s_tr s_oT s_prod s_y s_yg s_x s_st s_tick".split()]
        block = ctx.enter_context(nc.Block())


        @block.sync
        def _(sp):
            sp.dma_start(wp[:], g.wpT.rearrange("(k p) n -> p k n", p=P)).then_inc(s_par, 16)
            sp.dma_start(pb[:], g.proj_b.partition_broadcast(P)).then_inc(s_par, 16)
            sp.wait_ge(s_par, 32)

        @block.gpsimd
        def _(pool):
            with pool.Fori(0, B) as b:
                with pool.Fori(0, 2) as half:
                    m = 2 * b + half

                    def pick(r):
                        t = GROUP * m + r
                        if r >= 2:
                            pool.wait_ge(s_tr, t - 1)
                            pool.sem_inc(s_tick)
                        src = g.O[:].rearrange("p (b h) t e -> p b h t e", b=B)
                        nc.gpsimd.tensor_copy(
                            oc[:, r % 2, :].rearrange("p (h e) -> p h e", h=PAIRS),
                            src[:, bass.ds(b, 1), :, bass.ds(8 * half + r, 1), :].rearrange("p o h u e -> p (o h u) e")
                        ).then_inc(s_oc, 1)

                    def gate(r):
                        t = GROUP * m + r
                        pool.wait_ge(s_y, t + 1)
                        if r >= 2:
                            pool.wait_ge(s_x, t - 1)
                        pool.sem_inc(s_tick)
                        nc.gpsimd.tensor_mul(yg[:, r % 2, :], y[:, r % 2, :],
                                             g.mod[:, bass.ds(b, 1), 2, :].rearrange("p o d -> p (o d)")
                                             ).then_inc(s_yg, 1)

                    for k in range(GROUP + 1):
                        if k < GROUP:
                            pick(k)
                        if k:
                            gate(k - 1)

        @block.scalar
        def _(act):
            with act.Fori(0, T // GROUP) as m:
                for r in range(GROUP):
                    t = GROUP * m + r
                    act.wait_ge(s_tr, t + 1)
                    if r >= 2:
                        act.wait_ge(s_prod, t - 1)
                    nc.scalar.copy(oT[:, r % 2, :, :], pst[r % 2][:]).then_inc(s_oT, 1)

        @block.vector
        def _(dve):
            dve.wait_ge(s_par, 32)
            with dve.Fori(0, T // GROUP) as m:
                def add_bias(r):
                    t = GROUP * m + r
                    dve.wait_ge(s_prod, t + 1)
                    if r >= 2:
                        dve.wait_ge(s_yg, t - 1)
                    nc.vector.tensor_add(y[:, r % 2, :], psy[r % 2][:, 0:D], pb[:]).then_inc(s_y, 1)

                def residual(r):
                    t = GROUP * m + r
                    x = g.X[:, bass.ds(t, 1), :].rearrange("p o d -> p (o d)")
                    dve.wait_ge(s_yg, t + 1)
                    nc.vector.tensor_add(x, x, yg[:, r % 2, :]).then_inc(s_x, 1)

                def statistics(r):
                    t = GROUP * m + r
                    dve.wait_ge(s_x, t + 1)
                    dve.sem_inc(s_tick)
                    nc.vector.bn_stats(st[:, bass.ds(t, 1), :].rearrange("p o d -> p (o d)"),
                                       g.X[:, bass.ds(t, 1), :].rearrange("p o d -> p (o d)")).then_inc(s_st, 1)

                for k in range(GROUP + 2):
                    if k < GROUP:
                        add_bias(k)
                    if 1 <= k <= GROUP:
                        residual(k - 1)
                    if k >= 2:
                        statistics(k - 2)
            dve.wait_ge(s_st, T)
            for t in range(T):
                last = nc.vector.bn_aggr(g.mv[:, t, :], st[:, t, :])
            last.then_inc(s_st, 1)
            dve.wait_ge(s_st, T + 1)
            nc.vector.tensor_scalar_add(g.sd[:, 1, :], g.mv[:, :, 1], EPS).then_inc(s_st, 1)

        @block.tensor
        def _(pe):
            pe.wait_ge(s_par, 32)
            with pe.Fori(0, T // GROUP) as m:
                def turn(r):
                    t = GROUP * m + r
                    pe.wait_ge(s_oc, t + 1)
                    if r >= 2:
                        pe.wait_ge(s_oT, t - 1)
                    for k in range(KD):
                        last = nc.tensor.transpose(pst[r % 2][:, k, :], oc[:, r % 2, k * P:(k + 1) * P], g.ident[:])
                    last.then_inc(s_tr, 1)

                def project(r):
                    t = GROUP * m + r
                    pe.wait_ge(s_oT, t + 1)
                    if r >= 2:
                        pe.wait_ge(s_y, t - 1)
                    for k in range(KD):
                        last = nc.tensor.matmul(psy[r % 2][:, 0:D], oT[:, r % 2, k, :], wp[:, k, :],
                                                start=k == 0, stop=k == KD - 1)
                    last.then_inc(s_prod, 1)

                for k in range(GROUP + 1):
                    if k < GROUP:
                        turn(k)
                    if k:
                        project(k - 1)
                pe.wait_ge(s_y, GROUP * m + GROUP)


def gate_stage(nc, g):
    with ExitStack() as ctx:
        sem = open_sem(ctx, nc, "gate")
        sb, ps = open_mem(ctx, nc, "gate")
        gw = sb("gw", [P, KD, E])
        bias = sb("bias", [P, 2, E])
        hn = sb("hn", [P, 2, D])
        hm = sb("hm", [P, 2, D])
        hT = sb("hT", [P, 2, KD, P])
        lg = sb("lg", [P, 2, E])
        pst = [ps(f"pst{i}", [P, KD, P]) for i in range(2)]
        psg = [ps(f"psg{i}", [P, CH]) for i in range(2)]
        (s_par, s_sd, s_v, s_hn, s_hm, s_tr, s_hT, s_h2, s_prod, s_lg, s_out, s_tick) = [
            sem(n) for n in "s_par s_sd s_v s_hn s_hm s_tr s_hT s_h2 s_prod s_lg s_out s_tick".split()]
        block = ctx.enter_context(nc.Block())

        @block.sync
        def _(sp):
            sp.dma_start(gw[:], g.gwT.rearrange("(k p) n -> p k n", p=P)).then_inc(s_par, 16)
            sp.dma_start(bias[:, 0, :], g.gate_b.partition_broadcast(P)).then_inc(s_par, 16)
            sp.dma_start(bias[:, 1, :], g.expert_bias.partition_broadcast(P)).then_inc(s_par, 16)
            sp.wait_ge(s_par, 48)

        @block.gpsimd
        def _(pool):
            with pool.Fori(0, B) as b:
                with pool.Fori(0, 2) as half:
                    for r in range(GROUP):
                        t = GROUP * (2 * b + half) + r
                        pool.wait_ge(s_hn, t + 1)
                        if r >= 2:
                            pool.wait_ge(s_h2, t - 1)
                        pool.sem_inc(s_tick)
                        nc.gpsimd.tensor_mul(hm[:, r % 2, :], hn[:, r % 2, :],
                                             g.mod[:, bass.ds(b, 1), 4, :].rearrange("p o d -> p (o d)")
                                             ).then_inc(s_hm, 1)
                        pool.wait_ge(s_hm, 2 * t + 1)
                        pool.sem_inc(s_tick)
                        nc.gpsimd.tensor_add(hm[:, r % 2, :], hm[:, r % 2, :],
                                             g.mod[:, bass.ds(b, 1), 3, :].rearrange("p o d -> p (o d)")
                                             ).then_inc(s_hm, 1)

        @block.scalar
        def _(act):
            nc.scalar.activation(g.sd[:, 0, :], g.sd[:, 1, :], ACT.Sqrt).then_inc(s_sd, 1)
            with act.Fori(0, T // GROUP) as m:
                for r in range(GROUP):
                    t = GROUP * m + r
                    act.wait_ge(s_tr, t + 1)
                    act.sem_inc(s_tick)
                    nc.scalar.copy(g.H2[:, bass.ds(t, 1), :].rearrange("p o d -> p (o d)"), hm[:, r % 2, :]
                                   ).then_inc(s_h2, 1)
                    if r >= 2:
                        act.wait_ge(s_prod, t - 1)
                    nc.scalar.copy(hT[:, r % 2, :, :], pst[r % 2][:]).then_inc(s_hT, 1)

        @block.vector
        def _(dve):
            inverse_deviation(nc, dve, g, s_sd, s_v, 0)
            dve.wait_ge(s_par, 48)
            with dve.Fori(0, T // GROUP) as m:
                for k in range(GROUP + 1):
                    if k < GROUP:
                        t = GROUP * m + k
                        if k >= 2:
                            dve.wait_ge(s_hm, 2 * t - 2)
                        nc.vector.tensor_scalar(hn[:, k % 2, :], g.X[:, bass.ds(t, 1), :].rearrange("p o d -> p (o d)"),
                                                g.mv[:, bass.ds(t, 1), 0], g.rs[:, bass.ds(t, 1)],
                                                ALU.subtract, ALU.mult).then_inc(s_hn, 1)
                    if k:
                        r = k - 1
                        t = GROUP * m + r
                        dve.wait_ge(s_prod, t + 1)
                        nc.vector.tensor_add(lg[:, r % 2, :], psg[r % 2][:, 0:E], bias[:, 0, :]).then_inc(s_lg, 1)
                        dve.wait_ge(s_lg, t + 1)
                        nc.vector.tensor_add(g.logits[:, bass.ds(t, 1), :].rearrange("p o e -> p (o e)"),
                                             lg[:, r % 2, :], bias[:, 1, :]).then_inc(s_out, 1)

        @block.tensor
        def _(pe):
            pe.wait_ge(s_par, 48)
            with pe.Fori(0, T // GROUP) as m:
                for k in range(GROUP + 1):
                    if k < GROUP:
                        t = GROUP * m + k
                        pe.wait_ge(s_hm, 2 * t + 2)
                        if k >= 2:
                            pe.wait_ge(s_hT, t - 1)
                        for c in range(KD):
                            last = nc.tensor.transpose(pst[k % 2][:, c, :], hm[:, k % 2, c * P:(c + 1) * P], g.ident[:])
                        last.then_inc(s_tr, 1)
                    if k:
                        r = k - 1
                        t = GROUP * m + r
                        pe.wait_ge(s_hT, t + 1)
                        if r >= 2:
                            pe.wait_ge(s_lg, t - 1)
                        for c in range(KD):
                            last = nc.tensor.matmul(psg[r % 2][:, 0:E], hT[:, r % 2, c, :], gw[:, c, :],
                                                    start=c == 0, stop=c == KD - 1)
                        last.then_inc(s_prod, 1)
                pe.wait_ge(s_lg, GROUP * m + GROUP)


def routing(nc, g):
    KS = B * N // FT
    with ExitStack() as ctx:
        sem = open_sem(ctx, nc, "route")
        sb, ps = open_mem(ctx, nc, "route")
        row = sb("row", [P, g.row.shape[-1]])
        rev, first, number = row[:, 0:E], row[:, E:E + KS], row[:, E + KS:E + KS + NT]
        below = sb("below", [P, P])
        ones = sb("ones", [P, P])
        best = sb("best", [P, T])
        eq = sb("eq", [P, T, E])
        hot = sb("hot", [P, T, E])
        cnt = sb("cnt", [P, T, E])
        upto = sb("upto", [P, E, T])
        more = sb("more", [P, E, KS])
        tiles = sb("tiles", [P, E])
        end = sb("end", [P, E])
        start = sb("start", [P, E])
        place = sb("place", [P, T, E])
        slotf = sb("slotf", [P, T])
        past = sb("past", [P, NT, E])
        which = sb("which", [P, NT])
        psr = ps("psr", [P, CH])
        psc = ps("psc", [P, CH])
        s_par, s_set, s_v, s_hot, s_cnt, s_slot, s_put = [
            sem(n) for n in "s_par s_set s_v s_hot s_cnt s_slot s_put".split()]
        block = ctx.enter_context(nc.Block())

        @block.sync
        def _(sp):
            sp.dma_start(row[:], g.row.partition_broadcast(P)).then_inc(s_par, 16)
            sp.wait_ge(s_par, 16)

        @block.tensor
        def _(pe):
            pe.wait_ge(s_hot, 1)
            pe.wait_ge(s_set, 3)
            flat = hot[:].rearrange("p t e -> p (t e)")
            nc.tensor.matmul(psr[:, 0:T * E], below[:], flat, start=True, stop=True).then_inc(s_cnt, 1)
            nc.tensor.matmul(psc[:, 0:T * E], ones[:], flat, start=True, stop=True).then_inc(s_cnt, 1)

        @block.gpsimd
        def _(pool):
            nc.gpsimd.memset(ones[:], 1.0).then_inc(s_set, 1)
            nc.gpsimd.memset(below[:], 1.0).then_inc(s_set, 1)
            pool.wait_ge(s_set, 2)
            nc.gpsimd.affine_select(out=below[:], in_=below[:], compare_op=ALU.is_ge, fill=0.0, base=-1,
                                    pattern=[[1, P]], channel_multiplier=-1).then_inc(s_set, 1)
            pool.wait_ge(s_slot, 1)
            for t in range(T):
                nc.gpsimd.indirect_dma_start(g.hs, bass.IndirectOffsetOnAxis(g.slot[:, t:t + 1], 0), g.H2[:, t, :], None
                                             ).then_inc(s_put, 16)
            pool.wait_ge(s_put, 16 * T)

        @block.vector
        def _(dve):
            done = [0]

            def then(ins):
                done[0] += 1
                ins.then_inc(s_v, 1)
                dve.wait_ge(s_v, done[0])

            over_t = lambda a: a.unsqueeze(1).to_broadcast([P, T, E])
            over_e = lambda a: a.unsqueeze(2).to_broadcast([P, T, E])
            dve.wait_ge(s_par, 16)
            then(nc.vector.reduce_max(best[:], g.logits[:], AX))
            then(nc.vector.tensor_tensor(eq[:], g.logits[:], over_e(best[:]), ALU.is_equal))
            then(nc.vector.tensor_tensor(eq[:], eq[:], over_t(rev), ALU.mult))
            then(nc.vector.reduce_max(best[:], eq[:], AX))
            nc.vector.tensor_tensor(hot[:], over_t(rev), over_e(best[:]), ALU.is_equal).then_inc(s_hot, 1)
            dve.wait_ge(s_cnt, 2)
            then(nc.vector.tensor_copy(cnt[:], psc[:, 0:T * E].rearrange("p (t e) -> p t e", e=E)))
            dve.wait_ge(s_set, 1)
            for e in range(E):
                last = nc.vector.tensor_tensor_scan(upto[:, e, :], ones[:, 0:T], cnt[:, :, e], 0.0, ALU.mult, ALU.add)
            then(last)
            then(nc.vector.tensor_tensor(more[:], upto[:, :, T - 1:T].to_broadcast([P, E, KS]),
                                         first.unsqueeze(1).to_broadcast([P, E, KS]), ALU.is_gt))
            then(nc.vector.reduce_sum(tiles[:], more[:], AX))
            then(nc.vector.tensor_tensor_scan(end[:], ones[:, 0:E], tiles[:], 0.0, ALU.mult, ALU.add))
            then(nc.vector.tensor_sub(start[:], end[:], tiles[:]))
            then(nc.vector.tensor_scalar_mul(start[:], start[:], float(FT)))
            then(nc.vector.tensor_sub(place[:], upto[:].rearrange("p e t -> p t e"), cnt[:]))
            then(nc.vector.tensor_add(place[:], place[:], psr[:, 0:T * E].rearrange("p (t e) -> p t e", e=E)))
            then(nc.vector.tensor_add(place[:], place[:], over_t(start[:])))
            then(nc.vector.tensor_mul(place[:], place[:], hot[:]))
            then(nc.vector.reduce_sum(slotf[:], place[:], AX))
            nc.vector.tensor_copy(g.slot[:], slotf[:]).then_inc(s_slot, 1)
            then(nc.vector.tensor_tensor(past[:], end[:].unsqueeze(1).to_broadcast([P, NT, E]),
                                         number.unsqueeze(2).to_broadcast([P, NT, E]), ALU.is_le))
            then(nc.vector.reduce_sum(which[:], past[:], AX))
            then(nc.vector.tensor_scalar_min(which[:], which[:], float(E - 1)))
            nc.vector.tensor_copy(g.which[:], which[:]).then_inc(s_v, 1)


def experts(nc, g):
    SUB = FT // P
    with ExitStack() as ctx:
        sem = open_sem(ctx, nc, "ffn")
        sb, ps = open_mem(ctx, nc, "ffn")
        w1 = [sb(f"w1_{i}", [P, KD, F]) for i in range(2)]
        w2 = [sb(f"w2_{i}", [P, KF, D]) for i in range(2)]
        b1 = [sb(f"b1_{i}", [P, KF]) for i in range(2)]
        b2 = [sb(f"b2_{i}", [P, D]) for i in range(2)]
        rows = [sb(f"rows{i}", [P, SUB, D]) for i in range(2)]
        hT = [sb(f"hT{i}", [P, KD, FT]) for i in range(2)]
        hid = sb("hid", [P, KF, FT])
        y = [sb(f"y{i}", [P, SUB, D]) for i in range(2)]
        pst = [ps(f"pst{i}", [P, KD, FT]) for i in range(2)]
        psh = [ps(f"psh{i}", [P, 2, FT]) for i in range(4)]
        psy = [ps(f"psy{i}", [P, SUB, D]) for i in range(2)]
        in1 = [sem(f"in1_{i}") for i in range(2)]
        in2 = [sem(f"in2_{i}") for i in range(2)]
        in3 = [sem(f"in3_{i}") for i in range(2)]
        turned, hT_ready, layer1, hid_ready, layer2, y_ready, tick, tick_act = [
            sem(n) for n in "turned hT_ready layer1 hid_ready layer2 y_ready tick tick_act".split()]
        stored = [sem(f"stored{i}") for i in range(2)]
        block = ctx.enter_context(nc.Block())

        def over_tiles(eng, tile):
            with eng.Fori(0, NT // 2) as i:
                for par in range(2):
                    tile(2 * i + par, par, i, False)
            if NT % 2:
                tile(NT - 1, 0, NT // 2, True)

        @block.sync
        def _(sp):
            def hold(semaphore, value):
                sp.wait_ge(semaphore, value)
                sp.sem_inc(tick)

            def load(k, par, i, last):
                e = sp.value_load(g.which[0:1, k:k + 1] if isinstance(k, int) else g.which[0:1, bass.ds(k, 1)],
                                  min_val=0, max_val=E - 1)
                hold(turned, k + 1)
                sp.dma_start(rows[par][:], g.hs.rearrange("(k s p) d -> k p s d", s=SUB, p=P)[bass.ds(k, 1)]
                             .rearrange("o p s d -> p (o s) d")).then_inc(in3[par], 16)
                hold(hid_ready, KF * k + KF)
                sp.dma_start(w1[par][:], g.w1[bass.ds(e, 1)].rearrange("o (k p) f -> p (o k) f", p=P)
                             ).then_inc(in1[par], 16)
                sp.dma_start(b1[par][:], g.b1T[bass.ds(e, 1)].rearrange("o p k -> p (o k)")).then_inc(in1[par], 16)
                hold(y_ready, k + 1)
                sp.dma_start(w2[par][:], g.w2[bass.ds(e, 1)].rearrange("o (k p) d -> p (o k) d", p=P)
                             ).then_inc(in2[par], 16)
                sp.dma_start(b2[par][:], g.b2[bass.ds(e, 1)].rearrange("o d -> (o d)").partition_broadcast(P)
                             ).then_inc(in2[par], 16)

            over_tiles(sp, load)

        @block.scalar
        def _(act):
            act.sem_inc(hid_ready, AHEAD * KF)

            def copy_turned(k, par, i):
                act.wait_ge(turned, k + 1 + AHEAD)
                nc.scalar.copy(hT[par][:], pst[par][:]).then_inc(hT_ready, 1)

            def store(k, par):
                act.wait_ge(y_ready, k + 1 + AHEAD)
                act.sem_inc(tick_act)
                act.dma_start(g.ys.rearrange("(k s p) d -> k p s d", s=SUB, p=P)[bass.ds(k, 1)]
                              .rearrange("o p s d -> p (o s) d"), y[par][:]).then_inc(stored[par], 16)

            for par in range(2):
                act.sem_inc(stored[par], 16)
            copy_turned(0, 0, 0)

            def tile(k, par, i, last):
                act.wait_ge(in1[par], 32 * (i + 1))
                act.wait_ge(layer2, k + 1)
                for f in range(KF):
                    act.wait_ge(layer1, KF * k + f // 2 * 2 + 2)
                    nc.scalar.activation(hid[:, f, :], psh[f // 2][:, f % 2, :], ACT.Relu, bias=b1[par][:, f:f + 1]
                                         ).then_inc(hid_ready, 1)
                if not last:
                    copy_turned(k + 1, 1 - par, i)
                store(k, par)

            over_tiles(act, tile)
            for par in range(2):
                act.wait_ge(stored[par], 16 * ((NT + 1 - par) // 2) + 16)

        @block.vector
        def _(dve):
            dve.sem_inc(y_ready, AHEAD)

            def tile(k, par, i, last):
                dve.wait_ge(in2[par], 32 * (i + 1))
                dve.wait_ge(stored[par], 16 * (i + 1))
                dve.wait_ge(layer2, k + 2)
                nc.vector.tensor_add(y[par][:], psy[par][:], b2[par][:].unsqueeze(1).to_broadcast([P, SUB, D])
                                     ).then_inc(y_ready, 1)

            over_tiles(dve, tile)

        @block.tensor
        def _(pe):
            pe.sem_inc(turned, AHEAD)
            pe.sem_inc(layer2, 1)

            def turn(k, par, i):
                pe.wait_ge(in3[par], 16 * (i + 1))
                for s in range(SUB):
                    for c in range(KD):
                        last = nc.tensor.transpose(pst[par][:, c, s * P:(s + 1) * P],
                                                   rows[par][:, s, c * P:(c + 1) * P], g.ident[:])
                last.then_inc(turned, 1)

            turn(0, 0, 0)

            def tile(k, par, i, last):
                pe.wait_ge(hT_ready, k + 1)
                pe.wait_ge(in1[par], 32 * (i + 1))
                for f in range(KF):
                    pe.wait_ge(hid_ready, KF * k + f + 1 + KF if f % 2 else KF * k + f + 2 + KF)
                    for c in range(KD):
                        last_mm = nc.tensor.matmul(psh[f // 2][:, f % 2, :], w1[par][:, c, f * P:(f + 1) * P],
                                                   hT[par][:, c, :], start=c == 0, stop=c == KD - 1)
                    last_mm.then_inc(layer1, 1)
                if not last:
                    turn(k + 1, 1 - par, i + par)
                pe.wait_ge(in2[par], 32 * (i + 1))
                pe.wait_ge(y_ready, k + 1)
                for s in range(SUB):
                    for f in range(KF):
                        if s == 0:
                            pe.wait_ge(hid_ready, KF * k + f + 1 + AHEAD * KF)
                        last_mm = nc.tensor.matmul(psy[par][:, s, :], hid[:, f, s * P:(s + 1) * P], w2[par][:, f, :],
                                                   start=f == 0, stop=f == KF - 1)
                last_mm.then_inc(layer2, 1)

            over_tiles(pe, tile)


def combine(nc, g):
    FLIGHT = 8
    with ExitStack() as ctx:
        sem = open_sem(ctx, nc, "comb")
        sb, ps = open_mem(ctx, nc, "comb")
        got = sb("got", [P, T, D])
        fetched = [sem(f"fetched{i}") for i in range(FLIGHT)]
        s_g, s_o, s_out = sem("s_g"), sem("s_o"), sem("s_out")
        block = ctx.enter_context(nc.Block())
        LOT = 4

        @block.gpsimd
        def _(pool):
            for t in range(T):
                if t >= FLIGHT:
                    pool.wait_ge(fetched[t % FLIGHT], 16 * (t // FLIGHT))
                nc.gpsimd.indirect_dma_start(got[:, t, :], None, g.ys, bass.IndirectOffsetOnAxis(g.slot[:, t:t + 1], 0)
                                             ).then_inc(fetched[t % FLIGHT], 16)

        @block.vector
        def _(dve):
            for t in range(T):
                b = t // TB
                dve.wait_ge(fetched[t % FLIGHT], 16 * (t // FLIGHT + 1))
                nc.vector.tensor_mul(got[:, t, :], got[:, t, :], g.mod[:, b, 5, :]).then_inc(s_g, 1)
                if t:
                    dve.wait_ge(s_g, t)
                    nc.vector.tensor_add(g.X[:, t - 1, :], g.X[:, t - 1, :], got[:, t - 1, :]).then_inc(s_o, 1)
            dve.wait_ge(s_g, T)
            nc.vector.tensor_add(g.X[:, T - 1, :], g.X[:, T - 1, :], got[:, T - 1, :]).then_inc(s_o, 1)

        @block.sync
        def _(sp):
            dst = g.out.rearrange("b (t p) d -> p (b t) d", p=P)
            for t in range(0, T, LOT):
                sp.wait_ge(s_o, t + LOT)
                sp.dma_start(dst[:, t:t + LOT, :], g.X[:, t:t + LOT, :]).then_inc(s_out, 16)
            sp.wait_ge(s_out, 16 * T // LOT)



def build(nc, ins, consts, out, debug=None):
    g = Ctx()
    (g.x, g.wqkvT, g.qkv_b, g.wpT, g.proj_b, g.gwT, g.gate_b, g.expert_bias, g.w1, g.b1T, g.w2, g.b2, g.cT,
     g.wmod) = ins
    g.rope, g.row = consts
    g.out = out
    g.qkT = [nc.dram_tensor(f"qkT_{part}", (2, B * D, N), F32, kind="Internal").ap() for part in ("hi", "lo")]
    g.hs = nc.dram_tensor("routed_rows", (NT * FT, D), F32, kind="Internal").ap()
    g.ys = nc.dram_tensor("expert_rows", (NT * FT, D), F32, kind="Internal").ap()
    with ExitStack() as ctx:
        sb, _ = open_mem(ctx, nc, "all")
        g.ident = sb("ident", [P, P])
        g.X = sb("X", [P, T, D])
        g.mv = sb("mv", [P, T, 2])
        g.sd = sb("sd", [P, 3, T])
        g.rs = sb("rs", [P, T])
        g.mod = sb("mod", [P, B, 6, D])
        with ExitStack() as inner:
            g.V = inner.enter_context(nc.sbuf_tensor("V", [P, UNITS, TB, 2 * HD], F32))
            setup(nc, g)
            qkv_stage(nc, g)
            g.O = inner.enter_context(nc.sbuf_tensor("O", [P, UNITS, TB, 2 * HD], F32))
            attention(nc, g)
            if debug == 3:
                dump(nc, g, None)
            projection(nc, g)
            if debug == 1:
                dump(nc, g, g.qkT[0][0])
            if debug == 2:
                dump(nc, g, g.qkT[1][1])
        with ExitStack() as inner:
            isb, _ = open_mem(inner, nc, "ffn_all")
            g.logits = isb("logits", [P, T, E])
            g.slot = isb("slot", [P, T], I32)
            g.which = isb("which_i", [P, NT], I32)
            with ExitStack() as rows:
                g.H2 = rows.enter_context(nc.sbuf_tensor("H2", [P, T, D], F32))
                gate_stage(nc, g)
                routing(nc, g)
            experts(nc, g)
            combine(nc, g)


def dump(nc, g, src):
    with ExitStack() as ctx:
        s_d = ctx.enter_context(nc.semaphore("s_dump"))
        block = ctx.enter_context(nc.Block())

        @block.sync
        def _(sp):
            if src is None:
                for b in range(B):
                    for u in range(PAIRS):
                        sp.dma_start(g.out[b].rearrange("(t p) (h e) -> p h t e", p=P, h=PAIRS)[:, u],
                                     g.O[:, b * PAIRS + u]).then_inc(s_d, 16)
                sp.wait_ge(s_d, 16 * B * PAIRS)
                return
            sp.dma_start(g.out.rearrange("b n d -> (b n d)").rearrange("(a c) -> a c", c=2048), src).then_inc(s_d, 16)
            sp.wait_ge(s_d, 16)


def rope_tables():
    inv = (1.0 / np.float32(10000.0) ** (np.arange(0, HD, 2, dtype=np.float32) / np.float32(HD))).astype(np.float32)
    freqs = np.arange(N, dtype=np.float32)[:, None] * inv[None, :]
    cos, sin = np.cos(freqs).astype(np.float32), np.sin(freqs).astype(np.float32)
    return np.ascontiguousarray(np.stack([np.repeat(cos, 2, axis=1), np.stack([-sin, sin], axis=-1).reshape(N, HD)]))


def routing_row():
    return np.concatenate([E - np.arange(E), FT * np.arange(B * N // FT), np.arange(NT)]).astype(np.float32)


DEBUG = None


def kernel(L0_attn_x, L0_attn_qkv_w, L0_attn_qkv_b, L0_attn_proj_w, L0_attn_proj_b, L0_ffn_gate_w, L0_ffn_gate_b,
           L0_ffn_expert_bias, L0_ffn_w1, L0_ffn_b1, L0_ffn_w2, L0_ffn_b2, L0_c, L0_wmod):
    import concourse.bacc as bacc
    from concourse.bass_utils import run_bass_kernel_spmd

    laid = {
        "x": L0_attn_x, "wqkvT": np.asarray(L0_attn_qkv_w).T, "qkv_b": L0_attn_qkv_b,
        "wpT": np.asarray(L0_attn_proj_w).T, "proj_b": L0_attn_proj_b, "gwT": np.asarray(L0_ffn_gate_w).T,
        "gate_b": L0_ffn_gate_b, "expert_bias": L0_ffn_expert_bias, "w1": L0_ffn_w1,
        "b1T": np.asarray(L0_ffn_b1).reshape(E, KF, P).transpose(0, 2, 1), "w2": L0_ffn_w2, "b2": L0_ffn_b2,
        "cT": np.asarray(L0_c).T, "wmod": L0_wmod,
    }
    nc = bacc.Bacc("TRN2", target_bir_lowering=False, num_devices=1)
    arrays, ins = {}, []
    for name, a in laid.items():
        a = np.ascontiguousarray(a)
        arrays["in_" + name] = a
        ins.append(nc.dram_tensor("in_" + name, a.shape, mybir.dt.from_np(a.dtype), kind="ExternalInput").ap())
    consts = []
    for name, a in (("rope", rope_tables()), ("row", routing_row())):
        arrays["const_" + name] = a
        consts.append(nc.dram_tensor("const_" + name, a.shape, mybir.dt.from_np(a.dtype), kind="ExternalInput").ap())
    out = nc.dram_tensor("out", (B, N, D), F32, kind="ExternalOutput").ap()
    build(nc, ins, consts, out, DEBUG)
    return run_bass_kernel_spmd(nc, [arrays], core_ids=[0]).results[0]["out"]
```

```python
from contextlib import ExitStack

import numpy as np
import concourse.bass as bass
from concourse import mybir

ALU = mybir.AluOpType
ACT = mybir.ActivationFunctionType
AX = mybir.AxisListType.X
F32 = mybir.dt.float32
F32R = mybir.dt.float32r
I32 = mybir.dt.int32
U32 = mybir.dt.uint32

P = 128
B, N, D = 2, 2048, 256
H, HD = 16, 16
F, E = 1024, 8
T = B * N // P
TB = N // P
KD = D // P
KF = F // P
QKV = 3 * D
EPS = 1e-5
SCALE = HD ** -0.5
PAIRS = H // 2
UNITS = B * PAIRS
CH = 512
CHUNKS = N // CH
STEPS = UNITS * CHUNKS
ROWS = 50
GROUP = 8
FT = 256
NT = (B * N) // FT + E - 1
AHEAD = 2


class Ctx:
    pass


def open_sem(ctx, nc, stage):
    return lambda name: ctx.enter_context(nc.semaphore(f"{stage}_{name}"))


def open_mem(ctx, nc, stage):
    sb = lambda name, shape, dt=F32: ctx.enter_context(nc.sbuf_tensor(f"{stage}_{name}", shape, dt))
    ps = lambda name, shape, dt=F32: ctx.enter_context(nc.psum_tensor(f"{stage}_{name}", shape, dt))
    return sb, ps


def setup(nc, g):
    with ExitStack() as ctx:
        sem = open_sem(ctx, nc, "set")
        sb, ps = open_mem(ctx, nc, "set")
        cT = sb("cT", [P, KD, B])
        cs = sb("cs", [P, 3, KD * B])
        cb = sb("cb", [P, KD, B, P])
        wmod = sb("wmod", [P, KD, 6 * D])
        st = sb("st", [P, T, 6])
        mag = sb("mag", [P, B, D])
        psm = [ps(f"psm{b}", [P, 6 * D]) for b in range(B)]
        s_x, s_c, s_w, s_id = sem("s_x"), sem("s_c"), sem("s_w"), sem("s_id")
        s_exp, s_v, s_cb, s_mod, s_ev = sem("s_exp"), sem("s_v"), sem("s_cb"), sem("s_mod"), sem("s_ev")
        s_mv, s_sd = sem("s_mv"), sem("s_sd")
        block = ctx.enter_context(nc.Block())

        @block.sync
        def _(sp):
            sp.dma_start(cT[:], g.cT.rearrange("(k p) b -> p k b", p=P)).then_inc(s_c, 16)
            sp.dma_start(wmod[:], g.wmod.rearrange("(k p) n -> p k n", p=P)).then_inc(s_w, 16)
            xd = g.x.rearrange("b (t p) d -> p (b t) d", p=P)
            for i in range(4):
                sp.dma_start(g.X[:, i * 8:(i + 1) * 8, :], xd[:, i * 8:(i + 1) * 8, :]).then_inc(s_x, 16)
            sp.wait_ge(s_c, 16)
            sp.wait_ge(s_w, 16)
            sp.wait_ge(s_x, 64)

        @block.gpsimd
        def _(pool):
            nc.gpsimd.memset(g.ident[:], 0.0).then_inc(s_id, 1)
            pool.wait_ge(s_id, 1)
            nc.gpsimd.affine_select(out=g.ident[:], in_=g.ident[:], compare_op=ALU.not_equal, fill=1.0, base=0,
                                    pattern=[[-1, P]], channel_multiplier=1).then_inc(s_id, 1)
            pool.wait_ge(s_id, 2)

        @block.scalar
        def _(act):
            act.wait_ge(s_c, 16)
            nc.scalar.activation(cs[:, 0, :], cT[:].rearrange("p k b -> p (k b)"), ACT.Exp, scale=-1.0).then_inc(s_exp, 1)
            act.wait_ge(s_mv, 2)
            nc.scalar.activation(g.sd[:, 0, :], g.sd[:, 1, :], ACT.Sqrt).then_inc(s_sd, 1)

        @block.vector
        def _(dve):
            dve.wait_ge(s_exp, 1)
            nc.vector.tensor_scalar_add(cs[:, 1, :], cs[:, 0, :], 1.0).then_inc(s_v, 1)
            dve.wait_ge(s_v, 1)
            nc.vector.reciprocal(cs[:, 2, :], cs[:, 1, :]).then_inc(s_v, 1)
            dve.wait_ge(s_v, 2)
            nc.vector.tensor_mul(cs[:, 0, :], cs[:, 2, :], cT[:].rearrange("p k b -> p (k b)")).then_inc(s_v, 1)
            dve.wait_ge(s_v, 3)
            for k in range(KD):
                for b in range(B):
                    last = nc.vector.tensor_copy(cb[:, k, b, :], cs[:, 0, k * B + b:k * B + b + 1].to_broadcast([P, P]))
            last.then_inc(s_cb, 1)
            dve.wait_ge(s_x, 64)
            for t in range(T):
                last = nc.vector.bn_stats(st[:, t, :], g.X[:, t, :])
            last.then_inc(s_mv, 1)
            dve.wait_ge(s_mv, 1)
            for t in range(T):
                last = nc.vector.bn_aggr(g.mv[:, t, :], st[:, t, :])
            last.then_inc(s_v, 1)
            dve.wait_ge(s_v, 4)
            nc.vector.tensor_scalar_add(g.sd[:, 1, :], g.mv[:, :, 1], EPS).then_inc(s_mv, 1)
            dve.wait_ge(s_mod, 1)
            for b in range(B):
                for j, part in enumerate(("shift", "scale", "gate") * 2):
                    src, dst = psm[b][:, j * D:(j + 1) * D], g.mod[:, b, j, :]
                    if part == "scale":
                        nc.vector.tensor_scalar_add(dst, src, 1.0).then_inc(s_ev, 1)
                    else:
                        nc.vector.tensor_copy(dst, src).then_inc(s_ev, 1)
            dve.wait_ge(s_ev, 6 * B)
            n = 4
            for j in (2, 5):
                gate = g.mod[:, :, j, :]
                nc.vector.scalar_tensor_tensor(mag[:], gate, -1.0, gate, ALU.mult, ALU.max).then_inc(s_v, 1)
                dve.wait_ge(s_v, n + 1)
                nc.vector.tensor_scalar_max(mag[:], mag[:], 0.25).then_inc(s_v, 1)
                nc.vector.tensor_scalar(gate, gate, 0.0, 2.0, ALU.is_ge, ALU.mult).then_inc(s_v, 1)
                dve.wait_ge(s_v, n + 3)
                nc.vector.scalar_tensor_tensor(gate, gate, -1.0, mag[:], ALU.add, ALU.mult).then_inc(s_v, 1)
                dve.wait_ge(s_v, n + 4)
                n += 4
            inverse_deviation(nc, dve, g, s_sd, s_v, n)

        @block.tensor
        def _(pe):
            pe.wait_ge(s_cb, 1)
            pe.wait_ge(s_w, 16)
            for b in range(B):
                for j in range(3):
                    for k in range(KD):
                        last = nc.tensor.matmul(psm[b][:, j * 512:(j + 1) * 512], cb[:, k, b, :],
                                                wmod[:, k, j * 512:(j + 1) * 512], start=k == 0, stop=k == KD - 1)
            last.then_inc(s_mod, 1)


def inverse_deviation(nc, dve, g, s_sd, s_v, n):
    dve.wait_ge(s_sd, 1)
    nc.vector.reciprocal(g.sd[:, 2, :], g.sd[:, 0, :]).then_inc(s_v, 1)
    dve.wait_ge(s_v, n + 1)
    nc.vector.tensor_mul(g.sd[:, 2, :], g.sd[:, 2, :], g.sd[:, 1, :]).then_inc(s_v, 1)
    dve.wait_ge(s_v, n + 2)
    nc.vector.tensor_add(g.sd[:, 2, :], g.sd[:, 2, :], g.sd[:, 0, :]).then_inc(s_v, 1)
    dve.wait_ge(s_v, n + 3)
    nc.vector.tensor_scalar_mul(g.sd[:, 2, :], g.sd[:, 2, :], 0.5).then_inc(s_v, 1)
    dve.wait_ge(s_v, n + 4)
    nc.vector.reciprocal(g.rs[:], g.sd[:, 2, :]).then_inc(s_v, 1)
    dve.wait_ge(s_v, n + 5)


def qkv_stage(nc, g):
    with ExitStack() as ctx:
        sem = open_sem(ctx, nc, "qkv")
        sb, ps = open_mem(ctx, nc, "qkv")
        wq = sb("wq", [P, KD, QKV])
        qb = sb("qb", [P, QKV])
        tab = sb("tab", [P, 2, TB, HD])
        hn = sb("hn", [P, 2, D])
        hm = sb("hm", [P, 2, D])
        hT = sb("hT", [P, 2, KD, P])
        qk = sb("qk", [P, 2, 2 * D])
        rc = sb("rc", [P, 2, 2 * D])
        rw = sb("rw", [P, 2, 2 * D])
        rq = sb("rq", [P, 2, 2 * D])
        zero = sb("zero", [P, 2048])
        hi = [sb(f"hi{i}", [P, 4, CH], F32R) for i in range(2)]
        lo = [sb(f"lo{i}", [P, 4, CH], F32R) for i in range(2)]
        pst = [ps(f"pst{i}", [P, KD, P]) for i in range(2)]
        psq = [ps(f"psq{i}", [P, 1024]) for i in range(2)]
        psr = [ps(f"psr{i}", [P, 4, P]) for i in range(2)]
        names = "s_par s_zero s_fill s_hn s_hm s_tr s_hT s_q s_qb s_vb s_rc s_rw s_rq s_rt s_hi s_lo s_put0 s_put1 s_tick s_tick_sp"
        (s_par, s_zero, s_fill, s_hn, s_hm, s_tr, s_hT, s_q, s_qb, s_vb, s_rc, s_rw, s_rq, s_rt, s_hi, s_lo,
         s_put0, s_put1, s_tick, s_tick_sp) = [sem(n) for n in names.split()]
        s_put = [s_put0, s_put1]
        block = ctx.enter_context(nc.Block())


        @block.sync
        def _(sp):
            sp.dma_start(wq[:], g.wqkvT.rearrange("(k p) n -> p k n", p=P)).then_inc(s_par, 16)
            sp.dma_start(qb[:], g.qkv_b.partition_broadcast(P)).then_inc(s_par, 16)
            sp.dma_start(tab[:], g.rope.rearrange("a (t p) d -> p a t d", p=P)).then_inc(s_par, 16)
            sp.wait_ge(s_zero, 1)
            rows = 2048 // D
            left = g.hs.shape[0] // P - (g.hs.shape[0] // P // rows) * rows
            full = g.hs.shape[0] // P // rows
            hs = g.hs[0:full * rows * P, :].rearrange("(n p r) d -> n p (r d)", r=rows, p=P) if full else None
            for n in range(full):
                sp.dma_start(hs[n], zero[:]).then_inc(s_fill, 16)
            if left:
                sp.dma_start(g.hs[full * rows * P:, :].rearrange("(p r) d -> p (r d)", r=left, p=P),
                             zero[:, 0:left * D]).then_inc(s_fill, 16)
            for c in range(2):
                sp.sem_inc(s_put[c], 16)
            with sp.Fori(0, B) as b:
                for c in range(CHUNKS):
                    sp.wait_ge(s_lo, TB * b + 4 * c + 4 + AHEAD)
                    sp.sem_inc(s_tick_sp)
                    for part, buf in enumerate((hi, lo)):
                        dst = g.qkT[part].rearrange("q (b f p) n -> q b f p n", b=B, p=P)
                        for q in range(2):
                            sp.dma_start(
                                dst[q, bass.ds(b, 1), :, :, c * CH:(c + 1) * CH].rearrange("o f p n -> p (o f) n"),
                                buf[c % 2][:, 2 * q:2 * q + 2, :].bitcast(F32)).then_inc(s_put[c % 2], 16)
            for c in range(2):
                sp.wait_ge(s_put[c], 64 * B * CHUNKS // 2 + 16)
            sp.wait_ge(s_fill, 16 * (full + (1 if left else 0)))

        @block.gpsimd
        def _(pool):
            nc.gpsimd.memset(zero[:], 0.0).then_inc(s_zero, 1)
            pool.wait_ge(s_par, 48)
            with pool.Fori(0, B) as b:
                def modulate(r):
                    t = TB * b + r
                    pool.wait_ge(s_hn, t + 1)
                    if r >= 2:
                        pool.wait_ge(s_tr, t - 1)
                    pool.sem_inc(s_tick)
                    nc.gpsimd.tensor_mul(hm[:, r % 2, :], hn[:, r % 2, :], g.mod[:, bass.ds(b, 1), 1, :].rearrange("p o d -> p (o d)")).then_inc(s_hm, 1)
                    pool.wait_ge(s_hm, 2 * t + 1)
                    pool.sem_inc(s_tick)
                    nc.gpsimd.tensor_add(hm[:, r % 2, :], hm[:, r % 2, :], g.mod[:, bass.ds(b, 1), 0, :].rearrange("p o d -> p (o d)")).then_inc(s_hm, 1)

                def swapped(r):
                    t = TB * b + r
                    pool.wait_ge(s_qb, t + 1)
                    if r >= 2:
                        pool.wait_ge(s_rq, t - 1)
                    src = qk[:, r % 2, :].rearrange("p (h i e) -> p h i e", h=2 * H, e=2)
                    dst = rw[:, r % 2, :].rearrange("p (h i e) -> p h i e", h=2 * H, e=2)
                    sn = tab[:, 1, r:r + 1, :].rearrange("p o (i e) -> p o i e", e=2)
                    pool.sem_inc(s_tick)
                    for e in range(2):
                        last = nc.gpsimd.tensor_mul(dst[:, :, :, e], src[:, :, :, 1 - e],
                                                    sn[:, :, :, e].to_broadcast([P, 2 * H, HD // 2]))
                    last.then_inc(s_rw, 1)

                for k in range(TB + 2):
                    if k < TB:
                        modulate(k)
                    if k >= 2:
                        swapped(k - 2)

        @block.scalar
        def _(act):
            with act.Fori(0, B) as b:
                for k in range(TB + 3):
                    if k < TB:
                        t = TB * b + k
                        act.wait_ge(s_tr, t + 1)
                        if k >= 2:
                            act.wait_ge(s_q, t - 1)
                        nc.scalar.copy(hT[:, k % 2, :, :], pst[k % 2][:]).then_inc(s_hT, 1)
                    if k >= 3:
                        r = k - 3
                        c, o = r // 4 % 2, (r % 4) * P
                        act.wait_ge(s_rt, TB * b + r + 1)
                        if r % 4 == 0:
                            act.wait_ge(s_put[c], 64 * (2 * b + r // 8) + 16)
                        nc.scalar.mul(hi[c][:, 0:2, o:o + P], psr[r % 2][:, 0:2, :], SCALE)
                        nc.scalar.copy(hi[c][:, 2:4, o:o + P], psr[r % 2][:, 2:4, :]).then_inc(s_hi, 1)

        @block.vector
        def _(dve):
            dve.wait_ge(s_par, 48)
            dve.sem_inc(s_lo, AHEAD)
            with dve.Fori(0, B) as b:
                def normalise(r):
                    t = TB * b + r
                    if r >= 2:
                        dve.wait_ge(s_hm, 2 * t - 2)
                    nc.vector.tensor_scalar(hn[:, r % 2, :], g.X[:, bass.ds(t, 1), :].rearrange("p o d -> p (o d)"),
                                            g.mv[:, bass.ds(t, 1), 0], g.rs[:, bass.ds(t, 1)],
                                            ALU.subtract, ALU.mult).then_inc(s_hn, 1)

                def add_bias(r):
                    t = TB * b + r
                    dve.wait_ge(s_q, t + 1)
                    if r >= 2:
                        dve.wait_ge(s_rw, t - 1)
                    nc.vector.tensor_add(qk[:, r % 2, :], psq[r % 2][:, 0:2 * D], qb[:, 0:2 * D]).then_inc(s_qb, 1)
                    v = g.V[:].rearrange("p (b h) t e -> p b h t e", b=B)
                    nc.vector.tensor_add(
                        v[:, bass.ds(b, 1), :, r:r + 1, :].rearrange("p o h u e -> p (o h u) e"),
                        psq[r % 2][:, 2 * D:3 * D].rearrange("p (h e) -> p h e", h=PAIRS),
                        qb[:, 2 * D:3 * D].rearrange("p (h e) -> p h e", h=PAIRS)).then_inc(s_vb, 1)

                def times_cos(r):
                    t = TB * b + r
                    src = qk[:, r % 2, :].rearrange("p (h e) -> p h e", h=2 * H)
                    dve.wait_ge(s_qb, t + 1)
                    nc.vector.tensor_mul(rc[:, r % 2, :].rearrange("p (h e) -> p h e", h=2 * H), src,
                                         tab[:, 0, r:r + 1, :].to_broadcast([P, 2 * H, HD])).then_inc(s_rc, 1)

                def add_swapped(r):
                    t = TB * b + r
                    dve.wait_ge(s_rc, t + 1)
                    dve.wait_ge(s_rw, t + 1)
                    if r >= 2:
                        dve.wait_ge(s_rt, t - 1)
                    nc.vector.tensor_add(rq[:, r % 2, :], rc[:, r % 2, :], rw[:, r % 2, :]).then_inc(s_rq, 1)

                def low_part(r):
                    t = TB * b + r
                    c, o = r // 4 % 2, (r % 4) * P
                    dve.wait_ge(s_hi, t + 1)
                    if r % 4 == 0:
                        dve.wait_ge(s_put[c], 64 * (2 * b + r // 8) + 16)
                    for q, scale in ((0, SCALE), (1, 1.0)):
                        last = nc.vector.scalar_tensor_tensor(
                            lo[c][:, 2 * q:2 * q + 2, o:o + P], psr[r % 2][:, 2 * q:2 * q + 2, :], scale,
                            hi[c][:, 2 * q:2 * q + 2, o:o + P].bitcast(F32), ALU.mult, ALU.subtract)
                    last.then_inc(s_lo, 1)

                for k in range(TB + 4):
                    if k < TB:
                        normalise(k)
                    if 3 <= k <= TB + 2:
                        add_swapped(k - 3)
                    if 2 <= k <= TB + 1:
                        add_bias(k - 2)
                        times_cos(k - 2)
                    if k >= 4:
                        low_part(k - 4)

        @block.tensor
        def _(pe):
            pe.wait_ge(s_par, 48)
            with pe.Fori(0, B) as b:
                def tiles_in(r):
                    t = TB * b + r
                    pe.wait_ge(s_hm, 2 * t + 2)
                    if r >= 2:
                        pe.wait_ge(s_hT, t - 1)
                    for k in range(KD):
                        last = nc.tensor.transpose(pst[r % 2][:, k, :], hm[:, r % 2, k * P:(k + 1) * P], g.ident[:])
                    last.then_inc(s_tr, 1)

                def project(r):
                    t = TB * b + r
                    pe.wait_ge(s_hT, t + 1)
                    if r >= 2:
                        pe.wait_ge(s_vb, t - 1)
                    for n0, n1 in ((0, 512), (512, QKV)):
                        for k in range(KD):
                            last = nc.tensor.matmul(psq[r % 2][:, n0:n1], hT[:, r % 2, k, :], wq[:, k, n0:n1],
                                                    start=k == 0, stop=k == KD - 1)
                    last.then_inc(s_q, 1)

                def tiles_out(r):
                    t = TB * b + r
                    pe.wait_ge(s_rq, t + 1)
                    pe.wait_ge(s_lo, t - 1 + AHEAD if r >= 2 else t - r + AHEAD)
                    for k in range(4):
                        last = nc.tensor.transpose(psr[r % 2][:, k, :], rq[:, r % 2, k * P:(k + 1) * P], g.ident[:])
                    last.then_inc(s_rt, 1)

                for k in range(TB + 3):
                    if k < TB:
                        tiles_in(k)
                    if 1 <= k <= TB:
                        project(k - 1)
                    if k >= 3:
                        tiles_out(k - 3)


def attention(nc, g):
    KT = N // P
    GROUPS = KT // 2
    OVER = 2
    EARLY = 3
    SLOTS = 8
    BODY = GROUP
    ITERS = STEPS // BODY
    VW = 32
    WIDTH = HD + 1
    BANKS = 3
    EACH = 2 * KT
    USED = 64 + ROWS
    with ExitStack() as ctx:
        sem = open_sem(ctx, nc, "att")
        sb, ps = open_mem(ctx, nc, "att")
        K = [sb(f"K{i}", [P, N], F32R) for i in range(2)]
        QM = [sb(f"QM{i}", [P, 2, CH], F32R) for i in range(2)]
        QE = [sb(f"QE{i}", [P, 2, CH], F32R) for i in range(2)]
        VU = [sb(f"VU{i}", [P, KT, 2, VW]) for i in range(2)]
        probs = sb("probs", [P, SLOTS, 2 * CH])
        mx = sb("mx", [P, 2, 8, 4])
        m8 = sb("m8", [P, 8])
        mh = sb("mh", [P, 8], F32R)
        mt = sb("mt", [P, 4, P])
        sums = sb("sums", [P, CH])
        sel = sb("sel", [P, 2, WIDTH])
        PS = [ps(f"PS{i}", [P, CH]) for i in range(BANKS)]
        PM = [ps(f"PM{i}", [P, CH]) for i in range(BANKS)]
        PV = ps("PV", [P, CH])
        MISC = ps("MISC", [P, CH])

        keys_in = [sem(f"keys_in{i}") for i in range(2)]
        queries_in = [sem(f"queries_in{i}") for i in range(2)]
        queries_moved = sem("queries_moved")
        buffers_set = sem("buffers_set")
        sel_set = sem("sel_set")
        values_in = sem("values_in")
        max_products = sem("max_products")
        maxima = sem("maxima")
        row_maxima = sem("row_maxima")
        split = sem("split")
        shifts_ready = sem("shifts_ready")
        shifts_turned = sem("shifts_turned")
        shifts_placed = sem("shifts_placed")
        scores = sem("scores")
        exps = sem("exps")
        pv_groups = sem("pv_groups")
        sums_out = sem("sums_out")
        gathered = sem("gathered")
        outputs = sem("outputs")
        tick, tick_sp, tick_act = sem("tick"), sem("tick_sp"), sem("tick_act")
        block = ctx.enter_context(nc.Block())

        def last_user(n, i):
            return n - (BANKS if i >= BANKS - 1 else BANKS - 1) + 1

        def steps_done(n):
            return GROUPS * n + SLOTS // 2

        def over_iterations(eng, body):
            with eng.Fori(0, ITERS - 1) as it:
                body(it, False)
            body(ITERS - 1, True)

        @block.sync
        def _(sp):
            def hold(semaphore, value):
                sp.wait_ge(semaphore, value)
                sp.sem_inc(tick_sp)

            def rows(part, which, first, cols):
                return g.qkT[part][which, bass.ds(first, HD), cols]

            def load_keys(i, unit):
                for hh in range(2):
                    for at, part in ((0, 0), (16, 1), (34, 0)):
                        sp.dma_start(K[i][64 * hh + at:64 * hh + at + HD, :].bitcast(F32),
                                     rows(part, 1, unit * 2 * HD + HD * hh, slice(0, N))).then_inc(keys_in[i], 16)

            def load_queries(i, unit, c):
                for hh in range(2):
                    for at, part in ((0, 0), (16, 0), (34, 1)):
                        sp.dma_start(QM[i][64 * hh + at:64 * hh + at + HD, hh, :].bitcast(F32),
                                     rows(part, 0, unit * 2 * HD + HD * hh, slice(c * CH, (c + 1) * CH))
                                     ).then_inc(queries_in[i], 16)

            def move_queries(i):
                sp.dma_start(QE[i][:].bitcast(F32), QM[i][:].bitcast(F32)).then_inc(queries_moved, 16)

            hold(buffers_set, 8)
            load_keys(0, 0)
            load_queries(0, 0, 0)
            load_queries(1, 0, 1)
            load_keys(1, 1)
            hold(queries_in[0], 96)
            move_queries(0)
            hold(queries_moved, 16)
            hold(max_products, 32)
            load_queries(0, 0, 2)

            def body(it, last):
                for r in range(BODY):
                    s = BODY * it + r
                    if r % CHUNKS == 1 and not (last or r < CHUNKS):
                        hold(pv_groups, steps_done(s - 1))
                        load_keys(0, 2 * it + 2)
                    if not (last and r == BODY - 1):
                        n = (r + 1) // 2
                        hold(queries_in[(r + 1) % 2], 96 * (4 * it + n + 1))
                        hold(pv_groups, steps_done(s))
                        move_queries((r + 1) % 2)
                    if not (last and r >= BODY - 3):
                        hold(max_products, 32 * (s + 2))
                        hold(queries_moved, 16 * (s + 2))
                        n = r + 3
                        load_queries((r + 1) % 2, 2 * it + n // CHUNKS, n % CHUNKS)
                if not last:
                    hold(pv_groups, steps_done(BODY * it + BODY))
                    load_keys(1, 2 * it + 3)

            over_iterations(sp, body)

        @block.gpsimd
        def _(pool):
            for i in range(2):
                nc.gpsimd.memset(K[i][:].bitcast(F32), -1.0).then_inc(buffers_set, 1)
                nc.gpsimd.memset(QM[i][:].bitcast(F32), 0.0).then_inc(buffers_set, 1)
                nc.gpsimd.memset(VU[i][:], 0.0).then_inc(buffers_set, 1)
            nc.gpsimd.memset(mt[:], 0.0).then_inc(buffers_set, 1)
            nc.gpsimd.memset(sel[:], 0.0).then_inc(buffers_set, 1)
            pool.wait_ge(buffers_set, 8)
            for i in range(2):
                nc.gpsimd.memset(VU[i][:, :, :, HD:WIDTH], 1.0).then_inc(sel_set, 1)
            for hh in range(2):
                for par in range(2):
                    nc.gpsimd.affine_select(out=sel[:, hh, :], in_=sel[:, hh, :], compare_op=ALU.not_equal, fill=1.0,
                                            base=-32 * (2 * hh + par), pattern=[[-1, WIDTH]],
                                            channel_multiplier=1).then_inc(sel_set, 1)
                    pool.wait_ge(sel_set, 3 + 2 * hh + par)

            def load_values(i, unit):
                nc.gpsimd.tensor_copy(VU[i][:, :, :, 0:HD],
                                      g.V[:, bass.ds(unit, 1), :, :].rearrange("p o t (h e) -> p (o t) h e", h=2)
                                      ).then_inc(values_in, 1)

            load_values(0, 0)
            load_values(1, 1)

            def load_next(it, i):
                pool.wait_ge(pv_groups, steps_done(BODY * it + CHUNKS * (i + 1)))
                pool.sem_inc(tick)
                load_values(i, 2 * it + 2 + i)

            def shifts(s):
                pool.wait_ge(row_maxima, s + 1)
                if not (isinstance(s, int) and s == 0):
                    pool.wait_ge(shifts_turned, s)
                pool.sem_inc(tick)
                nc.gpsimd.tensor_copy(mh[:], m8[:]).then_inc(split, 1)
                pool.wait_ge(split, s + 1)
                pool.sem_inc(tick)
                cols = mt[:].rearrange("p q (h c) -> p q h c", h=2)
                m = m8[:].rearrange("p (q h) -> p q h", h=2)
                top = mh[:].bitcast(F32).rearrange("p (q h) -> p q h", h=2)
                nc.gpsimd.tensor_copy(cols[:, :, :, 32], top)
                nc.gpsimd.tensor_tensor(cols[:, :, :, 33], m, top, ALU.subtract).then_inc(shifts_ready, 1)

            shifts(0)

            def body(it, last):
                for r in range(BODY):
                    s = BODY * it + r
                    if not (last and r == BODY - 1):
                        shifts(s + 1)
                    if r == CHUNKS and not last:
                        load_next(it, 0)
                if not last:
                    load_next(it, 1)

            over_iterations(pool, body)

        @block.tensor
        def _(pe):
            def score_product(s, r, i):
                kt, hh = i // 2, i % 2
                pe.wait_ge(exps, last_user(EACH * s + i, i) + AHEAD)
                nc.tensor.matmul(PS[i % BANKS][:], K[r % BODY // CHUNKS][0:USED, kt * P:(kt + 1) * P],
                                 QE[r % 2][0:USED, hh, :], start=True, stop=True).then_inc(scores, 1)

            def max_product(s, r, it, i):
                qt, kc, hh, u = i // 8, i // 2 % 4, i % 2, (r % BODY) // CHUNKS
                if i == 0:
                    pe.wait_ge(queries_in[r % 2], 96 * (4 * it + r // 2 + 1))
                    if r % CHUNKS == 0:
                        pe.wait_ge(keys_in[u], 96 * (it + r // BODY + 1))
                pe.wait_ge(maxima, last_user(EACH * s + i, i) + AHEAD)
                nc.tensor.matmul(PM[i % BANKS][:], QM[r % 2][0:USED, hh, qt * P:(qt + 1) * P],
                                 K[u][0:USED, kc * CH:(kc + 1) * CH], start=True, stop=True
                                 ).then_inc(max_products, 1)

            def turn_shifts(s):
                pe.wait_ge(shifts_ready, s + 1)
                pe.wait_ge(outputs, s if not isinstance(s, int) else max(s, 1))
                for qt in range(4):
                    last = nc.tensor.transpose(MISC[:, qt * P:(qt + 1) * P], mt[:, qt, :], g.ident[:])
                last.then_inc(shifts_turned, 1)

            def value_products(s, r, it, j):
                pe.wait_ge(exps, EACH * s + 4 * j + 4 + AHEAD)
                if j == 0:
                    pe.wait_ge(sums_out, s + 1)
                    pe.wait_ge(values_in, 2 * it + r // CHUNKS + 1)
                for hh in range(2):
                    for par in range(2):
                        kt, quad = 2 * j + par, 2 * hh + par
                        last = nc.tensor.matmul(PV[32 * quad:32 * quad + VW, :], VU[r // CHUNKS][:, kt, hh, :],
                                                probs[:, kt % SLOTS, hh * CH:(hh + 1) * CH],
                                                start=j == 0, stop=j == GROUPS - 1, tile_position=(0, 32 * quad))
                last.then_inc(pv_groups, 1)

            def gather_ready(s):
                pe.wait_ge(sums_out, s + 2)
                pe.wait_ge(outputs, s + 1)
                if not (isinstance(s, int) and s == STEPS - 1):
                    pe.wait_ge(shifts_placed, 2 * s + 4)

            def gather(qt):
                nc.tensor.matmul(MISC[:, qt * 2 * WIDTH:(qt + 1) * 2 * WIDTH], sums[:, qt * P:(qt + 1) * P],
                                 sel[:].rearrange("p h e -> p (h e)"), start=True, stop=True).then_inc(gathered, 1)

            pe.sem_inc(pv_groups, SLOTS // 2)
            pe.sem_inc(gathered, 1)
            pe.wait_ge(sel_set, 6)
            for i in range(EACH):
                max_product(0, 0, 0, i)
            turn_shifts(0)
            for i in range(4 * EARLY):
                max_product(1, 1, 0, i)
            pe.wait_ge(shifts_placed, 2)
            for i in range(4):
                score_product(0, 0, i)

            def body(it, last):
                for r in range(BODY):
                    s = BODY * it + r
                    final = last and r == BODY - 1
                    for j in range(GROUPS):
                        if j == 2 and r > 0:
                            gather_ready(s - 1)
                        for h in range(4):
                            if j < GROUPS - EARLY:
                                if not final:
                                    max_product(s + 1, r + 1, it, 4 * (j + EARLY) + h)
                            elif not (last and r >= BODY - 2):
                                max_product(s + 2, r + 2, it, 4 * (j - GROUPS + EARLY) + h)
                            if j < GROUPS - 1:
                                score_product(s, r, 4 * (j + 1) + h)
                            elif not final:
                                if h == 0:
                                    pe.wait_ge(shifts_placed, 2 * s + 4)
                                score_product(s + 1, r + 1, h)
                            if j == 2 and r > 0:
                                gather(h)
                        if j == GROUPS - EARLY and not final:
                            turn_shifts(s + 1)
                        value_products(s, r, it, j)
                gather_ready(s)
                for qt in range(4):
                    gather(qt)

            over_iterations(pe, body)

        @block.scalar
        def _(act):
            def place_shifts(s, r):
                act.wait_ge(queries_moved, 16 * (s + 1))
                act.wait_ge(shifts_turned, s + 1)
                for hh in range(2):
                    at = slice(64 * hh + 32, 64 * hh + 34)
                    nc.scalar.copy(QE[r % 2][at, hh, :], MISC[at, :]).then_inc(shifts_placed, 1)

            def keep_outputs(s, it, r):
                act.wait_ge(gathered, 4 * s + 5)
                act.sem_inc(tick_act)
                t0 = CH // P * (r % CHUNKS)
                nc.scalar.copy(g.O[:, bass.ds(2 * it + r // CHUNKS, 1), t0:t0 + 4, :].rearrange("p o t e -> p (o t) e"),
                               MISC[:, 0:8 * WIDTH].rearrange("p (t e) -> p t e", t=4)).then_inc(outputs, 1)

            def exp_tile(s, kt):
                if kt % 2 == 0:
                    act.wait_ge(pv_groups, GROUPS * s + kt // 2 + 1)
                for hh in range(2):
                    i = 2 * kt + hh
                    act.wait_ge(scores, EACH * s + i + 1)
                    nc.scalar.activation(probs[:, kt % SLOTS, hh * CH:(hh + 1) * CH], PS[i % BANKS][:], ACT.Exp
                                         ).then_inc(exps, 1)

            act.sem_inc(exps, AHEAD)
            act.sem_inc(sums_out, 1)
            act.sem_inc(outputs, 1)
            place_shifts(0, 0)
            for kt in range(OVER):
                exp_tile(0, kt)

            def body(it, last):
                for r in range(BODY):
                    s = BODY * it + r
                    final = last and r == BODY - 1
                    for kt in range(OVER, KT):
                        if kt == 8 and r > 0:
                            keep_outputs(s - 1, it, r - 1)
                        if kt == KT - 2 * EARLY + 3 and not final:
                            place_shifts(s + 1, r + 1)
                        exp_tile(s, kt)
                    if not final:
                        for kt in range(OVER):
                            exp_tile(s + 1, kt)
                    act.wait_ge(pv_groups, steps_done(s + 1))
                    act.wait_ge(gathered, 4 * s + 1)
                    nc.scalar.copy(sums[:], PV[:]).then_inc(sums_out, 1)
                keep_outputs(s, it, r)

            over_iterations(act, body)

        @block.vector
        def _(dve):
            def max_group(s, r, grp):
                for i in range(4 * grp, 4 * grp + 4):
                    qt, kc, hh = i // 8, i // 2 % 4, i % 2
                    dve.wait_ge(max_products, EACH * s + i + 1)
                    nc.vector.reduce_max(mx[:, r % 2, 2 * qt + hh, kc:kc + 1], PM[i % BANKS][:], AX).then_inc(maxima, 1)

            def row_maximum(s, r):
                if not (isinstance(s, int) and s == 0):
                    dve.wait_ge(shifts_ready, s)
                dve.wait_ge(maxima, EACH * (s + 1) + AHEAD)
                nc.vector.reduce_max(m8[:], mx[:, r % 2, :, :], AX).then_inc(row_maxima, 1)

            dve.sem_inc(maxima, AHEAD)
            for grp in range(GROUPS):
                max_group(0, 0, grp)
            row_maximum(0, 0)
            for grp in range(EARLY):
                max_group(1, 1, grp)

            def body(it, last):
                for r in range(BODY):
                    s = BODY * it + r
                    final = last and r == BODY - 1
                    for j in range(GROUPS):
                        if j < GROUPS - EARLY:
                            if not final:
                                max_group(s + 1, r + 1, j + EARLY)
                                if j == GROUPS - EARLY - 1:
                                    row_maximum(s + 1, r + 1)
                        elif not (last and r >= BODY - 2):
                            max_group(s + 2, r + 2, j - GROUPS + EARLY)

            over_iterations(dve, body)



def projection(nc, g):
    with ExitStack() as ctx:
        sem = open_sem(ctx, nc, "proj")
        sb, ps = open_mem(ctx, nc, "proj")
        wp = sb("wp", [P, KD, D])
        pb = sb("pb", [P, D])
        oc = sb("oc", [P, 2, D])
        rden = sb("rden", [P, 2, PAIRS, 2])
        oT = sb("oT", [P, 2, KD, P])
        y = sb("y", [P, 2, D])
        yg = sb("yg", [P, 2, D])
        st = sb("st2", [P, T, 6])
        pst = [ps(f"pst{i}", [P, KD, P]) for i in range(2)]
        psy = [ps(f"psy{i}", [P, CH]) for i in range(2)]
        (s_par, s_rd, s_oc, s_tr, s_oT, s_prod, s_y, s_yg, s_x, s_st, s_tick) = [
            sem(n) for n in "s_par s_rd s_oc s_tr s_oT s_prod s_y s_yg s_x s_st s_tick".split()]
        block = ctx.enter_context(nc.Block())


        @block.sync
        def _(sp):
            sp.dma_start(wp[:], g.wpT.rearrange("(k p) n -> p k n", p=P)).then_inc(s_par, 16)
            sp.dma_start(pb[:], g.proj_b.partition_broadcast(P)).then_inc(s_par, 16)
            sp.wait_ge(s_par, 32)

        @block.gpsimd
        def _(pool):
            with pool.Fori(0, B) as b:
                with pool.Fori(0, 2) as half:
                    m = 2 * b + half

                    def gate(r):
                        t = GROUP * m + r
                        pool.wait_ge(s_y, t + 1)
                        if r >= 2:
                            pool.wait_ge(s_x, t - 1)
                        pool.sem_inc(s_tick)
                        nc.gpsimd.tensor_mul(yg[:, r % 2, :], y[:, r % 2, :],
                                             g.mod[:, bass.ds(b, 1), 2, :].rearrange("p o d -> p (o d)")
                                             ).then_inc(s_yg, 1)

                    for r in range(GROUP):
                        gate(r)

        @block.scalar
        def _(act):
            with act.Fori(0, T // GROUP) as m:
                for r in range(GROUP):
                    t = GROUP * m + r
                    act.wait_ge(s_tr, t + 1)
                    if r >= 2:
                        act.wait_ge(s_prod, t - 1)
                    nc.scalar.copy(oT[:, r % 2, :, :], pst[r % 2][:]).then_inc(s_oT, 1)

        @block.vector
        def _(dve):
            dve.wait_ge(s_par, 32)
            with dve.Fori(0, B) as b:
                with dve.Fori(0, 2) as half:
                    m = 2 * b + half

                    def tile_of_O(r, e0, e1):
                        src = g.O[:].rearrange("p (b h) t (c e) -> p b h t c e", b=B, c=2)
                        return src[:, bass.ds(b, 1), :, bass.ds(8 * half + r, 1), :, e0:e1].rearrange(
                            "p o h u c e -> p (o h u) c e")

                    def divide(r):
                        t = GROUP * m + r
                        nc.vector.reciprocal(rden[:, r % 2, :, :], tile_of_O(r, HD, HD + 1).rearrange(
                            "p h c e -> p h (c e)")).then_inc(s_rd, 1)
                        dve.wait_ge(s_rd, t + 1)
                        if r >= 2:
                            dve.wait_ge(s_tr, t - 1)
                        nc.vector.tensor_mul(oc[:, r % 2, :].rearrange("p (h c e) -> p h c e", h=PAIRS, c=2),
                                             tile_of_O(r, 0, HD),
                                             rden[:, r % 2, :, :].unsqueeze(3).to_broadcast([P, PAIRS, 2, HD])
                                             ).then_inc(s_oc, 1)

                    def add_bias(r):
                        t = GROUP * m + r
                        dve.wait_ge(s_prod, t + 1)
                        if r >= 2:
                            dve.wait_ge(s_yg, t - 1)
                        nc.vector.tensor_add(y[:, r % 2, :], psy[r % 2][:, 0:D], pb[:]).then_inc(s_y, 1)

                    def residual(r):
                        t = GROUP * m + r
                        x = g.X[:, bass.ds(t, 1), :].rearrange("p o d -> p (o d)")
                        dve.wait_ge(s_yg, t + 1)
                        nc.vector.tensor_add(x, x, yg[:, r % 2, :]).then_inc(s_x, 1)

                    def statistics(r):
                        t = GROUP * m + r
                        dve.wait_ge(s_x, t + 1)
                        dve.sem_inc(s_tick)
                        nc.vector.bn_stats(st[:, bass.ds(t, 1), :].rearrange("p o d -> p (o d)"),
                                           g.X[:, bass.ds(t, 1), :].rearrange("p o d -> p (o d)")).then_inc(s_st, 1)

                    for k in range(GROUP + 3):
                        if k < GROUP:
                            divide(k)
                        if 1 <= k <= GROUP:
                            add_bias(k - 1)
                        if 2 <= k <= GROUP + 1:
                            residual(k - 2)
                        if k >= 3:
                            statistics(k - 3)
            dve.wait_ge(s_st, T)
            for t in range(T):
                last = nc.vector.bn_aggr(g.mv[:, t, :], st[:, t, :])
            last.then_inc(s_st, 1)
            dve.wait_ge(s_st, T + 1)
            nc.vector.tensor_scalar_add(g.sd[:, 1, :], g.mv[:, :, 1], EPS).then_inc(s_st, 1)

        @block.tensor
        def _(pe):
            pe.wait_ge(s_par, 32)
            with pe.Fori(0, T // GROUP) as m:
                def turn(r):
                    t = GROUP * m + r
                    pe.wait_ge(s_oc, t + 1)
                    if r >= 2:
                        pe.wait_ge(s_oT, t - 1)
                    for k in range(KD):
                        last = nc.tensor.transpose(pst[r % 2][:, k, :], oc[:, r % 2, k * P:(k + 1) * P], g.ident[:])
                    last.then_inc(s_tr, 1)

                def project(r):
                    t = GROUP * m + r
                    pe.wait_ge(s_oT, t + 1)
                    if r >= 2:
                        pe.wait_ge(s_y, t - 1)
                    for k in range(KD):
                        last = nc.tensor.matmul(psy[r % 2][:, 0:D], oT[:, r % 2, k, :], wp[:, k, :],
                                                start=k == 0, stop=k == KD - 1)
                    last.then_inc(s_prod, 1)

                for k in range(GROUP + 1):
                    if k < GROUP:
                        turn(k)
                    if k:
                        project(k - 1)
                pe.wait_ge(s_y, GROUP * m + GROUP)


def gate_stage(nc, g):
    with ExitStack() as ctx:
        sem = open_sem(ctx, nc, "gate")
        sb, ps = open_mem(ctx, nc, "gate")
        gw = sb("gw", [P, KD, E])
        bias = sb("bias", [P, 2, E])
        hn = sb("hn", [P, 2, D])
        hm = sb("hm", [P, 2, D])
        hT = sb("hT", [P, 2, KD, P])
        lg = sb("lg", [P, 2, E])
        pst = [ps(f"pst{i}", [P, KD, P]) for i in range(2)]
        psg = [ps(f"psg{i}", [P, CH]) for i in range(2)]
        (s_par, s_sd, s_v, s_hn, s_hm, s_tr, s_hT, s_h2, s_prod, s_lg, s_out, s_tick) = [
            sem(n) for n in "s_par s_sd s_v s_hn s_hm s_tr s_hT s_h2 s_prod s_lg s_out s_tick".split()]
        block = ctx.enter_context(nc.Block())

        @block.sync
        def _(sp):
            sp.dma_start(gw[:], g.gwT.rearrange("(k p) n -> p k n", p=P)).then_inc(s_par, 16)
            sp.dma_start(bias[:, 0, :], g.gate_b.partition_broadcast(P)).then_inc(s_par, 16)
            sp.dma_start(bias[:, 1, :], g.expert_bias.partition_broadcast(P)).then_inc(s_par, 16)
            sp.wait_ge(s_par, 48)

        @block.gpsimd
        def _(pool):
            with pool.Fori(0, B) as b:
                with pool.Fori(0, 2) as half:
                    for r in range(GROUP):
                        t = GROUP * (2 * b + half) + r
                        pool.wait_ge(s_hn, t + 1)
                        if r >= 2:
                            pool.wait_ge(s_h2, t - 1)
                        pool.sem_inc(s_tick)
                        nc.gpsimd.tensor_mul(hm[:, r % 2, :], hn[:, r % 2, :],
                                             g.mod[:, bass.ds(b, 1), 4, :].rearrange("p o d -> p (o d)")
                                             ).then_inc(s_hm, 1)
                        pool.wait_ge(s_hm, 2 * t + 1)
                        pool.sem_inc(s_tick)
                        nc.gpsimd.tensor_add(hm[:, r % 2, :], hm[:, r % 2, :],
                                             g.mod[:, bass.ds(b, 1), 3, :].rearrange("p o d -> p (o d)")
                                             ).then_inc(s_hm, 1)

        @block.scalar
        def _(act):
            nc.scalar.activation(g.sd[:, 0, :], g.sd[:, 1, :], ACT.Sqrt).then_inc(s_sd, 1)
            with act.Fori(0, T // GROUP) as m:
                for r in range(GROUP):
                    t = GROUP * m + r
                    act.wait_ge(s_tr, t + 1)
                    act.sem_inc(s_tick)
                    nc.scalar.copy(g.H2[:, bass.ds(t, 1), :].rearrange("p o d -> p (o d)"), hm[:, r % 2, :]
                                   ).then_inc(s_h2, 1)
                    if r >= 2:
                        act.wait_ge(s_prod, t - 1)
                    nc.scalar.copy(hT[:, r % 2, :, :], pst[r % 2][:]).then_inc(s_hT, 1)

        @block.vector
        def _(dve):
            inverse_deviation(nc, dve, g, s_sd, s_v, 0)
            dve.wait_ge(s_par, 48)
            with dve.Fori(0, T // GROUP) as m:
                for k in range(GROUP + 1):
                    if k < GROUP:
                        t = GROUP * m + k
                        if k >= 2:
                            dve.wait_ge(s_hm, 2 * t - 2)
                        nc.vector.tensor_scalar(hn[:, k % 2, :], g.X[:, bass.ds(t, 1), :].rearrange("p o d -> p (o d)"),
                                                g.mv[:, bass.ds(t, 1), 0], g.rs[:, bass.ds(t, 1)],
                                                ALU.subtract, ALU.mult).then_inc(s_hn, 1)
                    if k:
                        r = k - 1
                        t = GROUP * m + r
                        dve.wait_ge(s_prod, t + 1)
                        nc.vector.tensor_add(lg[:, r % 2, :], psg[r % 2][:, 0:E], bias[:, 0, :]).then_inc(s_lg, 1)
                        dve.wait_ge(s_lg, t + 1)
                        nc.vector.tensor_add(g.logits[:, bass.ds(t, 1), :].rearrange("p o e -> p (o e)"),
                                             lg[:, r % 2, :], bias[:, 1, :]).then_inc(s_out, 1)

        @block.tensor
        def _(pe):
            pe.wait_ge(s_par, 48)
            with pe.Fori(0, T // GROUP) as m:
                for k in range(GROUP + 1):
                    if k < GROUP:
                        t = GROUP * m + k
                        pe.wait_ge(s_hm, 2 * t + 2)
                        if k >= 2:
                            pe.wait_ge(s_hT, t - 1)
                        for c in range(KD):
                            last = nc.tensor.transpose(pst[k % 2][:, c, :], hm[:, k % 2, c * P:(c + 1) * P], g.ident[:])
                        last.then_inc(s_tr, 1)
                    if k:
                        r = k - 1
                        t = GROUP * m + r
                        pe.wait_ge(s_hT, t + 1)
                        if r >= 2:
                            pe.wait_ge(s_lg, t - 1)
                        for c in range(KD):
                            last = nc.tensor.matmul(psg[r % 2][:, 0:E], hT[:, r % 2, c, :], gw[:, c, :],
                                                    start=c == 0, stop=c == KD - 1)
                        last.then_inc(s_prod, 1)
                pe.wait_ge(s_lg, GROUP * m + GROUP)


def routing(nc, g):
    KS = B * N // FT
    with ExitStack() as ctx:
        sem = open_sem(ctx, nc, "route")
        sb, ps = open_mem(ctx, nc, "route")
        row = sb("row", [P, g.row.shape[-1]])
        rev, first, number = row[:, 0:E], row[:, E:E + KS], row[:, E + KS:E + KS + NT]
        below = sb("below", [P, P])
        ones = sb("ones", [P, P])
        best = sb("best", [P, T])
        eq = sb("eq", [P, T, E])
        hot = sb("hot", [P, T, E])
        cnt = sb("cnt", [P, T, E])
        upto = sb("upto", [P, E, T])
        more = sb("more", [P, E, KS])
        tiles = sb("tiles", [P, E])
        end = sb("end", [P, E])
        start = sb("start", [P, E])
        place = sb("place", [P, T, E])
        slotf = sb("slotf", [P, T])
        past = sb("past", [P, NT, E])
        which = sb("which", [P, NT])
        psr = ps("psr", [P, CH])
        psc = ps("psc", [P, CH])
        s_par, s_set, s_v, s_hot, s_cnt, s_slot, s_put = [
            sem(n) for n in "s_par s_set s_v s_hot s_cnt s_slot s_put".split()]
        block = ctx.enter_context(nc.Block())

        @block.sync
        def _(sp):
            sp.dma_start(row[:], g.row.partition_broadcast(P)).then_inc(s_par, 16)
            sp.wait_ge(s_par, 16)

        @block.tensor
        def _(pe):
            pe.wait_ge(s_hot, 1)
            pe.wait_ge(s_set, 3)
            flat = hot[:].rearrange("p t e -> p (t e)")
            nc.tensor.matmul(psr[:, 0:T * E], below[:], flat, start=True, stop=True).then_inc(s_cnt, 1)
            nc.tensor.matmul(psc[:, 0:T * E], ones[:], flat, start=True, stop=True).then_inc(s_cnt, 1)

        @block.gpsimd
        def _(pool):
            nc.gpsimd.memset(ones[:], 1.0).then_inc(s_set, 1)
            nc.gpsimd.memset(below[:], 1.0).then_inc(s_set, 1)
            pool.wait_ge(s_set, 2)
            nc.gpsimd.affine_select(out=below[:], in_=below[:], compare_op=ALU.is_ge, fill=0.0, base=-1,
                                    pattern=[[1, P]], channel_multiplier=-1).then_inc(s_set, 1)
            pool.wait_ge(s_slot, 1)
            for t in range(T):
                nc.gpsimd.indirect_dma_start(g.hs, bass.IndirectOffsetOnAxis(g.slot[:, t:t + 1], 0), g.H2[:, t, :], None
                                             ).then_inc(s_put, 16)
            pool.wait_ge(s_put, 16 * T)

        @block.vector
        def _(dve):
            done = [0]

            def then(ins):
                done[0] += 1
                ins.then_inc(s_v, 1)
                dve.wait_ge(s_v, done[0])

            over_t = lambda a: a.unsqueeze(1).to_broadcast([P, T, E])
            over_e = lambda a: a.unsqueeze(2).to_broadcast([P, T, E])
            dve.wait_ge(s_par, 16)
            then(nc.vector.reduce_max(best[:], g.logits[:], AX))
            then(nc.vector.tensor_tensor(eq[:], g.logits[:], over_e(best[:]), ALU.is_equal))
            then(nc.vector.tensor_tensor(eq[:], eq[:], over_t(rev), ALU.mult))
            then(nc.vector.reduce_max(best[:], eq[:], AX))
            nc.vector.tensor_tensor(hot[:], over_t(rev), over_e(best[:]), ALU.is_equal).then_inc(s_hot, 1)
            dve.wait_ge(s_cnt, 2)
            then(nc.vector.tensor_copy(cnt[:], psc[:, 0:T * E].rearrange("p (t e) -> p t e", e=E)))
            dve.wait_ge(s_set, 1)
            for e in range(E):
                last = nc.vector.tensor_tensor_scan(upto[:, e, :], ones[:, 0:T], cnt[:, :, e], 0.0, ALU.mult, ALU.add)
            then(last)
            then(nc.vector.tensor_tensor(more[:], upto[:, :, T - 1:T].to_broadcast([P, E, KS]),
                                         first.unsqueeze(1).to_broadcast([P, E, KS]), ALU.is_gt))
            then(nc.vector.reduce_sum(tiles[:], more[:], AX))
            then(nc.vector.tensor_tensor_scan(end[:], ones[:, 0:E], tiles[:], 0.0, ALU.mult, ALU.add))
            then(nc.vector.tensor_sub(start[:], end[:], tiles[:]))
            then(nc.vector.tensor_scalar_mul(start[:], start[:], float(FT)))
            then(nc.vector.tensor_sub(place[:], upto[:].rearrange("p e t -> p t e"), cnt[:]))
            then(nc.vector.tensor_add(place[:], place[:], psr[:, 0:T * E].rearrange("p (t e) -> p t e", e=E)))
            then(nc.vector.tensor_add(place[:], place[:], over_t(start[:])))
            then(nc.vector.tensor_mul(place[:], place[:], hot[:]))
            then(nc.vector.reduce_sum(slotf[:], place[:], AX))
            nc.vector.tensor_copy(g.slot[:], slotf[:]).then_inc(s_slot, 1)
            then(nc.vector.tensor_tensor(past[:], end[:].unsqueeze(1).to_broadcast([P, NT, E]),
                                         number.unsqueeze(2).to_broadcast([P, NT, E]), ALU.is_le))
            then(nc.vector.reduce_sum(which[:], past[:], AX))
            then(nc.vector.tensor_scalar_min(which[:], which[:], float(E - 1)))
            nc.vector.tensor_copy(g.which[:], which[:]).then_inc(s_v, 1)


def experts(nc, g):
    SUB = FT // P
    with ExitStack() as ctx:
        sem = open_sem(ctx, nc, "ffn")
        sb, ps = open_mem(ctx, nc, "ffn")
        w1 = [sb(f"w1_{i}", [P, KD, F]) for i in range(2)]
        w2 = [sb(f"w2_{i}", [P, KF, D]) for i in range(2)]
        b1 = [sb(f"b1_{i}", [P, KF]) for i in range(2)]
        b2 = [sb(f"b2_{i}", [P, D]) for i in range(2)]
        rows = [sb(f"rows{i}", [P, SUB, D]) for i in range(2)]
        hT = [sb(f"hT{i}", [P, KD, FT]) for i in range(2)]
        hid = sb("hid", [P, KF, FT])
        y = [sb(f"y{i}", [P, SUB, D]) for i in range(2)]
        pst = [ps(f"pst{i}", [P, KD, FT]) for i in range(2)]
        psh = [ps(f"psh{i}", [P, 2, FT]) for i in range(4)]
        psy = [ps(f"psy{i}", [P, SUB, D]) for i in range(2)]
        in1 = [sem(f"in1_{i}") for i in range(2)]
        in2 = [sem(f"in2_{i}") for i in range(2)]
        in3 = [sem(f"in3_{i}") for i in range(2)]
        turned, hT_ready, layer1, hid_ready, layer2, y_ready, tick, tick_act = [
            sem(n) for n in "turned hT_ready layer1 hid_ready layer2 y_ready tick tick_act".split()]
        stored = [sem(f"stored{i}") for i in range(2)]
        block = ctx.enter_context(nc.Block())

        def over_tiles(eng, tile):
            with eng.Fori(0, NT // 2) as i:
                for par in range(2):
                    tile(2 * i + par, par, i, False)
            if NT % 2:
                tile(NT - 1, 0, NT // 2, True)

        @block.sync
        def _(sp):
            def hold(semaphore, value):
                sp.wait_ge(semaphore, value)
                sp.sem_inc(tick)

            def load(k, par, i, last):
                e = sp.value_load(g.which[0:1, k:k + 1] if isinstance(k, int) else g.which[0:1, bass.ds(k, 1)],
                                  min_val=0, max_val=E - 1)
                hold(turned, k + 1)
                sp.dma_start(rows[par][:], g.hs.rearrange("(k s p) d -> k p s d", s=SUB, p=P)[bass.ds(k, 1)]
                             .rearrange("o p s d -> p (o s) d")).then_inc(in3[par], 16)
                hold(hid_ready, KF * k + KF)
                sp.dma_start(w1[par][:], g.w1[bass.ds(e, 1)].rearrange("o (k p) f -> p (o k) f", p=P)
                             ).then_inc(in1[par], 16)
                sp.dma_start(b1[par][:], g.b1T[bass.ds(e, 1)].rearrange("o p k -> p (o k)")).then_inc(in1[par], 16)
                hold(y_ready, k + 1)
                sp.dma_start(w2[par][:], g.w2[bass.ds(e, 1)].rearrange("o (k p) d -> p (o k) d", p=P)
                             ).then_inc(in2[par], 16)
                sp.dma_start(b2[par][:], g.b2[bass.ds(e, 1)].rearrange("o d -> (o d)").partition_broadcast(P)
                             ).then_inc(in2[par], 16)

            over_tiles(sp, load)

        @block.scalar
        def _(act):
            act.sem_inc(hid_ready, AHEAD * KF)

            def copy_turned(k, par, i):
                act.wait_ge(turned, k + 1 + AHEAD)
                nc.scalar.copy(hT[par][:], pst[par][:]).then_inc(hT_ready, 1)

            def store(k, par):
                act.wait_ge(y_ready, k + 1 + AHEAD)
                act.sem_inc(tick_act)
                act.dma_start(g.ys.rearrange("(k s p) d -> k p s d", s=SUB, p=P)[bass.ds(k, 1)]
                              .rearrange("o p s d -> p (o s) d"), y[par][:]).then_inc(stored[par], 16)

            for par in range(2):
                act.sem_inc(stored[par], 16)
            copy_turned(0, 0, 0)

            def tile(k, par, i, last):
                act.wait_ge(in1[par], 32 * (i + 1))
                act.wait_ge(layer2, k + 1)
                for f in range(KF):
                    act.wait_ge(layer1, KF * k + f // 2 * 2 + 2)
                    nc.scalar.activation(hid[:, f, :], psh[f // 2][:, f % 2, :], ACT.Relu, bias=b1[par][:, f:f + 1]
                                         ).then_inc(hid_ready, 1)
                if not last:
                    copy_turned(k + 1, 1 - par, i)
                store(k, par)

            over_tiles(act, tile)
            for par in range(2):
                act.wait_ge(stored[par], 16 * ((NT + 1 - par) // 2) + 16)

        @block.vector
        def _(dve):
            dve.sem_inc(y_ready, AHEAD)

            def tile(k, par, i, last):
                dve.wait_ge(in2[par], 32 * (i + 1))
                dve.wait_ge(stored[par], 16 * (i + 1))
                dve.wait_ge(layer2, k + 2)
                nc.vector.tensor_add(y[par][:], psy[par][:], b2[par][:].unsqueeze(1).to_broadcast([P, SUB, D])
                                     ).then_inc(y_ready, 1)

            over_tiles(dve, tile)

        @block.tensor
        def _(pe):
            pe.sem_inc(turned, AHEAD)
            pe.sem_inc(layer2, 1)

            def turn(k, par, i):
                pe.wait_ge(in3[par], 16 * (i + 1))
                for s in range(SUB):
                    for c in range(KD):
                        last = nc.tensor.transpose(pst[par][:, c, s * P:(s + 1) * P],
                                                   rows[par][:, s, c * P:(c + 1) * P], g.ident[:])
                last.then_inc(turned, 1)

            turn(0, 0, 0)

            def tile(k, par, i, last):
                pe.wait_ge(hT_ready, k + 1)
                pe.wait_ge(in1[par], 32 * (i + 1))
                for f in range(KF):
                    pe.wait_ge(hid_ready, KF * k + f + 1 + KF if f % 2 else KF * k + f + 2 + KF)
                    for c in range(KD):
                        last_mm = nc.tensor.matmul(psh[f // 2][:, f % 2, :], w1[par][:, c, f * P:(f + 1) * P],
                                                   hT[par][:, c, :], start=c == 0, stop=c == KD - 1)
                    last_mm.then_inc(layer1, 1)
                if not last:
                    turn(k + 1, 1 - par, i + par)
                pe.wait_ge(in2[par], 32 * (i + 1))
                pe.wait_ge(y_ready, k + 1)
                for s in range(SUB):
                    for f in range(KF):
                        if s == 0:
                            pe.wait_ge(hid_ready, KF * k + f + 1 + AHEAD * KF)
                        last_mm = nc.tensor.matmul(psy[par][:, s, :], hid[:, f, s * P:(s + 1) * P], w2[par][:, f, :],
                                                   start=f == 0, stop=f == KF - 1)
                last_mm.then_inc(layer2, 1)

            over_tiles(pe, tile)


def combine(nc, g):
    FLIGHT = 8
    with ExitStack() as ctx:
        sem = open_sem(ctx, nc, "comb")
        sb, ps = open_mem(ctx, nc, "comb")
        got = sb("got", [P, T, D])
        fetched = [sem(f"fetched{i}") for i in range(FLIGHT)]
        s_g, s_o, s_out = sem("s_g"), sem("s_o"), sem("s_out")
        block = ctx.enter_context(nc.Block())
        LOT = 4

        @block.gpsimd
        def _(pool):
            for t in range(T):
                if t >= FLIGHT:
                    pool.wait_ge(fetched[t % FLIGHT], 16 * (t // FLIGHT))
                nc.gpsimd.indirect_dma_start(got[:, t, :], None, g.ys, bass.IndirectOffsetOnAxis(g.slot[:, t:t + 1], 0)
                                             ).then_inc(fetched[t % FLIGHT], 16)

        @block.vector
        def _(dve):
            for t in range(T):
                b = t // TB
                dve.wait_ge(fetched[t % FLIGHT], 16 * (t // FLIGHT + 1))
                nc.vector.tensor_mul(got[:, t, :], got[:, t, :], g.mod[:, b, 5, :]).then_inc(s_g, 1)
                if t:
                    dve.wait_ge(s_g, t)
                    nc.vector.tensor_add(g.X[:, t - 1, :], g.X[:, t - 1, :], got[:, t - 1, :]).then_inc(s_o, 1)
            dve.wait_ge(s_g, T)
            nc.vector.tensor_add(g.X[:, T - 1, :], g.X[:, T - 1, :], got[:, T - 1, :]).then_inc(s_o, 1)

        @block.sync
        def _(sp):
            dst = g.out.rearrange("b (t p) d -> p (b t) d", p=P)
            for t in range(0, T, LOT):
                sp.wait_ge(s_o, t + LOT)
                sp.dma_start(dst[:, t:t + LOT, :], g.X[:, t:t + LOT, :]).then_inc(s_out, 16)
            sp.wait_ge(s_out, 16 * T // LOT)



def build(nc, ins, consts, out, debug=None):
    g = Ctx()
    (g.x, g.wqkvT, g.qkv_b, g.wpT, g.proj_b, g.gwT, g.gate_b, g.expert_bias, g.w1, g.b1T, g.w2, g.b2, g.cT,
     g.wmod) = ins
    g.rope, g.row = consts
    g.out = out
    g.qkT = [nc.dram_tensor(f"qkT_{part}", (2, B * D, N), F32, kind="Internal").ap() for part in ("hi", "lo")]
    g.hs = nc.dram_tensor("routed_rows", (NT * FT, D), F32, kind="Internal").ap()
    g.ys = nc.dram_tensor("expert_rows", (NT * FT, D), F32, kind="Internal").ap()
    with ExitStack() as ctx:
        sb, _ = open_mem(ctx, nc, "all")
        g.ident = sb("ident", [P, P])
        g.X = sb("X", [P, T, D])
        g.mv = sb("mv", [P, T, 2])
        g.sd = sb("sd", [P, 3, T])
        g.rs = sb("rs", [P, T])
        g.mod = sb("mod", [P, B, 6, D])
        with ExitStack() as inner:
            g.V = inner.enter_context(nc.sbuf_tensor("V", [P, UNITS, TB, 2 * HD], F32))
            setup(nc, g)
            qkv_stage(nc, g)
            g.O = inner.enter_context(nc.sbuf_tensor("O", [P, UNITS, TB, 2 * (HD + 1)], F32))
            attention(nc, g)
            if debug == 3:
                dump(nc, g, None)
            projection(nc, g)
            if debug == 1:
                dump(nc, g, g.qkT[0][0])
            if debug == 2:
                dump(nc, g, g.qkT[1][1])
        with ExitStack() as inner:
            isb, _ = open_mem(inner, nc, "ffn_all")
            g.logits = isb("logits", [P, T, E])
            g.slot = isb("slot", [P, T], I32)
            g.which = isb("which_i", [P, NT], I32)
            with ExitStack() as rows:
                g.H2 = rows.enter_context(nc.sbuf_tensor("H2", [P, T, D], F32))
                gate_stage(nc, g)
                routing(nc, g)
            experts(nc, g)
            combine(nc, g)


def dump(nc, g, src):
    with ExitStack() as ctx:
        s_d = ctx.enter_context(nc.semaphore("s_dump"))
        block = ctx.enter_context(nc.Block())

        @block.sync
        def _(sp):
            if src is None:
                for b in range(B):
                    for u in range(PAIRS):
                        sp.dma_start(g.out[b].rearrange("(t p) (h e) -> p h t e", p=P, h=PAIRS)[:, u],
                                     g.O[:, b * PAIRS + u]).then_inc(s_d, 16)
                sp.wait_ge(s_d, 16 * B * PAIRS)
                return
            sp.dma_start(g.out.rearrange("b n d -> (b n d)").rearrange("(a c) -> a c", c=2048), src).then_inc(s_d, 16)
            sp.wait_ge(s_d, 16)


def rope_tables():
    inv = (1.0 / np.float32(10000.0) ** (np.arange(0, HD, 2, dtype=np.float32) / np.float32(HD))).astype(np.float32)
    freqs = np.arange(N, dtype=np.float32)[:, None] * inv[None, :]
    cos, sin = np.cos(freqs).astype(np.float32), np.sin(freqs).astype(np.float32)
    return np.ascontiguousarray(np.stack([np.repeat(cos, 2, axis=1), np.stack([-sin, sin], axis=-1).reshape(N, HD)]))


def routing_row():
    return np.concatenate([E - np.arange(E), FT * np.arange(B * N // FT), np.arange(NT)]).astype(np.float32)


DEBUG = None


def kernel(L0_attn_x, L0_attn_qkv_w, L0_attn_qkv_b, L0_attn_proj_w, L0_attn_proj_b, L0_ffn_gate_w, L0_ffn_gate_b,
           L0_ffn_expert_bias, L0_ffn_w1, L0_ffn_b1, L0_ffn_w2, L0_ffn_b2, L0_c, L0_wmod):
    import concourse.bacc as bacc
    from concourse.bass_utils import run_bass_kernel_spmd

    laid = {
        "x": L0_attn_x, "wqkvT": np.asarray(L0_attn_qkv_w).T, "qkv_b": L0_attn_qkv_b,
        "wpT": np.asarray(L0_attn_proj_w).T, "proj_b": L0_attn_proj_b, "gwT": np.asarray(L0_ffn_gate_w).T,
        "gate_b": L0_ffn_gate_b, "expert_bias": L0_ffn_expert_bias, "w1": L0_ffn_w1,
        "b1T": np.asarray(L0_ffn_b1).reshape(E, KF, P).transpose(0, 2, 1), "w2": L0_ffn_w2, "b2": L0_ffn_b2,
        "cT": np.asarray(L0_c).T, "wmod": L0_wmod,
    }
    nc = bacc.Bacc("TRN2", target_bir_lowering=False, num_devices=1)
    arrays, ins = {}, []
    for name, a in laid.items():
        a = np.ascontiguousarray(a)
        arrays["in_" + name] = a
        ins.append(nc.dram_tensor("in_" + name, a.shape, mybir.dt.from_np(a.dtype), kind="ExternalInput").ap())
    consts = []
    for name, a in (("rope", rope_tables()), ("row", routing_row())):
        arrays["const_" + name] = a
        consts.append(nc.dram_tensor("const_" + name, a.shape, mybir.dt.from_np(a.dtype), kind="ExternalInput").ap())
    out = nc.dram_tensor("out", (B, N, D), F32, kind="ExternalOutput").ap()
    build(nc, ins, consts, out, DEBUG)
    return run_bass_kernel_spmd(nc, [arrays], core_ids=[0]).results[0]["out"]
```

```python
from contextlib import ExitStack

import numpy as np
import concourse.bass as bass
from concourse import mybir

ALU = mybir.AluOpType
ACT = mybir.ActivationFunctionType
AX = mybir.AxisListType.X
F32 = mybir.dt.float32
F32R = mybir.dt.float32r
I32 = mybir.dt.int32
U32 = mybir.dt.uint32

P = 128
B, N, D = 2, 2048, 256
H, HD = 16, 16
F, E = 1024, 8
T = B * N // P
TB = N // P
KD = D // P
KF = F // P
QKV = 3 * D
EPS = 1e-5
SCALE = HD ** -0.5
PAIRS = H // 2
UNITS = B * PAIRS
CH = 512
CHUNKS = N // CH
STEPS = UNITS * CHUNKS
ROWS = 50
GROUP = 8
FT = 256
NT = (B * N) // FT + E - 1
AHEAD = 2


class Ctx:
    pass


def open_sem(ctx, nc, stage):
    return lambda name: ctx.enter_context(nc.semaphore(f"{stage}_{name}"))


def open_mem(ctx, nc, stage):
    sb = lambda name, shape, dt=F32: ctx.enter_context(nc.sbuf_tensor(f"{stage}_{name}", shape, dt))
    ps = lambda name, shape, dt=F32: ctx.enter_context(nc.psum_tensor(f"{stage}_{name}", shape, dt))
    return sb, ps


def setup(nc, g):
    with ExitStack() as ctx:
        sem = open_sem(ctx, nc, "set")
        sb, ps = open_mem(ctx, nc, "set")
        cT = sb("cT", [P, KD, B])
        cs = sb("cs", [P, 3, KD * B])
        cb = sb("cb", [P, KD, B, P])
        wmod = sb("wmod", [P, KD, 6 * D])
        st = sb("st", [P, T, 6])
        mag = sb("mag", [P, B, D])
        psm = [ps(f"psm{b}", [P, 6 * D]) for b in range(B)]
        LOTS = 4
        s_x = [sem(f"s_x{i}") for i in range(LOTS)]
        s_c, s_w, s_id = sem("s_c"), sem("s_w"), sem("s_id")
        s_exp, s_v, s_cb, s_mod = sem("s_exp"), sem("s_v"), sem("s_cb"), sem("s_mod")
        s_ev_dve, s_ev_act, s_front = sem("s_ev_dve"), sem("s_ev_act"), sem("s_front")
        s_mv, s_sd = sem("s_mv"), sem("s_sd")
        block = ctx.enter_context(nc.Block())

        @block.sync
        def _(sp):
            sp.dma_start(cT[:], g.cT.rearrange("(k p) b -> p k b", p=P)).then_inc(s_c, 16)
            sp.dma_start(wmod[:], g.wmod.rearrange("(k p) n -> p k n", p=P)).then_inc(s_w, 16)
            xd = g.x.rearrange("b (t p) d -> p (b t) d", p=P)
            for i in range(LOTS):
                lot = slice(i * T // LOTS, (i + 1) * T // LOTS)
                sp.dma_start(g.X[:, lot, :], xd[:, lot, :]).then_inc(s_x[i], 16)
            sp.dma_start(g.wq[:], g.wqkvT.rearrange("(k p) n -> p k n", p=P)).then_inc(s_front, 16)
            sp.dma_start(g.qb[:], g.qkv_b.partition_broadcast(P)).then_inc(s_front, 16)
            sp.dma_start(g.tab[:], g.rope.rearrange("a (t p) d -> p a t d", p=P)).then_inc(s_front, 16)
            sp.wait_ge(s_c, 16)
            sp.wait_ge(s_w, 16)
            for i in range(LOTS):
                sp.wait_ge(s_x[i], 16)
            sp.wait_ge(s_front, 48)

        @block.gpsimd
        def _(pool):
            nc.gpsimd.memset(g.ident[:], 0.0).then_inc(s_id, 1)
            pool.wait_ge(s_id, 1)
            nc.gpsimd.affine_select(out=g.ident[:], in_=g.ident[:], compare_op=ALU.not_equal, fill=1.0, base=0,
                                    pattern=[[-1, P]], channel_multiplier=1).then_inc(s_id, 1)
            for i in range(2):
                nc.gpsimd.memset(g.K[i][:].bitcast(F32), -1.0).then_inc(s_id, 1)
                nc.gpsimd.memset(g.QM[i][:].bitcast(F32), 0.0).then_inc(s_id, 1)
            nc.gpsimd.memset(g.zero[:], 0.0).then_inc(s_id, 1)
            pool.wait_ge(s_id, 7)

        @block.scalar
        def _(act):
            act.wait_ge(s_c, 16)
            nc.scalar.activation(cs[:, 0, :], cT[:].rearrange("p k b -> p (k b)"), ACT.Exp, scale=-1.0).then_inc(s_exp, 1)
            act.wait_ge(s_mod, B)
            nc.scalar.copy(g.mod[:, B - 1, :, :].rearrange("p j d -> p (j d)"), psm[B - 1][:]).then_inc(s_ev_act, 1)
            act.wait_ge(s_mv, 2)
            nc.scalar.activation(g.sd[:, 0, :], g.sd[:, 1, :], ACT.Sqrt).then_inc(s_sd, 1)

        @block.vector
        def _(dve):
            dve.wait_ge(s_exp, 1)
            nc.vector.tensor_scalar_add(cs[:, 1, :], cs[:, 0, :], 1.0).then_inc(s_v, 1)
            dve.wait_ge(s_v, 1)
            nc.vector.reciprocal(cs[:, 2, :], cs[:, 1, :]).then_inc(s_v, 1)
            dve.wait_ge(s_v, 2)
            nc.vector.tensor_mul(cs[:, 0, :], cs[:, 2, :], cT[:].rearrange("p k b -> p (k b)")).then_inc(s_v, 1)
            dve.wait_ge(s_v, 3)
            for k in range(KD):
                for b in range(B):
                    last = nc.vector.tensor_copy(cb[:, k, b, :], cs[:, 0, k * B + b:k * B + b + 1].to_broadcast([P, P]))
            last.then_inc(s_cb, 1)
            for t in range(T):
                if t % (T // LOTS) == 0:
                    dve.wait_ge(s_x[t // (T // LOTS)], 16)
                last = nc.vector.bn_stats(st[:, t, :], g.X[:, t, :])
            last.then_inc(s_mv, 1)
            dve.wait_ge(s_mv, 1)
            for t in range(T):
                last = nc.vector.bn_aggr(g.mv[:, t, :], st[:, t, :])
            last.then_inc(s_v, 1)
            dve.wait_ge(s_v, 4)
            nc.vector.tensor_scalar_add(g.sd[:, 1, :], g.mv[:, :, 1], EPS).then_inc(s_mv, 1)
            dve.wait_ge(s_mod, B - 1)
            nc.vector.tensor_copy(g.mod[:, 0:B - 1, :, :].rearrange("p b j d -> p (b j d)"), psm[0][:]).then_inc(s_ev_dve, 1)
            dve.wait_ge(s_ev_dve, 1)
            dve.wait_ge(s_ev_act, 1)
            for j in (1, 4):
                nc.vector.tensor_scalar_add(g.mod[:, :, j, :], g.mod[:, :, j, :], 1.0)
            n = 4
            for j in (2, 5):
                gate = g.mod[:, :, j, :]
                nc.vector.scalar_tensor_tensor(mag[:], gate, -1.0, gate, ALU.mult, ALU.max).then_inc(s_v, 1)
                dve.wait_ge(s_v, n + 1)
                nc.vector.tensor_scalar_max(mag[:], mag[:], 0.25).then_inc(s_v, 1)
                nc.vector.tensor_scalar(gate, gate, 0.0, 2.0, ALU.is_ge, ALU.mult).then_inc(s_v, 1)
                dve.wait_ge(s_v, n + 3)
                nc.vector.scalar_tensor_tensor(gate, gate, -1.0, mag[:], ALU.add, ALU.mult).then_inc(s_v, 1)
                dve.wait_ge(s_v, n + 4)
                n += 4
            inverse_deviation(nc, dve, g, s_sd, s_v, n)

        @block.tensor
        def _(pe):
            pe.wait_ge(s_cb, 1)
            pe.wait_ge(s_w, 16)
            for b in range(B):
                for j in range(3):
                    for k in range(KD):
                        last = nc.tensor.matmul(psm[b][:, j * 512:(j + 1) * 512], cb[:, k, b, :],
                                                wmod[:, k, j * 512:(j + 1) * 512], start=k == 0, stop=k == KD - 1)
                last.then_inc(s_mod, 1)


def inverse_deviation(nc, dve, g, s_sd, s_v, n):
    dve.wait_ge(s_sd, 1)
    nc.vector.reciprocal(g.sd[:, 2, :], g.sd[:, 0, :]).then_inc(s_v, 1)
    dve.wait_ge(s_v, n + 1)
    nc.vector.tensor_mul(g.sd[:, 2, :], g.sd[:, 2, :], g.sd[:, 1, :]).then_inc(s_v, 1)
    dve.wait_ge(s_v, n + 2)
    nc.vector.tensor_add(g.sd[:, 2, :], g.sd[:, 2, :], g.sd[:, 0, :]).then_inc(s_v, 1)
    dve.wait_ge(s_v, n + 3)
    nc.vector.tensor_scalar_mul(g.sd[:, 2, :], g.sd[:, 2, :], 0.5).then_inc(s_v, 1)
    dve.wait_ge(s_v, n + 4)
    nc.vector.reciprocal(g.rs[:], g.sd[:, 2, :]).then_inc(s_v, 1)
    dve.wait_ge(s_v, n + 5)


def qkv_stage(nc, g):
    with ExitStack() as ctx:
        sem = open_sem(ctx, nc, "qkv")
        sb, ps = open_mem(ctx, nc, "qkv")
        wq, qb, tab, zero = g.wq, g.qb, g.tab, g.zero
        hn = sb("hn", [P, 3, D])
        hm = sb("hm", [P, 3, D])
        hT = sb("hT", [P, 2, KD, P])
        qk = sb("qk", [P, 2, 2 * D])
        rc = sb("rc", [P, 2, 2 * D])
        rw = sb("rw", [P, 2, 2 * D])
        rq = sb("rq", [P, 2, 2 * D])
        hi = [sb(f"hi{i}", [P, 4, CH], F32R) for i in range(2)]
        lo = [sb(f"lo{i}", [P, 4, CH], F32R) for i in range(2)]
        pst = [ps(f"pst{i}", [P, KD, P]) for i in range(2)]
        psq = [ps(f"psq{i}", [P, 1024]) for i in range(2)]
        psr = [ps(f"psr{i}", [P, 4, P]) for i in range(2)]
        names = "s_fill s_hn s_hm s_tr s_hT s_q s_qb s_vb s_rc s_rw s_rq s_rt s_hi s_lo s_put0 s_put1 s_tick"
        (s_fill, s_hn, s_hm, s_tr, s_hT, s_q, s_qb, s_vb, s_rc, s_rw, s_rq, s_rt, s_hi, s_lo,
         s_put0, s_put1, s_tick) = [sem(n) for n in names.split()]
        s_put = [s_put0, s_put1]
        PUT = 16 * 8
        block = ctx.enter_context(nc.Block())


        @block.sync
        def _(sp):
            rows = 2048 // D
            left = g.hs.shape[0] // P - (g.hs.shape[0] // P // rows) * rows
            full = g.hs.shape[0] // P // rows
            hs = g.hs[0:full * rows * P, :].rearrange("(n p r) d -> n p (r d)", r=rows, p=P) if full else None
            for n in range(full):
                sp.dma_start(hs[n], zero[:]).then_inc(s_fill, 16)
            if left:
                sp.dma_start(g.hs[full * rows * P:, :].rearrange("(p r) d -> p (r d)", r=left, p=P),
                             zero[:, 0:left * D]).then_inc(s_fill, 16)
            for c in range(2):
                sp.sem_inc(s_put[c], 16)
            for b in range(B):
                for c in range(CHUNKS):
                    for cut in range(2):
                        sp.wait_ge(s_lo, TB * b + 4 * c + 2 * cut + 2 + AHEAD)
                        at, n0 = cut * CH // 2, c * CH + cut * CH // 2
                        for part, buf in enumerate((hi, lo)):
                            dst = g.qkT[part].rearrange("q (b f p) n -> q b f p n", b=B, p=P)
                            for q in range(2):
                                sp.dma_start(dst[q, b, :, :, n0:n0 + CH // 2].rearrange("f p n -> p f n"),
                                             buf[c % 2][:, 2 * q:2 * q + 2, at:at + CH // 2].bitcast(F32)
                                             ).then_inc(s_put[c % 2], 16)
                if b == 0:
                    for c in range(2):
                        sp.wait_ge(s_put[c], PUT * CHUNKS // 2 + 16)
                    load_keys(sp, g, 0, 0)
                    load_queries(sp, g, 0, 0, 0)
                    load_queries(sp, g, 1, 0, 1)
                    load_keys(sp, g, 1, 1)
            for c in range(2):
                sp.wait_ge(s_put[c], PUT * B * CHUNKS // 2 + 16)
            sp.wait_ge(s_fill, 16 * (full + (1 if left else 0)))
            for i in range(2):
                sp.wait_ge(g.keys_in[i], 96)
                sp.wait_ge(g.queries_in[i], 96)

        @block.gpsimd
        def _(pool):
            with pool.Fori(0, B) as b:
                def modulate(r):
                    t = TB * b + r
                    pool.wait_ge(s_hn, t + 1)
                    if r >= 3:
                        pool.wait_ge(s_tr, t - 2)
                    pool.sem_inc(s_tick)
                    nc.gpsimd.tensor_mul(hm[:, r % 3, :], hn[:, r % 3, :], g.mod[:, bass.ds(b, 1), 1, :].rearrange("p o d -> p (o d)")).then_inc(s_hm, 1)
                    pool.wait_ge(s_hm, 2 * t + 1)
                    pool.sem_inc(s_tick)
                    nc.gpsimd.tensor_add(hm[:, r % 3, :], hm[:, r % 3, :], g.mod[:, bass.ds(b, 1), 0, :].rearrange("p o d -> p (o d)")).then_inc(s_hm, 1)

                def swapped(r):
                    t = TB * b + r
                    pool.wait_ge(s_qb, t + 1)
                    if r >= 2:
                        pool.wait_ge(s_rq, t - 1)
                    src = qk[:, r % 2, :].rearrange("p (h i e) -> p h i e", h=2 * H, e=2)
                    dst = rw[:, r % 2, :].rearrange("p (h i e) -> p h i e", h=2 * H, e=2)
                    sn = tab[:, 1, r:r + 1, :].rearrange("p o (i e) -> p o i e", e=2)
                    pool.sem_inc(s_tick)
                    for e in range(2):
                        last = nc.gpsimd.tensor_mul(dst[:, :, :, e], src[:, :, :, 1 - e],
                                                    sn[:, :, :, e].to_broadcast([P, 2 * H, HD // 2]))
                    last.then_inc(s_rw, 1)

                modulate(0)
                for k in range(TB + 2):
                    if k + 1 < TB:
                        modulate(k + 1)
                    if k >= 2:
                        swapped(k - 2)

        @block.scalar
        def _(act):
            with act.Fori(0, B) as b:
                for k in range(TB + 3):
                    if k < TB:
                        t = TB * b + k
                        act.wait_ge(s_tr, t + 1)
                        if k >= 2:
                            act.wait_ge(s_q, t - 1)
                        nc.scalar.copy(hT[:, k % 2, :, :], pst[k % 2][:]).then_inc(s_hT, 1)
                    if k >= 3:
                        r = k - 3
                        c, o = r // 4 % 2, (r % 4) * P
                        act.wait_ge(s_rt, TB * b + r + 1)
                        if r % 4 == 0:
                            act.wait_ge(s_put[c], PUT * (2 * b + r // 8) + 16)
                        nc.scalar.mul(hi[c][:, 0:2, o:o + P], psr[r % 2][:, 0:2, :], SCALE)
                        nc.scalar.copy(hi[c][:, 2:4, o:o + P], psr[r % 2][:, 2:4, :]).then_inc(s_hi, 1)

        @block.vector
        def _(dve):
            dve.sem_inc(s_lo, AHEAD)
            with dve.Fori(0, B) as b:
                def normalise(r):
                    t = TB * b + r
                    if r >= 3:
                        dve.wait_ge(s_hm, 2 * t - 4)
                    nc.vector.tensor_scalar(hn[:, r % 3, :], g.X[:, bass.ds(t, 1), :].rearrange("p o d -> p (o d)"),
                                            g.mv[:, bass.ds(t, 1), 0], g.rs[:, bass.ds(t, 1)],
                                            ALU.subtract, ALU.mult).then_inc(s_hn, 1)

                def add_bias(r):
                    t = TB * b + r
                    dve.wait_ge(s_q, t + 1)
                    if r >= 2:
                        dve.wait_ge(s_rw, t - 1)
                    nc.vector.tensor_add(qk[:, r % 2, :], psq[r % 2][:, 0:2 * D], qb[:, 0:2 * D]).then_inc(s_qb, 1)
                    v = g.V[:].rearrange("p (b h) t e -> p b h t e", b=B)
                    nc.vector.tensor_add(
                        v[:, bass.ds(b, 1), :, r:r + 1, :].rearrange("p o h u e -> p (o h u) e"),
                        psq[r % 2][:, 2 * D:3 * D].rearrange("p (h e) -> p h e", h=PAIRS),
                        qb[:, 2 * D:3 * D].rearrange("p (h e) -> p h e", h=PAIRS)).then_inc(s_vb, 1)

                def times_cos(r):
                    t = TB * b + r
                    src = qk[:, r % 2, :].rearrange("p (h e) -> p h e", h=2 * H)
                    dve.wait_ge(s_qb, t + 1)
                    nc.vector.tensor_mul(rc[:, r % 2, :].rearrange("p (h e) -> p h e", h=2 * H), src,
                                         tab[:, 0, r:r + 1, :].to_broadcast([P, 2 * H, HD])).then_inc(s_rc, 1)

                def add_swapped(r):
                    t = TB * b + r
                    dve.wait_ge(s_rc, t + 1)
                    dve.wait_ge(s_rw, t + 1)
                    if r >= 2:
                        dve.wait_ge(s_rt, t - 1)
                    nc.vector.tensor_add(rq[:, r % 2, :], rc[:, r % 2, :], rw[:, r % 2, :]).then_inc(s_rq, 1)

                def low_part(r):
                    t = TB * b + r
                    c, o = r // 4 % 2, (r % 4) * P
                    dve.wait_ge(s_hi, t + 1)
                    if r % 4 == 0:
                        dve.wait_ge(s_put[c], PUT * (2 * b + r // 8) + 16)
                    for q, scale in ((0, SCALE), (1, 1.0)):
                        last = nc.vector.scalar_tensor_tensor(
                            lo[c][:, 2 * q:2 * q + 2, o:o + P], psr[r % 2][:, 2 * q:2 * q + 2, :], scale,
                            hi[c][:, 2 * q:2 * q + 2, o:o + P].bitcast(F32), ALU.mult, ALU.subtract)
                    last.then_inc(s_lo, 1)

                normalise(0)
                for k in range(TB + 4):
                    if k + 1 < TB:
                        normalise(k + 1)
                    if 3 <= k <= TB + 2:
                        add_swapped(k - 3)
                    if 2 <= k <= TB + 1:
                        add_bias(k - 2)
                        times_cos(k - 2)
                    if k >= 4:
                        low_part(k - 4)

        @block.tensor
        def _(pe):
            with pe.Fori(0, B) as b:
                def tiles_in(r):
                    t = TB * b + r
                    pe.wait_ge(s_hm, 2 * t + 2)
                    if r >= 2:
                        pe.wait_ge(s_hT, t - 1)
                    for k in range(KD):
                        last = nc.tensor.transpose(pst[r % 2][:, k, :], hm[:, r % 3, k * P:(k + 1) * P], g.ident[:])
                    last.then_inc(s_tr, 1)

                def project(r):
                    t = TB * b + r
                    pe.wait_ge(s_hT, t + 1)
                    if r >= 2:
                        pe.wait_ge(s_vb, t - 1)
                    for n0, n1 in ((0, 512), (512, QKV)):
                        for k in range(KD):
                            last = nc.tensor.matmul(psq[r % 2][:, n0:n1], hT[:, r % 2, k, :], wq[:, k, n0:n1],
                                                    start=k == 0, stop=k == KD - 1)
                    last.then_inc(s_q, 1)

                def tiles_out(r):
                    t = TB * b + r
                    pe.wait_ge(s_rq, t + 1)
                    pe.wait_ge(s_lo, t - 1 + AHEAD if r >= 2 else t - r + AHEAD)
                    for k in range(4):
                        last = nc.tensor.transpose(psr[r % 2][:, k, :], rq[:, r % 2, k * P:(k + 1) * P], g.ident[:])
                    last.then_inc(s_rt, 1)

                for k in range(TB + 3):
                    if k < TB:
                        tiles_in(k)
                    if 1 <= k <= TB:
                        project(k - 1)
                    if k >= 3:
                        tiles_out(k - 3)


def rows_of(g, part, which, first, cols):
    return g.qkT[part][which, bass.ds(first, HD), cols]


def load_keys(eng, g, i, unit):
    for hh in range(2):
        for at, part in ((0, 0), (16, 1), (34, 0)):
            eng.dma_start(g.K[i][64 * hh + at:64 * hh + at + HD, :].bitcast(F32),
                          rows_of(g, part, 1, unit * 2 * HD + HD * hh, slice(0, N))).then_inc(g.keys_in[i], 16)


def load_queries(eng, g, i, unit, c):
    for hh in range(2):
        for at, part in ((0, 0), (16, 0), (34, 1)):
            eng.dma_start(g.QM[i][64 * hh + at:64 * hh + at + HD, hh, :].bitcast(F32),
                          rows_of(g, part, 0, unit * 2 * HD + HD * hh, slice(c * CH, (c + 1) * CH))
                          ).then_inc(g.queries_in[i], 16)


def attention(nc, g):
    KT = N // P
    GROUPS = KT // 2
    OVER = 2
    EARLY = 3
    SLOTS = 8
    BODY = GROUP
    ITERS = STEPS // BODY
    VW = 32
    WIDTH = HD + 1
    BANKS = 3
    EACH = 2 * KT
    USED = 64 + ROWS
    with ExitStack() as ctx:
        sem = open_sem(ctx, nc, "att")
        sb, ps = open_mem(ctx, nc, "att")
        K, QM = g.K, g.QM
        keys_in, queries_in = g.keys_in, g.queries_in
        QE = [sb(f"QE{i}", [P, 2, CH], F32R) for i in range(2)]
        VU = [sb(f"VU{i}", [P, KT, 2, VW]) for i in range(2)]
        probs = sb("probs", [P, SLOTS, 2 * CH])
        mx = sb("mx", [P, 2, 8, 4])
        m8 = sb("m8", [P, 8])
        mh = sb("mh", [P, 8], F32R)
        mt = sb("mt", [P, 4, P], F32R)
        identity = sb("identity", [P, P], F32R)
        sums = sb("sums", [P, CH])
        sel = sb("sel", [P, 2, WIDTH])
        bias = sb("bias", [P, D])
        gated = sb("gated", [P, B, D])
        PS = [ps(f"PS{i}", [P, CH]) for i in range(BANKS)]
        PM = [ps(f"PM{i}", [P, CH]) for i in range(BANKS)]
        PV = ps("PV", [P, CH])
        MISC = ps("MISC", [P, CH])

        queries_moved = sem("queries_moved")
        buffers_set = sem("buffers_set")
        sel_set = sem("sel_set")
        values_in = sem("values_in")
        max_products = sem("max_products")
        maxima = sem("maxima")
        row_maxima = sem("row_maxima")
        split = sem("split")
        shifts_ready = sem("shifts_ready")
        shifts_turned = sem("shifts_turned")
        shifts_placed = sem("shifts_placed")
        scores = sem("scores")
        exps = sem("exps")
        pv_groups = sem("pv_groups")
        sums_out = sem("sums_out")
        gathered = sem("gathered")
        outputs = sem("outputs")
        bias_in, weights_in = sem("bias_in"), sem("weights_in")
        bias_gated = sem("bias_gated")
        inverted = sem("inverted")
        tick, tick_sp, tick_act, tick_dve = sem("tick"), sem("tick_sp"), sem("tick_act"), sem("tick_dve")
        block = ctx.enter_context(nc.Block())

        def last_user(n, i):
            return n - (BANKS if i >= BANKS - 1 else BANKS - 1) + 1

        def steps_done(n):
            return GROUPS * n + SLOTS // 2

        def over_iterations(eng, body):
            with eng.Fori(0, ITERS - 1) as it:
                body(it, False)
            body(ITERS - 1, True)

        def over_steps(eng, step):
            step(0, 0, False)
            with eng.Fori(0, ITERS - 1) as it:
                for r in range(1, BODY + 1):
                    step(it, r, False)
            for r in range(1, BODY):
                step(ITERS - 1, r, True)

        @block.sync
        def _(sp):
            def hold(semaphore, value):
                sp.wait_ge(semaphore, value)
                sp.sem_inc(tick_sp)

            def move_queries(i):
                sp.dma_start(QE[i][:].bitcast(F32), QM[i][:].bitcast(F32)).then_inc(queries_moved, 16)

            sp.dma_start(bias[:], g.proj_b.partition_broadcast(P)).then_inc(bias_in, 16)
            sp.dma_start(g.wp[:], g.wpT.rearrange("(k p) n -> p k n", p=P)).then_inc(weights_in, 16)
            hold(queries_in[0], 96)
            move_queries(0)
            hold(queries_moved, 16)
            hold(max_products, 32)
            load_queries(sp, g, 0, 0, 2)

            def body(it, last):
                for r in range(BODY):
                    s = BODY * it + r
                    if r % CHUNKS == 1 and not (last or r < CHUNKS):
                        hold(pv_groups, steps_done(s - 1))
                        load_keys(sp, g, 0, 2 * it + 2)
                    if not (last and r == BODY - 1):
                        n = (r + 1) // 2
                        hold(queries_in[(r + 1) % 2], 96 * (4 * it + n + 1))
                        hold(pv_groups, steps_done(s))
                        move_queries((r + 1) % 2)
                    if not (last and r >= BODY - 3):
                        hold(max_products, 32 * (s + 2))
                        hold(queries_moved, 16 * (s + 2))
                        n = r + 3
                        load_queries(sp, g, (r + 1) % 2, 2 * it + n // CHUNKS, n % CHUNKS)
                if not last:
                    hold(pv_groups, steps_done(BODY * it + BODY))
                    load_keys(sp, g, 1, 2 * it + 3)

            over_iterations(sp, body)
            sp.wait_ge(weights_in, 16)

        @block.gpsimd
        def _(pool):
            for i in range(2):
                nc.gpsimd.memset(VU[i][:], 0.0).then_inc(buffers_set, 1)
            nc.gpsimd.memset(mt[:].bitcast(F32), 0.0).then_inc(buffers_set, 1)
            nc.gpsimd.memset(sel[:], 0.0).then_inc(buffers_set, 1)
            pool.wait_ge(buffers_set, 4)
            nc.gpsimd.tensor_copy(identity[:], g.ident[:]).then_inc(sel_set, 1)
            for i in range(2):
                nc.gpsimd.memset(VU[i][:, :, :, HD:WIDTH], 1.0).then_inc(sel_set, 1)
            for hh in range(2):
                for par in range(2):
                    nc.gpsimd.affine_select(out=sel[:, hh, :], in_=sel[:, hh, :], compare_op=ALU.not_equal, fill=1.0,
                                            base=-32 * (2 * hh + par), pattern=[[-1, WIDTH]],
                                            channel_multiplier=1).then_inc(sel_set, 1)
                    pool.wait_ge(sel_set, 4 + 2 * hh + par)

            def load_values(i, unit):
                nc.gpsimd.tensor_copy(VU[i][:, :, :, 0:HD],
                                      g.V[:, bass.ds(unit, 1), :, :].rearrange("p o t (h e) -> p (o t) h e", h=2)
                                      ).then_inc(values_in, 1)

            load_values(0, 0)
            load_values(1, 1)

            def load_next(it, i):
                pool.wait_ge(pv_groups, steps_done(BODY * it + CHUNKS * (i + 1)))
                pool.sem_inc(tick)
                load_values(i, 2 * it + 2 + i)

            def shifts(s):
                pool.wait_ge(row_maxima, s + 1)
                if not (isinstance(s, int) and s == 0):
                    pool.wait_ge(shifts_turned, s)
                pool.sem_inc(tick)
                nc.gpsimd.tensor_copy(mh[:], m8[:]).then_inc(split, 1)
                pool.wait_ge(split, s + 1)
                pool.sem_inc(tick)
                cols = mt[:].rearrange("p q (h c) -> p q h c", h=2)
                m = m8[:].rearrange("p (q h) -> p q h", h=2)
                top = mh[:].bitcast(F32).rearrange("p (q h) -> p q h", h=2)
                nc.gpsimd.tensor_copy(cols[:, :, :, 32], top)
                nc.gpsimd.tensor_tensor(cols[:, :, :, 33], m, top, ALU.subtract).then_inc(shifts_ready, 1)

            shifts(0)

            def divide(it, i):
                unit = 2 * it + i
                o = g.O[:, bass.ds(unit, 1), :, :].rearrange("p o t (c e) -> p (o t) c e", c=2)
                pool.wait_ge(inverted, unit + 1)
                pool.sem_inc(tick)
                nc.gpsimd.tensor_mul(o[:, :, :, 0:HD], o[:, :, :, 0:HD],
                                     o[:, :, :, HD:WIDTH].to_broadcast([P, TB, 2, HD]))

            def step(it, r, last):
                s = BODY * it + r
                if r == BODY:
                    load_next(it, 1)
                if not (last and r == BODY - 1):
                    shifts(s + 1)
                if r == CHUNKS and not last:
                    load_next(it, 0)
                if r == CHUNKS + 1:
                    divide(it, 0)
                if r == BODY:
                    divide(it, 1)

            over_steps(pool, step)
            pool.wait_ge(bias_in, 16)
            for b in range(B):
                nc.gpsimd.tensor_mul(gated[:, b, :], bias[:], g.mod[:, b, 2, :]).then_inc(bias_gated, 1)
            pool.wait_ge(bias_gated, B)
            for b in range(B):
                x = g.X[:, b * TB:(b + 1) * TB, :]
                nc.gpsimd.tensor_add(x, x, gated[:, b:b + 1, :].to_broadcast([P, TB, D]))
            divide(ITERS - 1, 1)

        @block.tensor
        def _(pe):
            def score_product(s, r, i):
                kt, hh = i // 2, i % 2
                pe.wait_ge(exps, last_user(EACH * s + i, i) + AHEAD)
                nc.tensor.matmul(PS[i % BANKS][:], K[r % BODY // CHUNKS][0:USED, kt * P:(kt + 1) * P],
                                 QE[r % 2][0:USED, hh, :], start=True, stop=True).then_inc(scores, 1)

            def max_product(s, r, it, i):
                qt, kc, hh, u = i // 8, i // 2 % 4, i % 2, (r % BODY) // CHUNKS
                if i == 0:
                    pe.wait_ge(queries_in[r % 2], 96 * (4 * it + r // 2 + 1))
                    if r % CHUNKS == 0:
                        pe.wait_ge(keys_in[u], 96 * (it + r // BODY + 1))
                pe.wait_ge(maxima, last_user(EACH * s + i, i) + AHEAD)
                nc.tensor.matmul(PM[i % BANKS][:], QM[r % 2][0:USED, hh, qt * P:(qt + 1) * P],
                                 K[u][0:USED, kc * CH:(kc + 1) * CH], start=True, stop=True
                                 ).then_inc(max_products, 1)

            def turn_shifts(s):
                pe.wait_ge(shifts_ready, s + 1)
                pe.wait_ge(outputs, s if not isinstance(s, int) else max(s, 1))
                for qt in range(4):
                    last = nc.tensor.matmul(MISC[:, qt * P:(qt + 1) * P], mt[:, qt, :], identity[:],
                                            start=True, stop=True)
                last.then_inc(shifts_turned, 1)

            def value_products(s, r, it, j):
                pe.wait_ge(exps, EACH * s + 4 * j + 4 + AHEAD)
                if j == 0:
                    pe.wait_ge(sums_out, s + 1)
                    pe.wait_ge(values_in, 2 * it + r // CHUNKS + 1)
                for hh in range(2):
                    for par in range(2):
                        kt, quad = 2 * j + par, 2 * hh + par
                        last = nc.tensor.matmul(PV[32 * quad:32 * quad + VW, :], VU[r // CHUNKS % 2][:, kt, hh, :],
                                                probs[:, kt % SLOTS, hh * CH:(hh + 1) * CH],
                                                start=j == 0, stop=j == GROUPS - 1, tile_position=(0, 32 * quad))
                last.then_inc(pv_groups, 1)

            def gather_ready(s):
                pe.wait_ge(sums_out, s + 2)
                pe.wait_ge(outputs, s + 1)
                if not (isinstance(s, int) and s == STEPS - 1):
                    pe.wait_ge(shifts_placed, 2 * s + 4)

            def gather(qt):
                nc.tensor.matmul(MISC[:, qt * 2 * WIDTH:(qt + 1) * 2 * WIDTH], sums[:, qt * P:(qt + 1) * P],
                                 sel[:].rearrange("p h e -> p (h e)"), start=True, stop=True).then_inc(gathered, 1)

            pe.sem_inc(pv_groups, SLOTS // 2)
            pe.sem_inc(gathered, 1)
            for i in range(EACH):
                max_product(0, 0, 0, i)
            pe.wait_ge(sel_set, 7)
            turn_shifts(0)
            for i in range(4 * EARLY):
                max_product(1, 1, 0, i)
            pe.wait_ge(shifts_placed, 2)
            for i in range(4):
                score_product(0, 0, i)

            def step(it, r, last):
                s = BODY * it + r
                final = last and r == BODY - 1
                for j in range(GROUPS):
                    for h in range(4):
                        if j < GROUPS - EARLY:
                            if not final:
                                max_product(s + 1, r + 1, it, 4 * (j + EARLY) + h)
                        elif not (last and r >= BODY - 2):
                            max_product(s + 2, r + 2, it, 4 * (j - GROUPS + EARLY) + h)
                        if j < GROUPS - 1:
                            score_product(s, r, 4 * (j + 1) + h)
                        elif not final:
                            if h == 0:
                                pe.wait_ge(shifts_placed, 2 * s + 4)
                            score_product(s + 1, r + 1, h)
                    if j == GROUPS - EARLY and not final:
                        turn_shifts(s + 1)
                    if j == 2 and r > 0:
                        gather_ready(s - 1)
                        for qt in range(4):
                            gather(qt)
                    value_products(s, r, it, j)

            over_steps(pe, step)
            gather_ready(STEPS - 1)
            for qt in range(4):
                gather(qt)

        @block.scalar
        def _(act):
            def place_shifts(s, r):
                act.wait_ge(queries_moved, 16 * (s + 1))
                act.wait_ge(shifts_turned, s + 1)
                nc.scalar.copy(QE[r % 2][32:34, 0, :], MISC[32:34, :]).then_inc(shifts_placed, 1)

            def keep_outputs(s, it, r):
                act.wait_ge(gathered, 4 * s + 5)
                act.sem_inc(tick_act)
                t0 = CH // P * (r % CHUNKS)
                nc.scalar.copy(g.O[:, bass.ds(2 * it + r // CHUNKS, 1), t0:t0 + 4, :].rearrange("p o t e -> p (o t) e"),
                               MISC[:, 0:8 * WIDTH].rearrange("p (t e) -> p t e", t=4)).then_inc(outputs, 1)

            def exp_tile(s, kt):
                if kt % 2 == 0:
                    act.wait_ge(pv_groups, GROUPS * s + kt // 2 + 1)
                for hh in range(2):
                    i = 2 * kt + hh
                    act.wait_ge(scores, EACH * s + i + 1)
                    nc.scalar.activation(probs[:, kt % SLOTS, hh * CH:(hh + 1) * CH], PS[i % BANKS][:], ACT.Exp
                                         ).then_inc(exps, 1)

            act.sem_inc(exps, AHEAD)
            act.sem_inc(sums_out, 1)
            act.sem_inc(outputs, 1)
            place_shifts(0, 0)
            for kt in range(OVER):
                exp_tile(0, kt)

            def step(it, r, last):
                s = BODY * it + r
                final = last and r == BODY - 1
                for kt in range(OVER, KT):
                    if kt == 8 and r > 0:
                        keep_outputs(s - 1, it, r - 1)
                    if kt == KT - 2 * EARLY + 3 and not final:
                        place_shifts(s + 1, r + 1)
                    exp_tile(s, kt)
                if not final:
                    for kt in range(OVER):
                        exp_tile(s + 1, kt)
                act.wait_ge(pv_groups, steps_done(s + 1))
                act.wait_ge(gathered, 4 * s + 1)
                nc.scalar.copy(sums[:], PV[:]).then_inc(sums_out, 1)

            over_steps(act, step)
            keep_outputs(STEPS - 1, ITERS - 1, BODY - 1)

        @block.vector
        def _(dve):
            def max_group(s, r, grp):
                for i in range(4 * grp, 4 * grp + 4):
                    qt, kc, hh = i // 8, i // 2 % 4, i % 2
                    dve.wait_ge(max_products, EACH * s + i + 1)
                    nc.vector.reduce_max(mx[:, r % 2, 2 * qt + hh, kc:kc + 1], PM[i % BANKS][:], AX).then_inc(maxima, 1)

            def row_maximum(s, r):
                if not (isinstance(s, int) and s == 0):
                    dve.wait_ge(shifts_ready, s)
                dve.wait_ge(maxima, EACH * (s + 1) + AHEAD)
                nc.vector.reduce_max(m8[:], mx[:, r % 2, :, :], AX).then_inc(row_maxima, 1)

            def place_second(s, r):
                dve.wait_ge(shifts_placed, 2 * s + 1)
                nc.vector.tensor_copy(QE[r % 2][96:98, 1, :], MISC[96:98, :]).then_inc(shifts_placed, 1)

            dve.sem_inc(maxima, AHEAD)
            for grp in range(GROUPS):
                max_group(0, 0, grp)
            row_maximum(0, 0)
            place_second(0, 0)
            for grp in range(EARLY):
                max_group(1, 1, grp)

            def invert(it, i):
                unit = 2 * it + i
                den = g.O[:, bass.ds(unit, 1), :, :].rearrange("p o t (c e) -> p (o t) c e", c=2)[:, :, :, HD:WIDTH]
                dve.wait_ge(outputs, CHUNKS * (unit + 1) + 1)
                dve.sem_inc(tick_dve)
                nc.vector.reciprocal(den, den).then_inc(inverted, 1)

            def step(it, r, last):
                s = BODY * it + r
                final = last and r == BODY - 1
                for j in range(GROUPS):
                    if j < GROUPS - EARLY:
                        if not final:
                            max_group(s + 1, r + 1, j + EARLY)
                            if j == GROUPS - EARLY - 1:
                                row_maximum(s + 1, r + 1)
                    elif not (last and r >= BODY - 2):
                        max_group(s + 2, r + 2, j - GROUPS + EARLY)
                    if j == GROUPS - EARLY and not final:
                        place_second(s + 1, r + 1)
                if r in (CHUNKS, BODY):
                    invert(it, r // CHUNKS - 1)

            over_steps(dve, step)
            invert(ITERS - 1, 1)



def projection(nc, g):
    with ExitStack() as ctx:
        sem = open_sem(ctx, nc, "proj")
        sb, ps = open_mem(ctx, nc, "proj")
        oc = sb("oc", [P, 2, D])
        oT = sb("oT", [P, 2, KD, P])
        yg = sb("yg", [P, 3, D])
        st = sb("st2", [P, T, 6])
        pst = [ps(f"pst{i}", [P, KD, P]) for i in range(2)]
        psy = [ps(f"psy{i}", [P, CH]) for i in range(2)]
        (s_oc, s_tr, s_oT, s_prod, s_yg, s_x, s_st, s_tick) = [
            sem(n) for n in "s_oc s_tr s_oT s_prod s_yg s_x s_st s_tick".split()]
        block = ctx.enter_context(nc.Block())


        @block.scalar
        def _(act):
            with act.Fori(0, B) as b:
                def together(r):
                    t = TB * b + r
                    if r >= 2:
                        act.wait_ge(s_tr, t - 1)
                    act.sem_inc(s_tick)
                    o = g.O[:].rearrange("p (b h) t (c e) -> p b h t c e", b=B, c=2)
                    nc.scalar.copy(oc[:, r % 2, :].rearrange("p (h c e) -> p h c e", h=PAIRS, c=2),
                                   o[:, bass.ds(b, 1), :, r:r + 1, :, 0:HD].rearrange("p o h u c e -> p (o h u) c e")
                                   ).then_inc(s_oc, 1)

                def turned(r):
                    t = TB * b + r
                    act.wait_ge(s_tr, t + 1)
                    if r >= 2:
                        act.wait_ge(s_prod, t - 1)
                    nc.scalar.copy(oT[:, r % 2, :, :], pst[r % 2][:]).then_inc(s_oT, 1)

                together(0)
                for k in range(TB):
                    if k + 1 < TB:
                        together(k + 1)
                    turned(k)

        @block.vector
        def _(dve):
            with dve.Fori(0, B) as b:
                def gate(r):
                    t = TB * b + r
                    dve.wait_ge(s_prod, t + 1)
                    if r >= 3:
                        dve.wait_ge(s_x, t - 2)
                    nc.vector.tensor_mul(yg[:, r % 3, :], psy[r % 2][:, 0:D],
                                         g.mod[:, bass.ds(b, 1), 2, :].rearrange("p o d -> p (o d)")).then_inc(s_yg, 1)

                def residual(r):
                    t = TB * b + r
                    x = g.X[:, bass.ds(t, 1), :].rearrange("p o d -> p (o d)")
                    dve.wait_ge(s_yg, t + 1)
                    nc.vector.tensor_add(x, x, yg[:, r % 3, :]).then_inc(s_x, 1)

                def statistics(r):
                    t = TB * b + r
                    dve.wait_ge(s_x, t + 1)
                    dve.sem_inc(s_tick)
                    nc.vector.bn_stats(st[:, bass.ds(t, 1), :].rearrange("p o d -> p (o d)"),
                                       g.X[:, bass.ds(t, 1), :].rearrange("p o d -> p (o d)")).then_inc(s_st, 1)

                for k in range(TB + 2):
                    if k < TB:
                        gate(k)
                    if 1 <= k <= TB:
                        residual(k - 1)
                    if k >= 2:
                        statistics(k - 2)
            dve.wait_ge(s_st, T)
            for t in range(T):
                last = nc.vector.bn_aggr(g.mv[:, t, :], st[:, t, :])
            last.then_inc(s_st, 1)
            dve.wait_ge(s_st, T + 1)
            nc.vector.tensor_scalar_add(g.sd[:, 1, :], g.mv[:, :, 1], EPS).then_inc(s_st, 1)

        @block.tensor
        def _(pe):
            with pe.Fori(0, B) as b:
                def turn(r):
                    t = TB * b + r
                    pe.wait_ge(s_oc, t + 1)
                    if r >= 2:
                        pe.wait_ge(s_oT, t - 1)
                    for k in range(KD):
                        last = nc.tensor.transpose(pst[r % 2][:, k, :], oc[:, r % 2, k * P:(k + 1) * P], g.ident[:])
                    last.then_inc(s_tr, 1)

                def project(r):
                    t = TB * b + r
                    pe.wait_ge(s_oT, t + 1)
                    if r >= 2:
                        pe.wait_ge(s_yg, t - 1)
                    for k in range(KD):
                        last = nc.tensor.matmul(psy[r % 2][:, 0:D], oT[:, r % 2, k, :], g.wp[:, k, :],
                                                start=k == 0, stop=k == KD - 1)
                    last.then_inc(s_prod, 1)

                for k in range(TB + 1):
                    if k < TB:
                        turn(k)
                    if k:
                        project(k - 1)
                pe.wait_ge(s_yg, TB * b + TB)


def gate_stage(nc, g):
    with ExitStack() as ctx:
        sem = open_sem(ctx, nc, "gate")
        sb, ps = open_mem(ctx, nc, "gate")
        gw = sb("gw", [P, KD, E])
        bias = sb("bias", [P, 2, E])
        hs = sb("hs", [P, 3, D])
        hm = sb("hm", [P, 3, D])
        hT = sb("hT", [P, 2, KD, P])
        lg = sb("lg", [P, TB, E])
        pst = [ps(f"pst{i}", [P, KD, P]) for i in range(2)]
        psg = ps("psg", [P, TB, E])
        (s_par, s_sd, s_v, s_hs, s_hm, s_tr, s_hT, s_h2, s_prod, s_lg, s_out, s_tick) = [
            sem(n) for n in "s_par s_sd s_v s_hs s_hm s_tr s_hT s_h2 s_prod s_lg s_out s_tick".split()]
        block = ctx.enter_context(nc.Block())


        @block.sync
        def _(sp):
            sp.dma_start(gw[:], g.gwT.rearrange("(k p) n -> p k n", p=P)).then_inc(s_par, 16)
            sp.dma_start(bias[:, 0, :], g.gate_b.partition_broadcast(P)).then_inc(s_par, 16)
            sp.dma_start(bias[:, 1, :], g.expert_bias.partition_broadcast(P)).then_inc(s_par, 16)
            sp.wait_ge(s_par, 48)

        @block.scalar
        def _(act):
            nc.scalar.activation(g.sd[:, 0, :], g.sd[:, 1, :], ACT.Sqrt).then_inc(s_sd, 1)
            with act.Fori(0, B) as b:
                def keep(r):
                    t = TB * b + r
                    act.wait_ge(s_hm, t + 1)
                    act.sem_inc(s_tick)
                    nc.scalar.copy(g.H2[:, bass.ds(t, 1), :].rearrange("p o d -> p (o d)"), hm[:, r % 3, :]
                                   ).then_inc(s_h2, 1)

                def turned(r):
                    t = TB * b + r
                    act.wait_ge(s_tr, t + 1)
                    if r >= 2:
                        act.wait_ge(s_prod, t - 1)
                    nc.scalar.copy(hT[:, r % 2, :, :], pst[r % 2][:]).then_inc(s_hT, 1)

                for k in range(TB + 1):
                    if k < TB:
                        keep(k)
                    if k:
                        turned(k - 1)

        @block.vector
        def _(dve):
            inverse_deviation(nc, dve, g, s_sd, s_v, 0)
            dve.wait_ge(s_par, 48)
            with dve.Fori(0, B) as b:
                def vector_of(j):
                    return g.mod[:, bass.ds(b, 1), j, :].rearrange("p o d -> p (o d)")

                def scaled(r):
                    t = TB * b + r
                    if r >= 3:
                        dve.wait_ge(s_hm, t - 2)
                    nc.vector.scalar_tensor_tensor(hs[:, r % 3, :], g.X[:, bass.ds(t, 1), :].rearrange("p o d -> p (o d)"),
                                                   g.mv[:, bass.ds(t, 1), 0], vector_of(4),
                                                   ALU.subtract, ALU.mult).then_inc(s_hs, 1)

                def shifted(r):
                    t = TB * b + r
                    dve.wait_ge(s_hs, t + 1)
                    if r >= 3:
                        dve.wait_ge(s_h2, t - 2)
                        dve.wait_ge(s_tr, t - 2)
                    dve.sem_inc(s_tick)
                    nc.vector.scalar_tensor_tensor(hm[:, r % 3, :], hs[:, r % 3, :], g.rs[:, bass.ds(t, 1)], vector_of(3),
                                                   ALU.mult, ALU.add).then_inc(s_hm, 1)

                for k in range(TB + 1):
                    if k < TB:
                        scaled(k)
                    if k:
                        shifted(k - 1)
                dve.wait_ge(s_prod, TB * b + TB)
                nc.vector.tensor_add(lg[:], psg[:], bias[:, 0:1, :].to_broadcast([P, TB, E])).then_inc(s_lg, 1)
                dve.wait_ge(s_lg, b + 1)
                dve.sem_inc(s_tick)
                nc.vector.tensor_add(g.logits[:, bass.ds(TB * b, TB), :], lg[:], bias[:, 1:2, :].to_broadcast([P, TB, E])
                                     ).then_inc(s_out, 1)

        @block.tensor
        def _(pe):
            pe.wait_ge(s_par, 48)
            with pe.Fori(0, B) as b:
                def turn(r):
                    t = TB * b + r
                    pe.wait_ge(s_hm, t + 1)
                    if r >= 2:
                        pe.wait_ge(s_hT, t - 1)
                    for c in range(KD):
                        last = nc.tensor.transpose(pst[r % 2][:, c, :], hm[:, r % 3, c * P:(c + 1) * P], g.ident[:])
                    last.then_inc(s_tr, 1)

                def logits(r):
                    pe.wait_ge(s_hT, TB * b + r + 1)
                    for c in range(KD):
                        last = nc.tensor.matmul(psg[:, r, :], hT[:, r % 2, c, :], gw[:, c, :],
                                                start=c == 0, stop=c == KD - 1)
                    last.then_inc(s_prod, 1)

                for k in range(TB + 1):
                    if k < TB:
                        turn(k)
                    if k:
                        logits(k - 1)
                pe.wait_ge(s_lg, b + 1)


def routing(nc, g):
    KS = B * N // FT
    with ExitStack() as ctx:
        sem = open_sem(ctx, nc, "route")
        sb, ps = open_mem(ctx, nc, "route")
        row = sb("row", [P, g.row.shape[-1]])
        rev, first, number = row[:, 0:E], row[:, E:E + KS], row[:, E + KS:E + KS + NT]
        below = sb("below", [P, P])
        ones = sb("ones", [P, P])
        best = sb("best", [P, T])
        eq = sb("eq", [P, T, E])
        hot = sb("hot", [P, T, E])
        cnt = sb("cnt", [P, T, E])
        upto = sb("upto", [P, E, T])
        more = sb("more", [P, E, KS])
        tiles = sb("tiles", [P, E])
        end = sb("end", [P, E])
        start = sb("start", [P, E])
        place = sb("place", [P, T, E])
        slotf = sb("slotf", [P, T])
        past = sb("past", [P, NT, E])
        which = sb("which", [P, NT])
        psr = ps("psr", [P, CH])
        psc = ps("psc", [P, CH])
        s_par, s_set, s_v, s_hot, s_cnt = [sem(n) for n in "s_par s_set s_v s_hot s_cnt".split()]
        block = ctx.enter_context(nc.Block())

        @block.sync
        def _(sp):
            sp.dma_start(row[:], g.row.partition_broadcast(P)).then_inc(s_par, 16)
            sp.wait_ge(s_par, 16)

        @block.tensor
        def _(pe):
            pe.wait_ge(s_hot, 1)
            pe.wait_ge(s_set, 3)
            flat = hot[:].rearrange("p t e -> p (t e)")
            nc.tensor.matmul(psr[:, 0:T * E], below[:], flat, start=True, stop=True).then_inc(s_cnt, 1)
            nc.tensor.matmul(psc[:, 0:T * E], ones[:], flat, start=True, stop=True).then_inc(s_cnt, 1)

        @block.gpsimd
        def _(pool):
            nc.gpsimd.memset(ones[:], 1.0).then_inc(s_set, 1)
            nc.gpsimd.memset(below[:], 1.0).then_inc(s_set, 1)
            pool.wait_ge(s_set, 2)
            nc.gpsimd.affine_select(out=below[:], in_=below[:], compare_op=ALU.is_ge, fill=0.0, base=-1,
                                    pattern=[[1, P]], channel_multiplier=-1).then_inc(s_set, 1)

        @block.vector
        def _(dve):
            done = [0]

            def then(ins):
                done[0] += 1
                ins.then_inc(s_v, 1)
                dve.wait_ge(s_v, done[0])

            over_t = lambda a: a.unsqueeze(1).to_broadcast([P, T, E])
            over_e = lambda a: a.unsqueeze(2).to_broadcast([P, T, E])
            dve.wait_ge(s_par, 16)
            then(nc.vector.reduce_max(best[:], g.logits[:], AX))
            then(nc.vector.tensor_tensor(eq[:], g.logits[:], over_e(best[:]), ALU.is_equal))
            then(nc.vector.tensor_tensor(eq[:], eq[:], over_t(rev), ALU.mult))
            then(nc.vector.reduce_max(best[:], eq[:], AX))
            nc.vector.tensor_tensor(hot[:], over_t(rev), over_e(best[:]), ALU.is_equal).then_inc(s_hot, 1)
            dve.wait_ge(s_cnt, 2)
            then(nc.vector.tensor_copy(cnt[:], psc[:, 0:T * E].rearrange("p (t e) -> p t e", e=E)))
            dve.wait_ge(s_set, 1)
            for e in range(E):
                last = nc.vector.tensor_tensor_scan(upto[:, e, :], ones[:, 0:T], cnt[:, :, e], 0.0, ALU.mult, ALU.add)
            then(last)
            then(nc.vector.tensor_tensor(more[:], upto[:, :, T - 1:T].to_broadcast([P, E, KS]),
                                         first.unsqueeze(1).to_broadcast([P, E, KS]), ALU.is_gt))
            then(nc.vector.reduce_sum(tiles[:], more[:], AX))
            then(nc.vector.tensor_tensor_scan(end[:], ones[:, 0:E], tiles[:], 0.0, ALU.mult, ALU.add))
            then(nc.vector.tensor_sub(start[:], end[:], tiles[:]))
            then(nc.vector.tensor_scalar_mul(start[:], start[:], float(FT)))
            then(nc.vector.tensor_sub(place[:], upto[:].rearrange("p e t -> p t e"), cnt[:]))
            then(nc.vector.tensor_add(place[:], place[:], psr[:, 0:T * E].rearrange("p (t e) -> p t e", e=E)))
            then(nc.vector.tensor_add(place[:], place[:], over_t(start[:])))
            then(nc.vector.tensor_mul(place[:], place[:], hot[:]))
            then(nc.vector.reduce_sum(slotf[:], place[:], AX))
            nc.vector.tensor_copy(g.slot[:], slotf[:])
            then(nc.vector.tensor_tensor(past[:], end[:].unsqueeze(1).to_broadcast([P, NT, E]),
                                         number.unsqueeze(2).to_broadcast([P, NT, E]), ALU.is_le))
            then(nc.vector.reduce_sum(which[:], past[:], AX))
            then(nc.vector.tensor_scalar_min(which[:], which[:], float(E - 1)))
            nc.vector.tensor_copy(g.which[:], which[:]).then_inc(s_v, 1)


def experts(nc, g):
    SUB = FT // P
    PIECES = 2
    HPAIRS = KF // 2
    with ExitStack() as ctx:
        sem = open_sem(ctx, nc, "ffn")
        sb, ps = open_mem(ctx, nc, "ffn")
        w1 = sb("w1", [P, KD, F])
        w2 = sb("w2", [P, KF, D])
        late = [g.H2[:, i * KF:(i + 1) * KF, :].bitcast(F32R) for i in range(4)]
        w1_part = [[sb(f"w1_{part}", [P, KD, F], F32R) for part in ("hi", "lo")],
                   [a.rearrange("p (k x) d -> p k (x d)", k=KD) for a in late[0:2]]]
        w2_part = [[sb(f"w2_{part}", [P, KF, D], F32R) for part in ("hi", "lo")], late[2:4]]
        b1 = [sb(f"b1_{i}", [P, KF]) for i in range(2)]
        b2 = [sb(f"b2_{i}", [P, D]) for i in range(2)]
        rows = [sb(f"rows{i}", [P, SUB, D]) for i in range(2)]
        hT = [[sb(f"hT_{part}{i}", [P, KD, FT], F32R) for part in ("hi", "lo")] for i in range(2)]
        hid = sb("hid", [P, KF, FT])
        hid_part = [sb(f"hid_{part}", [P, KF, FT], F32R) for part in ("hi", "lo")]
        y = [sb(f"y{i}", [P, SUB, D]) for i in range(2)]
        pst = [ps(f"pst{i}", [P, KD, FT]) for i in range(2)]
        psh = [ps(f"psh{i}", [P, 2, FT]) for i in range(4)]
        psy = [ps(f"psy{i}", [P, SUB, D]) for i in range(2)]
        scattered = sem("scattered")
        in_w1, in_w2 = sem("in_w1"), sem("in_w2")
        in_b1 = [sem(f"in_b1_{i}") for i in range(2)]
        in_b2 = [sem(f"in_b2_{i}") for i in range(2)]
        in_rows = [sem(f"in_rows{i}") for i in range(2)]
        w1_hi, w2_hi = sem("w1_hi"), sem("w2_hi")
        w1_lo, w2_lo = sem("w1_lo"), sem("w2_lo")
        turned, hT_hi, hT_lo = sem("turned"), sem("hT_hi"), sem("hT_lo")
        layer1 = sem("layer1")
        hidden = sem("hidden")
        hid_hi, hid_lo = sem("hid_hi"), sem("hid_lo")
        layer2, y_ready = sem("layer2"), sem("y_ready")
        stored = [sem(f"stored{i}") for i in range(2)]
        tick, tick_act = sem("tick"), sem("tick_act")
        block = ctx.enter_context(nc.Block())

        def piece(w, c):
            n = w.shape[1] // PIECES
            return w[:, c * n:(c + 1) * n, :]

        def over_tiles(eng, tile):
            rounds = (NT - 4) // 2
            for k in range(2):
                tile(k, k % 2, k // 2)
            with eng.Fori(1, 1 + rounds) as i:
                for par in range(2):
                    tile(2 * i + par, par, i)
            for k in range(2 + 2 * rounds, NT):
                tile(k, k % 2, k // 2)

        def there(k, n):
            return not isinstance(k, int) or 0 <= k + n < NT

        @block.sync
        def _(sp):
            def hold(semaphore, value):
                sp.wait_ge(semaphore, value)
                sp.sem_inc(tick)

            def load(k, par, i):
                e = sp.value_load(g.which[0:1, k:k + 1] if isinstance(k, int) else g.which[0:1, bass.ds(k, 1)],
                                  min_val=0, max_val=E - 1)

                def load_rows():
                    hold(turned, k + 1)
                    sp.dma_start(rows[par][:], g.hs.rearrange("(k s p) d -> k p s d", s=SUB, p=P)[bass.ds(k, 1)]
                                 .rearrange("o p s d -> p (o s) d")).then_inc(in_rows[par], 16)

                if there(k, -1):
                    load_rows()
                hold(w1_lo, PIECES * (k + 1))
                sp.dma_start(w1[:], g.w1[bass.ds(e, 1)].rearrange("o (k p) f -> p (o k) f", p=P)).then_inc(in_w1, 16)
                hold(hidden, KF * (k + 1))
                sp.dma_start(b1[par][:], g.b1T[bass.ds(e, 1)].rearrange("o p k -> p (o k)")).then_inc(in_b1[par], 16)
                hold(w2_lo, PIECES * (k + 1))
                sp.dma_start(w2[:], g.w2[bass.ds(e, 1)].rearrange("o (k p) d -> p (o k) d", p=P)).then_inc(in_w2, 16)
                hold(y_ready, k + 1)
                sp.dma_start(b2[par][:], g.b2[bass.ds(e, 1)].rearrange("o d -> (o d)").partition_broadcast(P)
                             ).then_inc(in_b2[par], 16)
                if not there(k, -1):
                    hold(scattered, 16 * T)
                    load_rows()

            over_tiles(sp, load)

        @block.gpsimd
        def _(pool):
            for t in range(T):
                nc.gpsimd.indirect_dma_start(g.hs, bass.IndirectOffsetOnAxis(g.slot[:, t:t + 1], 0), g.H2[:, t, :], None
                                             ).then_inc(scattered, 16)

            def split(k, par, i):
                if not there(k, -1):
                    return
                for c in range(PIECES):
                    pool.wait_ge(w1_hi, PIECES * k + c + 1)
                    nc.gpsimd.tensor_tensor(piece(w1_part[par][1], c), piece(w1, c),
                                            piece(w1_part[par][0], c).bitcast(F32), ALU.subtract).then_inc(w1_lo, 1)

            over_tiles(pool, split)

        @block.scalar
        def _(act):
            def first_weights(k, par):
                act.wait_ge(in_w1, 16 * (k + 1))
                for c in range(PIECES):
                    nc.scalar.copy(piece(w1_part[par][0], c), piece(w1, c)).then_inc(w1_hi, 1)

            def second_weights(k, par):
                act.wait_ge(in_w2, 16 * (k + 1))
                if there(k, -2):
                    act.wait_ge(layer2, k)
                for c in range(PIECES):
                    nc.scalar.copy(piece(w2_part[par][0], c), piece(w2, c)).then_inc(w2_hi, 1)

            def copy_turned(k, par):
                act.wait_ge(turned, k + 1 + AHEAD)
                nc.scalar.copy(hT[par][0][:], pst[par][:]).then_inc(hT_hi, 1)

            def store(k, par):
                act.wait_ge(y_ready, k + 1 + AHEAD)
                act.sem_inc(tick_act)
                act.dma_start(g.ys.rearrange("(k s p) d -> k p s d", s=SUB, p=P)[bass.ds(k, 1)]
                              .rearrange("o p s d -> p (o s) d"), y[par][:]).then_inc(stored[par], 16)

            act.sem_inc(hidden, AHEAD * KF)
            for par in range(2):
                act.sem_inc(stored[par], 16)
            first_weights(0, 0)
            second_weights(0, 0)
            copy_turned(0, 0)
            act.wait_ge(scattered, 16 * T)
            first_weights(1, 1)

            def tile(k, par, i):
                act.wait_ge(in_b1[par], 16 * (i + 1))
                for f in range(KF):
                    act.wait_ge(layer1, KF * k + f // 2 * 2 + 2)
                    act.wait_ge(hid_lo, HPAIRS * k + f // 2 + 1)
                    nc.scalar.activation(hid[:, f, :], psh[f // 2][:, f % 2, :], ACT.Relu, bias=b1[par][:, f:f + 1]
                                         ).then_inc(hidden, 1)
                if there(k, 1):
                    copy_turned(k + 1, 1 - par)
                if there(k, -1):
                    store(k - 1, 1 - par)
                if there(k, 1):
                    second_weights(k + 1, 1 - par)
                if there(k, 2):
                    first_weights(k + 2, par)

            over_tiles(act, tile)
            store(NT - 1, (NT - 1) % 2)
            for par in range(2):
                act.wait_ge(stored[par], 16 * ((NT + 1 - par) // 2) + 16)

        @block.vector
        def _(dve):
            def low_rows(k, par):
                dve.wait_ge(hT_hi, k + 1)
                nc.vector.tensor_tensor(hT[par][1][:], pst[par][:], hT[par][0][:].bitcast(F32), ALU.subtract
                                        ).then_inc(hT_lo, 1)

            def low_weights(k, par):
                for c in range(PIECES):
                    dve.wait_ge(w2_hi, PIECES * k + c + 1)
                    nc.vector.tensor_tensor(piece(w2_part[par][1], c), piece(w2, c),
                                            piece(w2_part[par][0], c).bitcast(F32), ALU.subtract).then_inc(w2_lo, 1)

            def add_bias(k, par, n):
                dve.wait_ge(in_b2[par], 16 * n)
                dve.wait_ge(stored[par], 16 * n)
                dve.wait_ge(layer2, k + 2)
                nc.vector.tensor_add(y[par][:], psy[par][:], b2[par][:].unsqueeze(1).to_broadcast([P, SUB, D])
                                     ).then_inc(y_ready, 1)

            dve.sem_inc(y_ready, AHEAD)
            dve.sem_inc(w2_lo, PIECES)
            dve.sem_inc(hid_lo, HPAIRS)
            dve.sem_inc(w1_lo, PIECES)
            for c in range(PIECES):
                dve.wait_ge(w1_hi, c + 1)
                nc.vector.tensor_tensor(piece(w1_part[0][1], c), piece(w1, c), piece(w1_part[0][0], c).bitcast(F32),
                                        ALU.subtract).then_inc(w1_lo, 1)
            low_weights(0, 0)
            low_rows(0, 0)

            def tile(k, par, i):
                if there(k, -1):
                    add_bias(k - 1, 1 - par, i + par)
                for p in range(HPAIRS):
                    two = slice(2 * p, 2 * p + 2)
                    dve.wait_ge(hidden, KF * k + 2 * p + 2 + AHEAD * KF)
                    nc.vector.tensor_copy(hid_part[0][:, two, :], hid[:, two, :]).then_inc(hid_hi, 1)
                    dve.wait_ge(hid_hi, HPAIRS * k + p + 1)
                    nc.vector.tensor_tensor(hid_part[1][:, two, :], hid[:, two, :],
                                            hid_part[0][:, two, :].bitcast(F32), ALU.subtract).then_inc(hid_lo, 1)
                if there(k, 1):
                    low_rows(k + 1, 1 - par)
                    low_weights(k + 1, 1 - par)

            over_tiles(dve, tile)
            add_bias(NT - 1, (NT - 1) % 2, (NT + 1) // 2)

        @block.tensor
        def _(pe):
            PARTS = ((0, 0), (0, 1), (1, 0))

            def turn(k, par, n):
                pe.wait_ge(in_rows[par], 16 * n)
                for s in range(SUB):
                    for c in range(KD):
                        last = nc.tensor.transpose(pst[par][:, c, s * P:(s + 1) * P],
                                                   rows[par][:, s, c * P:(c + 1) * P], g.ident[:])
                last.then_inc(turned, 1)

            pe.sem_inc(turned, AHEAD)
            pe.sem_inc(layer2, 1)
            turn(0, 0, 1)

            def tile(k, par, i):
                pe.wait_ge(hT_hi, k + 1)
                pe.wait_ge(hT_lo, k + 1)
                pe.wait_ge(w1_hi, PIECES * (k + 1))
                pe.wait_ge(w1_lo, PIECES * (k + 2))
                for f in range(KF):
                    pe.wait_ge(hidden, KF * k + f + 1 + KF if f % 2 else KF * k + f + 2 + KF)
                    steps = [(c, a, b) for c in range(KD) for a, b in PARTS]
                    for n, (c, a, b) in enumerate(steps):
                        last = nc.tensor.matmul(psh[f // 2][:, f % 2, :], w1_part[par][a][:, c, f * P:(f + 1) * P],
                                                hT[par][b][:, c, :], start=n == 0, stop=n == len(steps) - 1)
                    last.then_inc(layer1, 1)
                if there(k, 1):
                    turn(k + 1, 1 - par, i + 1 + par)
                pe.wait_ge(w2_hi, PIECES * (k + 1))
                pe.wait_ge(w2_lo, PIECES * (k + 2))
                pe.wait_ge(y_ready, k + 1)
                for s in range(SUB):
                    for f in range(KF):
                        if s == 0:
                            pe.wait_ge(hid_lo, HPAIRS * (k + 1) + f // 2 + 1)
                        for a, b in PARTS:
                            last = nc.tensor.matmul(psy[par][:, s, :], hid_part[a][:, f, s * P:(s + 1) * P],
                                                    w2_part[par][b][:, f, :], start=f == 0 and (a, b) == PARTS[0],
                                                    stop=f == KF - 1 and (a, b) == PARTS[-1])
                last.then_inc(layer2, 1)

            over_tiles(pe, tile)


def combine(nc, g):
    FLIGHT = 8
    with ExitStack() as ctx:
        sem = open_sem(ctx, nc, "comb")
        sb, ps = open_mem(ctx, nc, "comb")
        got = sb("got", [P, T, D])
        fetched = [sem(f"fetched{i}") for i in range(FLIGHT)]
        s_g, s_o, s_out = sem("s_g"), sem("s_o"), sem("s_out")
        block = ctx.enter_context(nc.Block())
        LOT = 2

        @block.gpsimd
        def _(pool):
            for t in range(T):
                if t >= FLIGHT:
                    pool.wait_ge(fetched[t % FLIGHT], 16 * (t // FLIGHT))
                nc.gpsimd.indirect_dma_start(got[:, t, :], None, g.ys, bass.IndirectOffsetOnAxis(g.slot[:, t:t + 1], 0)
                                             ).then_inc(fetched[t % FLIGHT], 16)

        @block.vector
        def _(dve):
            for t in range(T):
                b = t // TB
                dve.wait_ge(fetched[t % FLIGHT], 16 * (t // FLIGHT + 1))
                nc.vector.tensor_mul(got[:, t, :], got[:, t, :], g.mod[:, b, 5, :]).then_inc(s_g, 1)
                if t:
                    dve.wait_ge(s_g, t)
                    nc.vector.tensor_add(g.X[:, t - 1, :], g.X[:, t - 1, :], got[:, t - 1, :]).then_inc(s_o, 1)
            dve.wait_ge(s_g, T)
            nc.vector.tensor_add(g.X[:, T - 1, :], g.X[:, T - 1, :], got[:, T - 1, :]).then_inc(s_o, 1)

        @block.sync
        def _(sp):
            dst = g.out.rearrange("b (t p) d -> p (b t) d", p=P)
            for t in range(0, T, LOT):
                sp.wait_ge(s_o, t + LOT)
                sp.dma_start(dst[:, t:t + LOT, :], g.X[:, t:t + LOT, :]).then_inc(s_out, 16)
            sp.wait_ge(s_out, 16 * T // LOT)



def build(nc, ins, consts, out):
    g = Ctx()
    (g.x, g.wqkvT, g.qkv_b, g.wpT, g.proj_b, g.gwT, g.gate_b, g.expert_bias, g.w1, g.b1T, g.w2, g.b2, g.cT,
     g.wmod) = ins
    g.rope, g.row = consts
    g.out = out
    g.qkT = [nc.dram_tensor(f"qkT_{part}", (2, B * D, N), F32, kind="Internal").ap() for part in ("hi", "lo")]
    g.hs = nc.dram_tensor("routed_rows", (NT * FT, D), F32, kind="Internal").ap()
    g.ys = nc.dram_tensor("expert_rows", (NT * FT, D), F32, kind="Internal").ap()
    with ExitStack() as ctx:
        sb, _ = open_mem(ctx, nc, "all")
        g.ident = sb("ident", [P, P])
        g.X = sb("X", [P, T, D])
        g.mv = sb("mv", [P, T, 2])
        g.sd = sb("sd", [P, 3, T])
        g.rs = sb("rs", [P, T])
        g.mod = sb("mod", [P, B, 6, D])
        with ExitStack() as inner:
            g.V = inner.enter_context(nc.sbuf_tensor("V", [P, UNITS, TB, 2 * HD], F32))
            g.K = [inner.enter_context(nc.sbuf_tensor(f"K{i}", [P, N], F32R)) for i in range(2)]
            g.QM = [inner.enter_context(nc.sbuf_tensor(f"QM{i}", [P, 2, CH], F32R)) for i in range(2)]
            g.keys_in = [inner.enter_context(nc.semaphore(f"keys_in{i}")) for i in range(2)]
            g.queries_in = [inner.enter_context(nc.semaphore(f"queries_in{i}")) for i in range(2)]
            with ExitStack() as front:
                fsb, _ = open_mem(front, nc, "front")
                g.wq = fsb("wq", [P, KD, QKV])
                g.qb = fsb("qb", [P, QKV])
                g.tab = fsb("tab", [P, 2, TB, HD])
                g.zero = fsb("zero", [P, 2048])
                setup(nc, g)
                qkv_stage(nc, g)
            g.wp = inner.enter_context(nc.sbuf_tensor("wp", [P, KD, D], F32))
            g.O = inner.enter_context(nc.sbuf_tensor("O", [P, UNITS, TB, 2 * (HD + 1)], F32))
            attention(nc, g)
            projection(nc, g)
        with ExitStack() as inner:
            isb, _ = open_mem(inner, nc, "ffn_all")
            g.logits = isb("logits", [P, T, E])
            g.slot = isb("slot", [P, T], I32)
            g.which = isb("which_i", [P, NT], I32)
            with ExitStack() as rows:
                g.H2 = rows.enter_context(nc.sbuf_tensor("H2", [P, T, D], F32))
                gate_stage(nc, g)
                routing(nc, g)
                experts(nc, g)
            combine(nc, g)


def rope_tables():
    inv = (1.0 / np.float32(10000.0) ** (np.arange(0, HD, 2, dtype=np.float32) / np.float32(HD))).astype(np.float32)
    freqs = np.arange(N, dtype=np.float32)[:, None] * inv[None, :]
    cos, sin = np.cos(freqs).astype(np.float32), np.sin(freqs).astype(np.float32)
    return np.ascontiguousarray(np.stack([np.repeat(cos, 2, axis=1), np.stack([-sin, sin], axis=-1).reshape(N, HD)]))


def routing_row():
    return np.concatenate([E - np.arange(E), FT * np.arange(B * N // FT), np.arange(NT)]).astype(np.float32)


def kernel(L0_attn_x, L0_attn_qkv_w, L0_attn_qkv_b, L0_attn_proj_w, L0_attn_proj_b, L0_ffn_gate_w, L0_ffn_gate_b,
           L0_ffn_expert_bias, L0_ffn_w1, L0_ffn_b1, L0_ffn_w2, L0_ffn_b2, L0_c, L0_wmod):
    import concourse.bacc as bacc
    from concourse.bass_utils import run_bass_kernel_spmd

    laid = {
        "x": L0_attn_x, "wqkvT": np.asarray(L0_attn_qkv_w).T, "qkv_b": L0_attn_qkv_b,
        "wpT": np.asarray(L0_attn_proj_w).T, "proj_b": L0_attn_proj_b, "gwT": np.asarray(L0_ffn_gate_w).T,
        "gate_b": L0_ffn_gate_b, "expert_bias": L0_ffn_expert_bias, "w1": L0_ffn_w1,
        "b1T": np.asarray(L0_ffn_b1).reshape(E, KF, P).transpose(0, 2, 1), "w2": L0_ffn_w2, "b2": L0_ffn_b2,
        "cT": np.asarray(L0_c).T, "wmod": L0_wmod,
    }
    nc = bacc.Bacc("TRN2", target_bir_lowering=False, num_devices=1)
    arrays, ins = {}, []
    for name, a in laid.items():
        a = np.ascontiguousarray(a)
        arrays["in_" + name] = a
        ins.append(nc.dram_tensor("in_" + name, a.shape, mybir.dt.from_np(a.dtype), kind="ExternalInput").ap())
    consts = []
    for name, a in (("rope", rope_tables()), ("row", routing_row())):
        arrays["const_" + name] = a
        consts.append(nc.dram_tensor("const_" + name, a.shape, mybir.dt.from_np(a.dtype), kind="ExternalInput").ap())
    out = nc.dram_tensor("out", (B, N, D), F32, kind="ExternalOutput").ap()
    build(nc, ins, consts, out)
    return run_bass_kernel_spmd(nc, [arrays], core_ids=[0]).results[0]["out"]
```
